# Optimizing a Trainium2 kernel written in Bass

```python
import numpy as np
import jax
import jax.numpy as jnp

def _softmax(x, axis=-1):
    return jax.nn.softmax(x, axis=axis)

def _gelu(x):
    return jax.nn.gelu(x, approximate=True)

def _silu(x):
    return jax.nn.silu(x)

def _sigmoid(x):
    return jax.nn.sigmoid(x)

def _layernorm(x, axis=-1, eps=1e-05):
    m = jnp.mean(x, axis=axis, keepdims=True)
    v = jnp.var(x, axis=axis, keepdims=True)
    return (x - m) / jnp.sqrt(v + eps)

def _scatter_add(tgt, idx, src, axis=0):
    return tgt.at[idx].add(src)

def _segment_sum(src, seg, n):
    return jax.ops.segment_sum(src, seg, n)
kernel_name = 'mk_gps_d1_gnn_r8_f12034'

def setup_inputs(seed: int=0):
    np.random.seed(seed)
    _w = jnp.asarray

    def _rec_inputs():
        import jax
        import jax.numpy as jnp
        _gk = jax.random.key(seed)
        x = -0.0003713 + 1 * jax.random.normal(jax.random.fold_in(_gk, 1), (6250, 256), jnp.float32)
        src = jax.random.randint(jax.random.fold_in(_gk, 2), (200000,), 0, 6250, jnp.int32)
        dst = jax.random.randint(jax.random.fold_in(_gk, 3), (200000,), 0, 6250, jnp.int32)
        _o = jnp.argsort(dst, stable=True)
        src = src[_o]
        dst = dst[_o]
        return (x, src, dst)
    x, src, dst = _rec_inputs()

    def _L0_gnn_setup():
        import jax, jax.numpy as jnp
        import numpy as np
        N_NODES = 6250
        EPS = 1e-12
        key = jax.random.key(seed)
        k1, k2, k3 = jax.random.split(key, 3)
        d_in, d_out, n_edges = (256, 256, 100000)
        input_matrix = jax.random.normal(k1, (N_NODES, d_in), dtype=jnp.float32)
        adjacency_coo_matrix = jax.random.randint(k2, (2, n_edges), 0, N_NODES, dtype=jnp.int64)
        W = jax.random.normal(k3, (2 * d_in, d_out), dtype=jnp.float32) * (1.0 / np.sqrt(2 * d_in))
        b = jnp.zeros((d_out,), dtype=jnp.float32)
        return {'input_matrix': input_matrix, 'adjacency_coo_matrix': adjacency_coo_matrix, 'W': W, 'b': b}
    _L0_gnn_all = _L0_gnn_setup()
    _L0_gnn_in = {k: v for k, v in _L0_gnn_all.items() if k in ('W', 'b')}
    del _L0_gnn_all

    def _L0_mix_setup():
        import math
        import jax, jax.numpy as jnp
        import numpy as np
        EPS_DIV = 1e-07
        EPS_NORM = 1e-12

        def _l2_normalize(x, axis):
            n = jnp.sqrt(jnp.sum(x * x, axis=axis, keepdims=True))
            return x / jnp.maximum(n, EPS_NORM)
        key = jax.random.key(seed)
        ks = jax.random.split(key, 5)
        b, N, C = (8, 512, 256)
        x = jax.random.normal(ks[0], (b, N, C), dtype=jnp.float32)
        W_qkv = jax.random.normal(ks[1], (C, 3 * C), dtype=jnp.float32) * (1.0 / math.sqrt(C))
        b_qkv = jax.random.normal(ks[2], (3 * C,), dtype=jnp.float32) * 0.02
        W_out = jax.random.normal(ks[3], (C, C), dtype=jnp.float32) * (1.0 / math.sqrt(C))
        b_out = jax.random.normal(ks[4], (C,), dtype=jnp.float32) * 0.02
        return {'x': x, 'W_qkv': W_qkv, 'b_qkv': b_qkv, 'W_out': W_out, 'b_out': b_out}
    _L0_mix_all = _L0_mix_setup()
    _L0_mix_in = {k: v for k, v in _L0_mix_all.items() if k in ('W_qkv', 'b_qkv', 'W_out', 'b_out')}
    del _L0_mix_all

    def _L0_ffn_setup():
        import jax, jax.numpy as jnp
        import numpy as np
        N_EXPERTS = 8
        TOP_K = 2
        key = jax.random.key(seed)
        ks = jax.random.split(key, 5)
        B, T, C, E, H = (8, 256, 256, 8, 682)
        scale = 1.0 / np.sqrt(C)
        return {'x': jax.random.normal(ks[0], (B, T, C), dtype=jnp.float32), 'router_w': jax.random.normal(ks[1], (E, C), dtype=jnp.float32) * scale, 'w1': jax.random.normal(ks[2], (E, H, C), dtype=jnp.float32) * scale, 'w2': jax.random.normal(ks[3], (E, C, H), dtype=jnp.float32) * (1.0 / np.sqrt(H)), 'w3': jax.random.normal(ks[4], (E, H, C), dtype=jnp.float32) * scale}
    _L0_ffn_all = _L0_ffn_setup()
    _L0_ffn_in = {k: v for k, v in _L0_ffn_all.items() if k in ('router_w', 'w1', 'w2', 'w3')}
    del _L0_ffn_all
    return {'x': x, 'src': src, 'dst': dst, 'L0_gnn_W': _L0_gnn_in['W'], 'L0_gnn_b': _L0_gnn_in['b'], 'L0_mix_W_qkv': _L0_mix_in['W_qkv'], 'L0_mix_b_qkv': _L0_mix_in['b_qkv'], 'L0_mix_W_out': _L0_mix_in['W_out'], 'L0_mix_b_out': _L0_mix_in['b_out'], 'L0_ffn_router_w': _L0_ffn_in['router_w'], 'L0_ffn_w1': _L0_ffn_in['w1'], 'L0_ffn_w2': _L0_ffn_in['w2'], 'L0_ffn_w3': _L0_ffn_in['w3']}

def reference(x, src, dst, L0_gnn_W, L0_gnn_b, L0_mix_W_qkv, L0_mix_b_qkv, L0_mix_W_out, L0_mix_b_out, L0_ffn_router_w, L0_ffn_w1, L0_ffn_w2, L0_ffn_w3):
    import jax
    import jax.numpy as jnp

    def _L0_gnn_ref(input_matrix, adjacency_coo_matrix, W, b):
        import jax, jax.numpy as jnp
        import numpy as np
        N_NODES = 6250
        EPS = 1e-12
        src = adjacency_coo_matrix[0]
        dst = adjacency_coo_matrix[1]
        neigh_sum = jax.ops.segment_sum(input_matrix[src], dst, num_segments=N_NODES)
        deg = jax.ops.segment_sum(jnp.ones_like(dst, dtype=input_matrix.dtype), dst, num_segments=N_NODES)
        neigh_mean = neigh_sum / jnp.maximum(deg, 1.0)[:, None]
        h = jnp.concatenate([input_matrix, neigh_mean], axis=-1)
        out = jax.nn.relu(h @ W + b)
        norm = jnp.maximum(jnp.linalg.norm(out, axis=-1, keepdims=True), EPS)
        return out / norm

    def _L0_mix_ref(x, W_qkv, b_qkv, W_out, b_out):
        import math
        import jax, jax.numpy as jnp
        import numpy as np
        EPS_DIV = 1e-07
        EPS_NORM = 1e-12

        def _l2_normalize(x, axis):
            n = jnp.sqrt(jnp.sum(x * x, axis=axis, keepdims=True))
            return x / jnp.maximum(n, EPS_NORM)
        b, N, C = x.shape
        qkv = x @ W_qkv + b_qkv
        q, k, v = jnp.split(qkv, 3, axis=2)
        q = q - jnp.mean(q, axis=2, keepdims=True)
        k = k - jnp.mean(k, axis=2, keepdims=True)
        q2 = q * q
        k2 = k * k
        q2s = jnp.sum(q2, axis=2, keepdims=True)
        k2s = jnp.sum(k2, axis=2, keepdims=True)
        k2 = _l2_normalize(k2 / (k2s + EPS_DIV), axis=-2)
        q2 = _l2_normalize(q2 / (q2s + EPS_DIV), axis=-1)
        kv = jnp.einsum('bnc,bnd->bcd', k2, v)
        t2 = jnp.einsum('bnc,bcd->bnd', q2, kv) / math.sqrt(N)
        attn = v + t2
        return attn @ W_out + b_out

    def _L0_ffn_ref(x, router_w, w1, w2, w3):
        import jax, jax.numpy as jnp
        import numpy as np
        N_EXPERTS = 8
        TOP_K = 2
        B, T, C = x.shape
        flat = x.reshape(-1, C)
        logits = flat @ router_w.T
        probs = jax.nn.softmax(logits, axis=-1)
        topk_probs, topk_idx = jax.lax.top_k(probs, TOP_K)
        topk_probs = topk_probs / (jnp.sum(topk_probs, axis=-1, keepdims=True) + 1e-09)
        onehot = jax.nn.one_hot(topk_idx, N_EXPERTS, dtype=flat.dtype)
        gates = jnp.einsum('nk,nke->ne', topk_probs, onehot)
        h1 = jnp.einsum('nc,ehc->neh', flat, w1)
        h3 = jnp.einsum('nc,ehc->neh', flat, w3)
        h = jax.nn.silu(h1) * h3
        y = jnp.einsum('neh,ech->nec', h, w2)
        out = jnp.einsum('ne,nec->nc', gates, y)
        return out.reshape(B, T, C)
    edge_index = jnp.stack([src, dst])
    xn = _layernorm(x, axis=-1)
    x = x + _L0_gnn_ref(xn, edge_index, L0_gnn_W, L0_gnn_b) + _L0_mix_ref(xn[None], L0_mix_W_qkv, L0_mix_b_qkv, L0_mix_W_out, L0_mix_b_out)[0]
    x = x + _L0_ffn_ref(_layernorm(x, axis=-1)[None], L0_ffn_router_w, L0_ffn_w1, L0_ffn_w2, L0_ffn_w3)[0]
    return x

_drawn_inputs = setup_inputs


def setup_inputs(seed=0):
    import zlib

    import numpy as np

    out = dict(_drawn_inputs(seed))
    spreads = {'L0_gnn_b': (0.0, 0.444)}
    factors = {}
    for name, (base, spread) in spreads.items():
        noise = np.random.default_rng([zlib.crc32(name.encode()), seed]).standard_normal(out[name].shape)
        drawn = base * np.exp(spread * noise) if base else spread * noise
        out[name] = jnp.asarray(drawn.astype(out[name].dtype))
    for name, factor in factors.items():
        out[name] = (out[name] * factor).astype(out[name].dtype)
    return out
```

```python
import concourse.bass as bass
from concourse import mybir
from contextlib import ExitStack

P = 128
F32 = mybir.dt.float32
F16 = mybir.dt.float16
I32 = mybir.dt.int32
U32 = mybir.dt.uint32
ALU = mybir.AluOpType
ACT = mybir.ActivationFunctionType
AX = mybir.AxisListType
RMAX = bass.bass_isa.ReduceOp.max

NODES = 6250
C = 256
KC = C // P
TILES = -(-NODES // P)
NPAD = TILES * P
LAST = NODES - (TILES - 1) * P
EDGES = 200000
ET = -(-EDGES // P)
W = 36
WG = 4
GROUPS = W // WG
RG = 3
ETW = ET + W + 1
EJ = -(-ET // P)
EXP = 8
HID = 682
FULL = HID // P
HT_FULL = EXP * FULL
REST = HID - FULL * P
HT = HT_FULL + -(-EXP * REST // P)
HPAD = HT * P
BT = 4
NB = BT * P
BLOCKS = TILES // BT
GLOADS = EXP + HT - HT_FULL
GSLOTS = 3
XS = 1024.0
TROW = 64
NW13 = 48
WCH = 4
SPLITS = 8
SCOL = HPAD * KC // SPLITS
EPS_LN, EPS_DIV, EPS_NORM = 1e-5, 1e-7, 1e-12
TINY = 1e-30
RSQRT_MAGIC = float(0x5F3759DF)

AHEAD = BT + 1

GROUP_AT = [[] for _ in range(HT)]
for _g in range(BT * GROUPS):
    GROUP_AT[int((_g + 0.5) * (HT - BT) / (BT * GROUPS))].append((_g // GROUPS, _g % GROUPS))
POST = 10
STAGES = dict(enumerate("ABCDEFGHI", 1))


def stages_at(step, tiles):
    q, k = divmod(step, POST)
    return [(q, STAGES[k])] if q in tiles and k in STAGES else []


def some(n):
    return not (isinstance(n, int) and n == 0)


def segments(tile):
    first = (tile - HT_FULL) * P
    out, r = [], first
    while r < min(first + P, EXP * REST):
        e = r // REST
        end = min((e + 1) * REST, first + P, EXP * REST)
        out.append((r - first, end - first, e))
        r = end
    return out


def gnn_mix_moe(nc, x, srcT, dstT, dst_rows, Wg, bg, Wq, Wk, WvT, bq, bk, bv, Wo, bo,
                rwT, w1n, w3n, w2n, w13T, w2T, outT):
    with ExitStack() as ctx:
        def sb(name, shape, dt=F32):
            return ctx.enter_context(nc.sbuf_tensor(name, shape, dt))

        def sem(name):
            return ctx.enter_context(nc.semaphore(name))

        def sems(name, n):
            return [sem(f"{name}_{i}") for i in range(n)]

        def dram(name, shape, dt=F32):
            return nc.dram_tensor(name, shape, dt).ap()

        XH = dram("xn_split", (NPAD, 2 * C), F16)
        XN = dram("xn_rows", (NPAD, C))
        XT = dram("xn_cols", (NPAD, C))
        GT = dram("gates_t", (EXP, NPAD))

        w13 = sb("w13", [P, 2, KC, 2, HPAD], F16)
        w2 = sb("w2", [P, 2, HT, C], F16)
        x2s = sb("x2s", [P, 2 * KC, NB], F16)
        x2a = sb("x2a", [P, 2 * KC, NB], F16)
        x1s = sb("x1s", [P, KC * NB])
        x1a = sb("x1a", [P, KC * NB])
        gate = sb("gate", [P, GSLOTS * NB])
        sig = sb("sig", [P, 2 * NB])
        hid = sb("hid", [P, 2 * NB])
        hh = sb("hh", [P, 3 * 2, NB], F16)
        rows = sb("rows", [P, RG * WG, 2 * C + 2], F16)
        hot = sb("hot", [P, RG, WG, P], F16)
        wq_s = sb("wq_s", [P, KC, C])
        wg_s = sb("wg_s", [P, 2 * KC, C])
        mix = sb("mix", [P, KC, C])
        wvo = sb("wvo", [P, KC, C])
        bq_b = sb("bq_b", [P, C])
        bg_b = sb("bg_b", [P, C])
        co_b = sb("co_b", [P, C])
        rw_s = sb("rw_s", [P, KC, EXP])
        ident = sb("ident", [P, P])
        lane = sb("lane", [P, P], F16)
        xt = sb("xt", [P, 2, C])
        xnt = sb("xnt", [P, 2, C])
        neigh = sb("neigh", [P, 2, C])
        tmp = sb("tmp", [P, 5, C])
        srcw = sb("srcw", [P, 2, W], I32)
        dstw = sb("dstw", [P, 2, W], I32)
        dstf = sb("dstf", [P, 2, W])
        base = sb("base", [P, TILES])
        tab = sb("tab", [P, 3, TROW], I32)
        xsrc = sb("xsrc", [P, 1], I32)
        xdst = sb("xdst", [P, 1], I32)
        xdf = sb("xdf", [P, 1])
        xrow = sb("xrow", [P, 2 * C + 2], F16)
        xhot = sb("xhot", [P, P], F16)
        sc = sb("sc", [P, 96])
        cst = sb("cst", [P, 8])
        lane8 = sb("lane8", [P, EXP])
        idx8 = sb("idx8", [P, EXP], U32)
        gts = sb("gts", [EXP, P])
        one = sb("one", [P, 1])

        ring6 = [x1s[:, :], x1a[:, :], x2s[:, :, :].rearrange("p a n -> p (a n)").bitcast(F32),
                 x2a[:, :, :].rearrange("p a n -> p (a n)").bitcast(F32), sig[:, :], hid[:, :]]
        xhb = [x2s[:, :, :], x2a[:, :, :]]
        ring6 = [r.rearrange("p (t c) -> p t c", c=C) for r in ring6]
        xin, xtb = ring6[0:2], ring6[4:6]
        kxn, kxt = ring6[0:3], ring6[3:6]
        keyb = [tmp[:, i, :] for i in range(3)]
        key2 = [tmp[:, 3, :], tmp[:, 4, :], xt[:, 0, :]]
        key4 = [xt[:, 1, :], xnt[:, 0, :], xnt[:, 1, :]]
        wk_s, bk_b = mix, co_b
        gflat = gate[:, :]
        hflat = hh[:, :, :].rearrange("p a n -> p (a n)").bitcast(F32)
        stage = [gflat[:, 0:SCOL], hflat[:, 0:SCOL]]
        wvt_s = gflat[:, 0:512].rearrange("p (k c) -> p k c", c=C)
        wo_s = gflat[:, 512:1024].rearrange("p (k c) -> p k c", c=C)
        bv_s = gflat[:, 1024:1024 + KC]
        bvr = gflat[:, 1040:1040 + KC * P].rearrange("p (k c) -> p k c", c=P)
        kxs = tmp[:, 0:2, :]
        sbv, bo_b = tmp[:, 2, :], tmp[:, 3, :]
        nst = [hflat[:, 0:WCH * C].rearrange("p (t c) -> p t c", c=C), tmp[:, 0:WCH, :]]
        nst2 = [hflat[:, 0:HID], tmp[:, :, :].rearrange("p a c -> p (a c)")[:, 0:HID]]
        drow = w2[:, 0, 0:EJ, :].rearrange("p t c -> p (t c)").bitcast(I32).rearrange("p (j e) -> p j e", e=P)
        rng = w2[:, 1, :, :].rearrange("p t c -> p (t c)").bitcast(F32)
        kidx, dmin, dmax = rng[:, 0:EJ], rng[:, 20:20 + EJ], rng[:, 40:40 + EJ]
        ra = rng[:, 100:100 + TILES * EJ].rearrange("p (t j) -> p t j", j=EJ)
        rb = rng[:, 800:800 + TILES * EJ].rearrange("p (t j) -> p t j", j=EJ)
        rloc, rall = rng[:, 2800:2800 + 2 * TILES], rng[:, 3000:3000 + 2 * TILES]
        run = [rng[:, 3200 + 64 * i:3200 + 64 * i + TILES] for i in range(2)]
        ssq = rng[:, 4000:4000 + 2 * NW13 + 16]

        bank = [ctx.enter_context(nc.psum_tensor(f"bank{i}", [P, 512], F32)) for i in range(8)]
        Y, H1, H3, AG, PB = bank[0:2], bank[2:4], bank[4:6], bank[6], bank[7]

        s_wld = sem("s_wld")
        s_bo = sem("s_bo")
        s_rng = sem("s_rng")
        s_x = sems("s_x", 2)
        s_xst = sems("s_xst", 2)
        s_nw = sems("s_nw", 2)
        s_k = sems("s_k", 3)
        s_st = sems("s_st", 2)
        s_win = sems("s_win", 2)
        s_row = sems("s_row", RG)
        s_tile = sems("s_tile", 2)
        s_gst = sem("s_gst")
        s_gld = sems("s_gld", GSLOTS)
        s_out = sem("s_out")
        s_xi = sem("s_xi")
        s_xr = sem("s_xr")
        s_const, s_ident, s_rloc, s_rall, s_tab = map(sem, ("s_const", "s_ident", "s_rloc", "s_rall", "s_tab"))
        s_nloc, s_nall, s_ssq, s_cst = map(sem, ("s_nloc", "s_nall", "s_ssq", "s_cst"))
        s_zero = sem("s_zero")
        s_lnr = sem("s_lnr")
        s_lnx = sem("s_lnx")
        s_lnh = sem("s_lnh")
        s_lnl = sem("s_lnl")
        s_lnt = sem("s_lnt")
        s_lnc = sem("s_lnc")
        s_cent = sem("s_cent")
        s_kp = sem("s_kp")
        s_kb = sem("s_kb")
        s_k2 = sem("s_k2")
        s_k2n = sem("s_k2n")
        s_k4 = sem("s_k4")
        s_kx = sem("s_kx")
        s_wvo, s_wvc, s_kxs, s_mp, s_mix = map(sem, ("s_wvo", "s_wvc", "s_kxs", "s_mp", "s_mix"))
        s_whi = sem("s_whi")
        s_wlo = sem("s_wlo")
        s_dst = sem("s_dst")
        s_hot = sem("s_hot")
        s_used = sem("s_used")
        s_agg = sem("s_agg")
        s_nei = sem("s_nei")
        s_pool = sem("s_pool")
        s_sp = sem("s_sp")
        s_xs = sem("s_xs")
        s_xh = sem("s_xh")
        s_xd = sem("s_xd")
        (s_pA, s_dA, s_aA, s_dB, s_pB, s_dC, s_aC, s_dD, s_pC, s_dE, s_pD, s_dF, s_aF, s_dG, s_pE, s_dH, s_aH, s_dI,
         s_pF, s_dJ) = (sem(f"s_{n}") for n in "pA dA aA dB pB dC aC dD pC dE pD dF aF dG pE dH aH dI pF dJ".split())
        s_h1 = sem("s_h1")
        s_h3 = sem("s_h3")
        s_sig = sem("s_sig")
        s_u = sem("s_u")
        s_t = sem("s_t")
        s_hi = sem("s_hi")
        s_lo = sem("s_lo")
        s_f2 = sem("s_f2")
        s_x2 = sem("s_x2")
        s_x1 = sem("s_x1")
        s_y = sem("s_y")

        block = ctx.enter_context(nc.Block())
        ds = bass.ds

        def rows_of(t, first, n):
            return t[ds(first * P, n * P), :].rearrange("(t p) c -> p t c", p=P)

        def split_to(c, half):
            n, k = divmod(c, SPLITS)
            if n == 2:
                return w2[:, half, :, :].rearrange("p t c -> p (t c)")[:, k * SCOL:(k + 1) * SCOL]
            kc, m = divmod(k, SPLITS // KC)
            return w13[:, n, kc, half, m * SCOL:(m + 1) * SCOL]

        @block.sync
        def _(sp):
            sp.dma_start(drow, dst_rows.rearrange("(p j) e -> p j e", j=EJ)).then_inc(s_rng, 16)

            def load_nodes(first, n, h, use):
                if some(use):
                    sp.wait_ge(s_xst[h], 48 * use)
                sp.dma_start(xin[h][:, 0:n, :], rows_of(x, first, n)).then_inc(s_x[h], 16)

            def store_nodes(first, n, h, part):
                sp.wait_ge(s_lnl, part + 1)
                sp.dma_start(rows_of(XH, first, n), xhb[h][:, 0:n, :]).then_inc(s_xst[h], 16)
                sp.dma_start(rows_of(XN, first, n), xin[h][:, 0:n, :]).then_inc(s_xst[h], 16)
                sp.wait_ge(s_lnc, part + 2)
                sp.dma_start(rows_of(XT, first, n), xtb[h][:, 0:n, :]).then_inc(s_xst[h], 16)

            def norms_and_nodes(i, following):
                for n, wn in enumerate((w1n, w3n)):
                    for m in range(2):
                        sp.wait_ge(s_ssq, 4 * i + 2 * n + 1)
                        sp.dma_start(nst[m], rows_of(wn, WCH * (2 * i + m), WCH)).then_inc(s_nw[m], 16)
                for h in range(2):
                    store_nodes(8 * i + 4 * h, 4, h, 2 * i + h)
                    if following[h]:
                        load_nodes(8 * i + 8 + 4 * h, following[h], h, i + 1)

            for h in range(2):
                load_nodes(4 * h, 4, h, 0)
            with sp.Fori(0, 5) as i:
                norms_and_nodes(i, (4, 4))
            norms_and_nodes(5, (1, 0))
            for dst_, src_ in ((wq_s[:, :, :], Wq), (wk_s[:, :, :], Wk), (wvt_s, WvT), (wo_s, Wo),
                               (rw_s[:, :, :], rwT), (wg_s[:, :, :], Wg)):
                sp.dma_start(dst_, src_.rearrange("(k p) c -> p k c", p=P)).then_inc(s_wld, 16)
            for dst_, src_ in ((bq_b, bq), (bk_b, bk), (bg_b, bg)):
                sp.dma_start(dst_[:, :], src_.broadcast_to((P, C))).then_inc(s_wld, 16)
            for k in range(KC):
                sp.dma_start(bv_s[:, k:k + 1], bv[k * P:(k + 1) * P, :]).then_inc(s_wld, 16)
            store_nodes(48, 1, 0, 12)
            for m in range(16):
                sp.wait_ge(s_ssq, 24 + max(m - 1, 0) + 1)
                sp.dma_start(nst2[m % 2], w2n[m * P:(m + 1) * P, :]).then_inc(s_nw[m % 2], 16)

            def load_window(t, par, n):
                if some(n):
                    sp.wait_ge(s_agg, n)
                first = sp.value_load(tab[0:1, 0, ds(t, 1)], min_val=0, max_val=ET - 1)
                sp.dma_start(srcw[:, par, :], srcT[:, ds(first, W)]).then_inc(s_win[par], 16)
                sp.dma_start(dstw[:, par, :], dstT[:, ds(first, W)]).then_inc(s_win[par], 16)

            def load_tile(t, par, n):
                if some(n):
                    sp.wait_ge(s_pD, n)
                sp.dma_start(xt[:, par, :], x[ds(t * P, P), :]).then_inc(s_tile[par], 16)
                sp.dma_start(xnt[:, par, :], XT[ds(t * P, P), :]).then_inc(s_tile[par], 16)

            sp.wait_ge(s_tab, 1)
            load_window(0, 0, 0)
            load_window(1, 1, 0)
            sp.wait_ge(s_xst[0], 48 * 7)
            sp.wait_ge(s_xst[1], 48 * 6)

            def load_keys(first, n, buf, done):
                sp.wait_ge(s_kx, done + 1)
                sp.dma_start(kxn[buf][:, 0:n, :], rows_of(XN, first, n)).then_inc(s_k[buf], 16)
                sp.dma_start(kxt[buf][:, 0:n, :], rows_of(XT, first, n)).then_inc(s_k[buf], 16)

            for buf in range(3):
                load_keys(4 * buf, 4, buf, 0)
            with sp.Fori(0, 3) as i:
                for buf in range(3):
                    load_keys(12 * i + 12 + 4 * buf, 4, buf, 12 * i + 4 * buf + 4)
            load_keys(48, 1, 0, 40)
            sp.wait_ge(s_kx, TILES + 1)
            sp.dma_start(bo_b, bo.broadcast_to((P, C))).then_inc(s_bo, 16)
            load_tile(0, 0, 0)
            load_tile(1, 1, 0)

            def load_split(c):
                n, k = divmod(c, SPLITS)
                if c < 2:
                    sp.wait_ge(s_mix, 1)
                else:
                    sp.wait_ge(s_wlo, c - 1)
                src_ = w13T[n, :, :] if n < 2 else w2T
                sp.dma_start(stage[c % 2], src_[:, k * SCOL:(k + 1) * SCOL]).then_inc(s_st[c % 2], 16)

            def store_gates(t, n):
                sp.wait_ge(s_dJ, n)
                sp.sem_inc(s_sp, 1)
                sp.dma_start(GT[:, ds(t * P, P)], gts[:, :]).then_inc(s_gst, 16)

            def load_gate(b, i, cols):
                slot = i % GSLOTS
                to = gate[:, slot * NB:slot * NB + cols]
                if i < EXP:
                    sp.dma_start(to, GT[i:i + 1, ds(b * NB, cols)].broadcast_to((P, cols))).then_inc(s_gld[slot], 16)
                    return
                for r0, r1, e in segments(HT_FULL + i - EXP):
                    sp.dma_start(to[r0:r1, :], GT[e:e + 1, ds(b * NB, cols)].broadcast_to((r1 - r0, cols)))\
                        .then_inc(s_gld[slot], 16)

            load_window(2, 0, 1)
            for p in range(BT):
                for c in range(6 * p, 6 * p + 6):
                    load_split(c)
                if p < BT - 1:
                    load_window(p + 3, (p + 3) % 2, p + 2)
                    load_tile(p + 2, p % 2, p + 1)
                store_gates(p, p + 1)
            sp.wait_ge(s_gst, 16 * BT)
            sp.wait_ge(s_wlo, 3 * SPLITS)
            for i in range(GSLOTS):
                load_gate(0, i, NB)

            def ffn_block(b, agg, tiles, cols, nxt):
                t0 = BT * b + BT
                for j in range(HT):
                    if agg and j % POST == 1 and j // POST in tiles:
                        q = j // POST
                        load_window(t0 + q + 2, q % 2, t0 + q + 1)
                        load_tile(t0 + q + 1, (q + 1) % 2, t0 + q)
                    if j and j % FULL == 0:
                        sp.wait_ge(s_t, HT * b + j)
                        sp.sem_inc(s_sp, 1)
                        load_gate(b, j // FULL - 1 + GSLOTS, cols)
                    if j % POST == 9 and j // POST in tiles:
                        store_gates(t0 + j // POST, t0 + j // POST + 1)
                if nxt:
                    sp.wait_ge(s_gst, 16 * (t0 + len(tiles)))
                    sp.sem_inc(s_sp, 1)
                    sp.wait_ge(s_t, HT * b + HT)
                    sp.sem_inc(s_sp, 1)
                    for i in range(GSLOTS):
                        load_gate(b + 1, i, nxt)
                for k in range(KC):
                    n = min(cols, NODES - NB * b) if isinstance(b, int) else cols
                    sp.wait_ge(s_y, KC * b + k + 2)
                    sp.dma_start(outT[k * P:(k + 1) * P, ds(b * NB, n)], x1a[:, k * NB:k * NB + n]).then_inc(s_out, 16)

            with sp.Fori(0, BLOCKS - 1) as b:
                ffn_block(b, True, range(BT), NB, NB)
            ffn_block(BLOCKS - 1, False, range(1), NB, P)
            ffn_block(BLOCKS, False, (), P, 0)
            sp.wait_ge(s_out, 16 * KC * (BLOCKS + 1) + 1)

        @block.gpsimd
        def _(pool):
            pool.iota(lane[:, :], [[1, P]], base=0, channel_multiplier=0, allow_small_or_imprecise_dtypes=True)\
                .then_inc(s_const, 1)
            pool.iota(lane8[:, :], [[1, EXP]], base=0, channel_multiplier=0, allow_small_or_imprecise_dtypes=True)\
                .then_inc(s_const, 1)
            pool.iota(base[:, :], [[P, TILES]], base=0, channel_multiplier=0, allow_small_or_imprecise_dtypes=True)\
                .then_inc(s_const, 1)
            pool.iota(kidx, [[1, EJ]], base=0, channel_multiplier=EJ, allow_small_or_imprecise_dtypes=True)\
                .then_inc(s_const, 1)
            pool.memset(one[:, :], 1.0).then_inc(s_const, 1)
            pool.memset(rows[:, :, 2 * C:2 * C + 2], 1.0).then_inc(s_const, 1)
            pool.memset(xrow[:, 2 * C:2 * C + 2], 1.0).then_inc(s_const, 1)
            pool.memset(ident[:, :], 0.0).then_inc(s_ident, 1)
            pool.wait_ge(s_ident, 1)
            pool.affine_select(out=ident[:, :], in_=ident[:, :], compare_op=ALU.not_equal, fill=1.0,
                               base=0, pattern=[[-1, P]], channel_multiplier=1).then_inc(s_ident, 1)
            pool.wait_ge(s_rloc, 1)
            pool.partition_all_reduce(rall, rloc, P, RMAX).then_inc(s_rall, 1)

            def gather_group(t, i, par):
                pool.wait_ge(s_used, GROUPS * t + i + 1)
                pool.sem_inc(s_pool, 1)
                g = i % RG
                for m in range(WG):
                    e = WG * i + m
                    pool.indirect_dma_start(rows[:, g * WG + m, 0:2 * C], None, XH,
                                            bass.IndirectOffsetOnAxis(ap=srcw[:, par, e:e + 1], axis=0))\
                        .then_inc(s_row[g], 16)

            def gather_extra(t):
                first = pool.value_load(tab[0:1, 0, ds(t, 1)], min_val=0, max_val=ET - 1)
                n = pool.value_load(tab[0:1, 1, ds(t, 1)], min_val=0, max_val=ET)
                done = pool.value_load(tab[0:1, 2, ds(t, 1)], min_val=0, max_val=ET * TILES)
                with pool.If(n > 0):
                    with pool.Fori(0, n) as i:
                        pool.wait_ge(s_xd, done + i + 1)
                        col = nc.s_assert_within(first + i + W, 0, ETW - 1,
                                                 skip_runtime_bounds_check_because="the table's counts end at the last edge tile")
                        pool.dma_start(xsrc[:, :], srcT[:, ds(col, 1)], allow_slow_non_contiguous=True).then_inc(s_xi, 16)
                        pool.dma_start(xdst[:, :], dstT[:, ds(col, 1)], allow_slow_non_contiguous=True).then_inc(s_xi, 16)
                        pool.wait_ge(s_xi, (done + i) * 32 + 32)
                        pool.sem_inc(s_xs, 1)
                        pool.indirect_dma_start(xrow[:, 0:2 * C], None, XH,
                                                bass.IndirectOffsetOnAxis(ap=xsrc[:, 0:1], axis=0)).then_inc(s_xr, 16)

            def gather_tile(t, par, use):
                pool.wait_ge(s_win[par], 32 * use)
                gather_group(t, 0, par)
                gather_extra(t)
                for i in range(1, GROUPS):
                    gather_group(t, i, par)

            pool.wait_ge(s_nloc, 1)
            pool.partition_all_reduce(sc[:, 4:7], sc[:, 0:3], P, RMAX).then_inc(s_nall, 1)
            pool.wait_ge(s_xst[0], 48 * 7)
            pool.wait_ge(s_xst[1], 48 * 6)
            for t in range(AHEAD):
                gather_tile(t, t % 2, t // 2 + 1)
            with pool.Fori(0, BLOCKS - 1) as b:
                for q in range(BT):
                    gather_tile(BT * b + AHEAD + q, (AHEAD + q) % 2, 2 * b + (AHEAD + q) // 2 + 1)

        @block.scalar
        def _(act):
            def norm_rows(n, i):
                for m in range(2):
                    act.wait_ge(s_nw[m], 16 * (2 * i + n) + 16)
                    for k in range(WCH):
                        last = act.activation(nst[m][:, k, :], nst[m][:, k, :], ACT.Square,
                                              accum_out=ssq[:, ds(8 * i + (NW13 * n + 4 * m + k), 1)])
                    last.then_inc(s_ssq, 1)

            def layer_norm(h, n, use, part):
                act.wait_ge(s_lnr, part + 1)
                for k in range(n):
                    last = act.activation(xin[h][:, k, :], xin[h][:, k, :], ACT.Identity,
                                          scale=sc[:, 16 + 8 * h + k:17 + 8 * h + k],
                                          bias=sc[:, 20 + 8 * h + k:21 + 8 * h + k])
                last.then_inc(s_lnx, 1)
                act.wait_ge(s_lnx, part + 1)
                act.activation(xhb[h][:, 0:n, 0:C], xin[h][:, 0:n, :], ACT.Copy, scale=XS).then_inc(s_lnh, 1)
                act.wait_ge(s_lnt, part + 1)
                for k in range((n + 1) // 2):
                    m = min(2, n - 2 * k)
                    last = act.activation(xtb[h][:, 2 * k:2 * k + m, :].rearrange("p t c -> p (t c)"),
                                          bank[2 + 2 * h + k][:, 0:m * C], ACT.Copy)
                last.then_inc(s_lnc, 1)

            with act.Fori(0, 6) as i:
                for h in range(2):
                    layer_norm(h, 4, i, 2 * i + h)
                    norm_rows(h, i)
            layer_norm(0, 1, 6, 12)
            for m in range(16):
                act.wait_ge(s_nw[m % 2], 16 * (12 + m // 2) + 16)
                act.activation(nst2[m % 2], nst2[m % 2], ACT.Square,
                               accum_out=ssq[:, 2 * NW13 + m:2 * NW13 + m + 1]).then_inc(s_ssq, 1)

            def key_square(n, k, first):
                act.wait_ge(s_kb, n + 2)
                act.activation(key2[k % 3], keyb[k % 3], ACT.Square, accum_out=sc[:, 32 + k % 3:33 + k % 3])\
                    .then_inc(s_k2, 1)

            def key_fourth(n, k):
                act.wait_ge(s_k2n, n + 1)
                act.activation(key4[k % 3], key2[k % 3], ACT.Square).then_inc(s_k4, 1)

            act.wait_ge(s_cst, 1)
            with act.Fori(0, 2) as turn:
                for k in range(24):
                    key_square(24 * turn + k, k, k == 0)
                    if k:
                        key_fourth(24 * turn + k - 1, k - 1)
                key_fourth(24 * turn + 23, 23)
            key_square(48, 0, False)
            key_fourth(48, 0)
            act.wait_ge(s_wvo, 1)
            act.activation(wvo[:, :, :].rearrange("p k c -> p (k c)"), bank[2][:, :], ACT.Copy).then_inc(s_wvc, 1)

            def split_high(c):
                act.wait_ge(s_st[c % 2], 16 * (c // 2 + 1))
                act.activation(split_to(c, 0), stage[c % 2], ACT.Copy,
                               scale=cst[:, c // SPLITS:c // SPLITS + 1]).then_inc(s_whi, 1)

            def update(t, q, stage_):
                if stage_ == "A":
                    act.wait_ge(s_dA, t + 1)
                    act.activation(tmp[:, 1, :], tmp[:, 1, :], ACT.Square, accum_out=sc[:, 0:1])
                    act.drain()
                    act.activation(tmp[:, 2, :], tmp[:, 1, :], ACT.Square, accum_out=sc[:, 1:2]).then_inc(s_aA, 1)
                if stage_ == "C":
                    act.wait_ge(s_dC, t + 1)
                    act.activation(tmp[:, 1, :], tmp[:, 1, :], ACT.Relu)
                    act.drain()
                    act.activation(tmp[:, 2, :], tmp[:, 1, :], ACT.Square, accum_out=sc[:, 2:3]).then_inc(s_aC, 1)
                if stage_ == "F":
                    act.wait_ge(s_dF, t + 1)
                    act.activation(x2s[:, 0:KC, q * P:(q + 1) * P],
                                   tmp[:, 0, :].rearrange("p (k n) -> p k n", k=KC), ACT.Copy).then_inc(s_aF, 1)
                if stage_ == "G":
                    act.wait_ge(s_dH, t + 1)
                    act.activation(sc[:, 72:80], sc[:, 64:72], ACT.Tanh, scale=1.0 / 16.0).then_inc(s_aH, 1)

            for p in range(BT):
                for k in range(POST):
                    if k in STAGES:
                        update(p, p, STAGES[k])
                    if k < 6:
                        split_high(6 * p + k)

            def ffn_block(b, tiles, cols):
                for j in range(HT):
                    act.wait_ge(s_u, HT * b + max(j - 1, 0) + 1)
                    act.wait_ge(s_h1, HT * b + j + 1)
                    act.activation(sig[:, (j % 2) * NB:(j % 2) * NB + cols], H1[j % 2][:, 0:cols], ACT.Silu,
                                   scale=cst[:, 3:4]).then_inc(s_sig, 1)
                    act.wait_ge(s_f2, HT * b + max(j - 2, 0) + 1)
                    act.wait_ge(s_t, HT * b + j + 1)
                    act.activation(hh[:, 2 * (j % 3), 0:cols], hid[:, (j % 2) * NB:(j % 2) * NB + cols], ACT.Copy)\
                        .then_inc(s_hi, 1)
                    if j == 3:
                        act.wait_ge(s_out, 16 * KC * b + 1)
                        act.activation(x1a[:, :], x1s[:, :], ACT.Copy).then_inc(s_x1, 1)
                    for q, s in stages_at(j, tiles):
                        update(BT * b + BT + q, q, s)

            with act.Fori(0, BLOCKS - 1) as b:
                ffn_block(b, range(BT), NB)
            ffn_block(BLOCKS - 1, range(1), NB)
            ffn_block(BLOCKS, (), P)

        @block.tensor
        def _(pe):
            pe.sem_inc(s_used, RG)
            for free in (s_xd, s_ssq, s_lnc, s_nei, s_kb, s_kx, s_y, s_u, s_f2, s_out):
                pe.sem_inc(free, 1)

            def transpose_nodes(h, n, part, done):
                pe.wait_ge(s_lnc, done + 1)
                pe.wait_ge(s_lnx, part + 1)
                for k in range(n):
                    for c in range(KC):
                        o = (k % 2) * C + c * P
                        last = pe.transpose(bank[2 + 2 * h + k // 2][:, o:o + P],
                                            xin[h][:, k, c * P:(c + 1) * P], ident[:, :])
                last.then_inc(s_lnt, 1)

            pe.wait_ge(s_ident, 2)
            with pe.Fori(0, 6) as i:
                for h in range(2):
                    transpose_nodes(h, 4, 2 * i + h, 2 * i)
            transpose_nodes(0, 1, 12, 12)

            def open_sum(bank_):
                pe.matmul(bank_[:, :], hot[:, 0, 0, :], hot[:, 0, :, :].rearrange("p a n -> p (a n)"),
                          start=True, stop=False, skip_group_check=True)

            def sum_group(t, i, turn=None):
                g = i % RG
                if i == 0:
                    pe.wait_ge(s_nei, t + 1)
                pe.wait_ge(s_row[g], (3 * t + i // RG) * 64 + 64)
                pe.wait_ge(s_hot, GROUPS * t + i + 1)
                for m in range(WG):
                    r = rows[:, g * WG + m, :]
                    pe.matmul(AG[:, 0:C], hot[:, g, m, :], r[:, 0:C], start=(i == 0 and m == 0), stop=False,
                              skip_group_check=True)
                    last = pe.matmul(AG[:, 0:C + 1], hot[:, g, m, :], r[:, C:2 * C + 1], start=False,
                                     stop=(i == GROUPS - 1 and m == WG - 1), skip_group_check=True)
                last.then_inc(s_used, 1)
                if i == 0:
                    n = pe.value_load(tab[0:1, 1, ds(t, 1)], min_val=0, max_val=ET)
                    done = pe.value_load(tab[0:1, 2, ds(t, 1)], min_val=0, max_val=ET * TILES)
                    with pe.If(n > 0):
                        with pe.Fori(0, n) as k:
                            pe.wait_ge(s_xr, (done + k) * 16 + 16)
                            pe.wait_ge(s_xh, done + k + 1)
                            pe.matmul(AG[:, 0:C], xhot[:, :], xrow[:, 0:C], start=False, stop=False,
                                      skip_group_check=True)
                            pe.matmul(AG[:, 0:C + 1], xhot[:, :], xrow[:, C:2 * C + 1], start=False, stop=False,
                                      skip_group_check=True).then_inc(s_xd, 1)
                if i == GROUPS - 1:
                    pe.drain().then_inc(s_agg, 1)

            def key_product(n, k):
                buf, m = (k // 4) % 3, k % 4
                pe.wait_ge(s_kb, n - 1 if k > 1 else n - k + 1)
                for c in range(KC):
                    last = pe.matmul(bank[2 + k % 3][:, 0:C], kxt[buf][:, m, c * P:(c + 1) * P], wk_s[:, c, :],
                                     start=(c == 0), stop=(c == KC - 1))
                last.then_inc(s_kp, 1)

            def key_sum(n, k, rows_):
                buf, m = (k // 4) % 3, k % 4
                pe.wait_ge(s_k4, n + 1)
                for c in range(KC):
                    pe.matmul(Y[0][:, c * C:(c + 1) * C], kxn[buf][0:rows_, m, c * P:(c + 1) * P],
                              key2[k % 3][0:rows_, :], start=False, stop=False, skip_group_check=True)
                for a, kk in enumerate((key2, key4)):
                    for c in range(KC):
                        last = pe.matmul(Y[1][:, 2 * a + c:2 * a + c + 1], kk[k % 3][0:rows_, c * P:(c + 1) * P],
                                         one[0:rows_, :], start=False, stop=False, skip_group_check=True)
                last.then_inc(s_kx, 1)

            pe.wait_ge(s_cent, 1)
            pe.wait_ge(s_lnc, 14)
            pe.wait_ge(s_zero, 1)
            open_sum(Y[0])
            open_sum(Y[1])
            pe.drain().then_inc(s_zero, 1)
            with pe.Fori(0, 2) as turn:
                for k in range(24 + 2):
                    if k < 24:
                        if k % 4 == 0:
                            pe.wait_ge(s_k[(k // 4) % 3], turn * 64 + 32 * (k // 12) + 32)
                        key_product(24 * turn + k, k)
                    if k >= 2:
                        key_sum(24 * turn + k - 2, k - 2, P)
                    if k % 2 and 5 <= k <= 21:
                        sum_group(turn, (k - 5) // 2)
            pe.wait_ge(s_k[0], 4 * 32 + 32)
            key_product(48, 0)
            key_sum(48, 0, LAST)
            pe.wait_ge(s_kb, TILES + 1)
            for k in range(KC):
                for d in range(KC):
                    pe.matmul(bank[2][:, k * C:(k + 1) * C], wvt_s[:, d, k * P:(k + 1) * P], wo_s[:, d, :],
                              start=(d == 0), stop=(d == KC - 1))
            for d in range(KC):
                last = pe.matmul(bank[3][:, 0:C], bvr[:, d, :], wo_s[:, d, :], start=(d == 0), stop=(d == KC - 1))
            last.then_inc(s_wvo, 1)
            pe.wait_ge(s_wvc, 1)
            pe.wait_ge(s_kxs, 1)
            for k in range(KC):
                for d in range(KC):
                    last = pe.matmul(bank[4][:, k * C:(k + 1) * C], kxs[:, d, k * P:(k + 1) * P], wvo[:, d, :],
                                     start=(d == 0), stop=(d == KC - 1))
            last.then_inc(s_mp, 1)

            def update(t, q, stage_):
                par = q % 2
                if stage_ == "A":
                    pe.wait_ge(s_nei, t + 2)
                    if some(t):
                        pe.wait_ge(s_dJ, t)
                    for c in range(KC):
                        pe.transpose(PB[:, c * P:(c + 1) * P], neigh[:, par, c * P:(c + 1) * P], ident[:, :])
                    pe.wait_ge(s_tile[par], 32 * ((t - q) // 2 + q // 2) + 32 if isinstance(t, int)
                               else (t - q) * 16 + 32 * (q // 2) + 32)
                    for c in range(KC):
                        last = pe.matmul(PB[:, C:2 * C], xnt[:, par, c * P:(c + 1) * P], wq_s[:, c, :],
                                         start=(c == 0), stop=(c == KC - 1))
                    last.then_inc(s_pA, 1)
                if stage_ == "C":
                    pe.wait_ge(s_dB, t + 1)
                    for c in range(KC):
                        pe.transpose(PB[:, c * P:(c + 1) * P], tmp[:, 3, c * P:(c + 1) * P], ident[:, :])
                    for c in range(2 * KC):
                        lhs = xnt[:, par, c * P:(c + 1) * P] if c < KC else tmp[:, 0, (c - KC) * P:(c - KC + 1) * P]
                        last = pe.matmul(PB[:, C:2 * C], lhs, wg_s[:, c, :], start=(c == 0), stop=(c == 2 * KC - 1))
                    last.then_inc(s_pB, 1)
                if stage_ == "D":
                    pe.wait_ge(s_dC, t + 1)
                    for c in range(2 * KC):
                        lhs = xnt[:, par, c * P:(c + 1) * P] if c < KC else tmp[:, 4, (c - KC) * P:(c - KC + 1) * P]
                        last = pe.matmul(PB[:, 0:C], lhs, (wvo if c < KC else mix)[:, c % KC, :],
                                         start=(c == 0), stop=(c == 2 * KC - 1))
                    last.then_inc(s_pC, 1)
                if stage_ == "F":
                    pe.wait_ge(s_dE, t + 1)
                    for c in range(KC):
                        pe.transpose(PB[:, c * P:(c + 1) * P], xt[:, par, c * P:(c + 1) * P], ident[:, :])
                        last = pe.transpose(PB[:, C + c * P:C + (c + 1) * P], tmp[:, 3, c * P:(c + 1) * P], ident[:, :])
                    last.then_inc(s_pD, 1)
                if stage_ == "G":
                    pe.wait_ge(s_dF, t + 1)
                    for c in range(KC):
                        last = pe.matmul(PB[:, 0:EXP], tmp[:, 0, c * P:(c + 1) * P], rw_s[:, c, :],
                                         start=(c == 0), stop=(c == KC - 1))
                    last.then_inc(s_pE, 1)
                if stage_ == "I":
                    pe.wait_ge(s_dI, t + 1)
                    pe.transpose(PB[0:EXP, 0:P], sc[:, 56:64], ident[:, :]).then_inc(s_pF, 1)

            pe.wait_ge(s_mix, 1)
            for p in range(BT):
                for k in range(POST):
                    if k in STAGES:
                        update(p, p, STAGES[k])
                    if p < BT - 1 and k < GROUPS:
                        sum_group(p + 2, k)

            def second(b, j, cols):
                pe.wait_ge(s_lo, HT * b + j + 1)
                if j == 0:
                    pe.wait_ge(s_y, KC * b + 1)
                hi, lo = hh[:, 2 * (j % 3), 0:cols], hh[:, 2 * (j % 3) + 1, 0:cols]
                for c in range(KC):
                    whi, wlo = w2[:, 0, j, c * P:(c + 1) * P], w2[:, 1, j, c * P:(c + 1) * P]
                    o = Y[c][:, 0:cols]
                    pe.matmul(o, whi, hi, start=(j == 0), stop=False)
                    pe.matmul(o, whi, lo, start=False, stop=False)
                    last = pe.matmul(o, wlo, hi, start=False, stop=(j == HT - 1))
                last.then_inc(s_f2, 1)

            def ffn_block(b, agg, tiles, cols):
                pe.wait_ge(s_x2, b + 1)
                for j in range(HT):
                    pe.wait_ge(s_u, HT * b + max(j - 1, 0) + 1)
                    for n, (H, done) in enumerate(((H1, s_h1), (H3, s_h3))):
                        o = H[j % 2][:, 0:cols]
                        for c in range(KC):
                            whi, wlo = (w13[:, n, c, h, j * P:(j + 1) * P] for h in range(2))
                            xhi, xlo = x2a[:, c, 0:cols], x2a[:, KC + c, 0:cols]
                            pe.matmul(o, whi, xhi, start=(c == 0), stop=False)
                            pe.matmul(o, whi, xlo, start=False, stop=False)
                            last = pe.matmul(o, wlo, xhi, start=False, stop=(c == KC - 1))
                        last.then_inc(done, 1)
                    if j >= 2:
                        second(b, j - 2, cols)
                    if agg:
                        for q, i in GROUP_AT[j]:
                            sum_group(BT * b + AHEAD + q, i)
                    for q, s in stages_at(j, tiles):
                        update(BT * b + BT + q, q, s)
                second(b, HT - 2, cols)
                second(b, HT - 1, cols)

            pe.wait_ge(s_wlo, 3 * SPLITS)
            with pe.Fori(0, BLOCKS - 1) as b:
                ffn_block(b, True, range(BT), NB)
            ffn_block(BLOCKS - 1, False, range(1), NB)
            ffn_block(BLOCKS, False, (), P)

        @block.vector
        def _(dve):
            def link(_=None):
                dve.drain()

            def rsqrt(y, v, t):
                link()
                dve.tensor_scalar(t.bitcast(I32), v.bitcast(I32), 1, None, ALU.logical_shift_right)
                link()
                dve.tensor_scalar(y.bitcast(I32), t.bitcast(I32), -1.0, RSQRT_MAGIC, ALU.mult, ALU.add)
                for _ in range(3):
                    link()
                    dve.tensor_tensor(t, y, y, ALU.mult)
                    link()
                    dve.tensor_tensor(t, t, v, ALU.mult)
                    link()
                    dve.tensor_scalar(t, t, -0.5, 1.5, ALU.mult, ALU.add)
                    link()
                    dve.tensor_tensor(y, y, t, ALU.mult)
                link()

            def rsqrt1(y, v, t):
                link()
                dve.tensor_scalar(t.bitcast(I32), v.bitcast(I32), 1, None, ALU.logical_shift_right)
                link()
                dve.tensor_scalar(y.bitcast(I32), t.bitcast(I32), -1.0, RSQRT_MAGIC, ALU.mult, ALU.add)
                for _ in range(3):
                    link()
                    dve.tensor_scalar(t, y, v, y, ALU.mult, ALU.mult)
                    link()
                    dve.tensor_scalar(t, t, -0.5, 1.5, ALU.mult, ALU.add)
                    link()
                    dve.tensor_tensor(y, y, t, ALU.mult)
                link()

            dve.memset(hot[:, :, :, :], 0.0).then_inc(s_zero, 1)
            dve.memset(tab[:, :, :], 0)
            dve.memset(ssq, 0.0)
            dve.wait_ge(s_rng, 16)
            dve.wait_ge(s_const, 7)
            dve.tensor_reduce(dmin, drow, AX.X, ALU.min)
            dve.tensor_reduce(dmax, drow, AX.X, ALU.max)
            link()
            by_tile = (P, TILES, EJ)
            thr = base[:, :, None].broadcast_to(by_tile)
            kk = kidx[:, None, :].broadcast_to(by_tile)
            dve.tensor_tensor(ra, dmax[:, None, :].broadcast_to(by_tile), thr, ALU.subtract)
            link()
            dve.tensor_scalar(rb, ra, 0.0, 1.0e6, ALU.is_lt, ALU.mult)
            link()
            dve.tensor_tensor(ra, rb, kk, ALU.add)
            link()
            dve.tensor_reduce(rall[:, 0:TILES], ra, AX.X, ALU.min)
            link()
            dve.tensor_scalar(rloc[:, 0:TILES], rall[:, 0:TILES], -1.0, None, ALU.mult)
            dve.tensor_tensor(ra, dmin[:, None, :].broadcast_to(by_tile), thr, ALU.subtract)
            link()
            dve.tensor_scalar(rb, ra, float(P), None, ALU.is_lt)
            link()
            dve.tensor_tensor(ra, rb, kk, ALU.mult)
            link()
            dve.tensor_tensor(ra, ra, rb, ALU.add)
            link()
            dve.tensor_reduce(rloc[:, TILES:2 * TILES], ra, AX.X, ALU.max)
            dve.drain().then_inc(s_rloc, 1)

            def node_scales(h, n, use, part):
                dve.wait_ge(s_x[h], 16 * use + 16)
                st = sc[:, 40:64].rearrange("p (t s) -> p t s", s=6)
                mv = sc[:, 64:72].rearrange("p (t s) -> p t s", s=2)
                for k in range(n):
                    dve.bn_stats(st[:, k, :], xin[h][:, k, :])
                link()
                for k in range(n):
                    dve.bn_aggr(mv[:, k, :], st[:, k, :])
                link()
                v, t = sc[:, 72:72 + n], sc[:, 76:76 + n]
                y, sh = sc[:, 16 + 8 * h:16 + 8 * h + n], sc[:, 20 + 8 * h:20 + 8 * h + n]
                dve.tensor_scalar(v, mv[:, 0:n, 1], EPS_LN, None, ALU.add)
                rsqrt(y, v, t)
                dve.tensor_tensor(t, mv[:, 0:n, 0], y, ALU.mult)
                link()
                dve.tensor_scalar(sh, t, -1.0, None, ALU.mult).then_inc(s_lnr, 1)

            def node_low(h, n, part):
                dve.wait_ge(s_lnh, part + 1)
                dve.scalar_tensor_tensor(out=xhb[h][:, 0:n, C:2 * C], in0=xin[h][:, 0:n, :], scalar=XS,
                                         in1=xhb[h][:, 0:n, 0:C], op0=ALU.mult, op1=ALU.subtract).then_inc(s_lnl, 1)

            node_scales(0, 4, 0, 0)
            node_scales(1, 4, 0, 1)
            with dve.Fori(0, 5) as i:
                for h in range(2):
                    node_low(h, 4, 2 * i + h)
                    node_scales(h, 4, i + 1, 2 * i + 2 + h)
            node_low(0, 4, 10)
            node_scales(0, 1, 6, 12)
            node_low(1, 4, 11)
            node_low(0, 1, 12)

            dve.wait_ge(s_rall, 1)
            dve.tensor_scalar(rall[:, 0:TILES], rall[:, 0:TILES], -1.0, float(ET - 1), ALU.mult, ALU.min)
            link()
            dve.tensor_copy(tab[:, 0, 0:TILES], rall[:, 0:TILES])
            dve.tensor_tensor(run[0], rall[:, TILES:2 * TILES], rall[:, 0:TILES], ALU.subtract)
            link()
            dve.tensor_scalar(run[0], run[0], -float(W), 0.0, ALU.add, ALU.max)
            link()
            dve.tensor_copy(tab[:, 1, 0:TILES], run[0])
            dve.tensor_copy(rall[:, 0:TILES], run[0])
            a, b_ = run
            for step in (1, 2, 4, 8, 16, 32):
                link()
                dve.tensor_copy(b_[:, 0:step], a[:, 0:step])
                dve.tensor_tensor(b_[:, step:TILES], a[:, step:TILES], a[:, 0:TILES - step], ALU.add)
                a, b_ = b_, a
            link()
            dve.tensor_tensor(a, a, rall[:, 0:TILES], ALU.subtract)
            link()
            dve.tensor_copy(tab[:, 2, 0:TILES], a)
            dve.drain().then_inc(s_tab, 1)

            dve.wait_ge(s_wld, 16 * 11)
            for i, wgt in enumerate((wq_s[:, 0, :], wq_s[:, 1, :], wk_s[:, 0, :], wk_s[:, 1, :], bq_b[:, :], bk_b[:, :])):
                dve.tensor_reduce(sc[:, 80 + i:81 + i], wgt, AX.X, ALU.add)
            link()
            dve.tensor_scalar(sc[:, 88:94], sc[:, 80:86], 1.0 / C, None, ALU.mult)
            link()
            for i, wgt in enumerate((wq_s[:, 0, :], wq_s[:, 1, :], wk_s[:, 0, :], wk_s[:, 1, :], bq_b[:, :], bk_b[:, :])):
                dve.tensor_scalar(wgt, wgt, sc[:, 88 + i:89 + i], None, ALU.subtract)
            for k in range(KC):
                dve.tensor_scalar(bvr[:, k, :], ident[:, :], 0.0, bv_s[:, k:k + 1], ALU.mult, ALU.add)
            dve.drain().then_inc(s_cent, 1)

            dve.wait_ge(s_ssq, 24 + 16 + 1)
            dve.tensor_reduce(sc[:, 0:2], ssq[:, 0:2 * NW13].rearrange("p (n t) -> p n t", n=2), AX.X, ALU.max)
            dve.tensor_reduce(sc[:, 2:3], ssq[:, 2 * NW13:2 * NW13 + 16], AX.X, ALU.max)
            dve.drain().then_inc(s_nloc, 1)

            def weight_scales():
                dve.wait_ge(s_nall, 1)
                dve.tensor_scalar(sc[:, 8:11], sc[:, 4:7], TINY, None, ALU.max)
                rsqrt(sc[:, 12:15], sc[:, 8:11], sc[:, 28:31])
                dve.tensor_tensor(sc[:, 8:11], sc[:, 8:11], sc[:, 12:15], ALU.mult)
                link()
                dve.tensor_scalar(sc[:, 8:11], sc[:, 8:11], 1.0001, None, ALU.mult)
                link()
                p = sc[:, 12:15]
                dve.tensor_scalar(p.bitcast(I32), sc[:, 8:11].bitcast(I32), 0x7F800000, None, ALU.bitwise_and)
                link()
                dve.tensor_scalar(cst[:, 0:3].bitcast(I32), p.bitcast(I32), -1.0, float((127 + 127 + 13) << 23),
                                  ALU.mult, ALU.add)
                dve.tensor_scalar(cst[:, 3:4], p[:, 0:1], 2.0 ** -23, None, ALU.mult)
                dve.tensor_tensor(cst[:, 5:6], p[:, 0:1], p[:, 1:2], ALU.mult)
                link()
                dve.tensor_scalar(cst[:, 4:5], cst[:, 0:1], 2.0 ** -31, None, ALU.mult)
                dve.tensor_scalar(cst[:, 5:6], cst[:, 5:6], p[:, 2:3], 2.0 ** -18, ALU.mult, ALU.mult)
                dve.drain().then_inc(s_cst, 1)

            def window(t, par, use, col=None):
                dve.wait_ge(s_win[par], 32 * use)
                dve.tensor_scalar(dstf[:, par, :], dstw[:, par, :], base[:, ds(t, 1)], None, ALU.subtract)
                link()

            def one_hots(t, i, par):
                dve.wait_ge(s_used, GROUPS * t + i + 1)
                dve.tensor_tensor(hot[:, i % RG, :, :], lane[:, None, :].broadcast_to((P, WG, P)),
                                  par_dst(par)[:, WG * i:WG * i + WG, None].broadcast_to((P, WG, P)), ALU.is_equal)\
                    .then_inc(s_hot, 1)
                if i == 0:
                    one_hots_extra(t)

            def par_dst(par):
                return dstf[:, par, :]

            def one_hots_extra(t):
                n = dve.value_load(tab[0:1, 1, ds(t, 1)], min_val=0, max_val=ET)
                done = dve.value_load(tab[0:1, 2, ds(t, 1)], min_val=0, max_val=ET * TILES)
                with dve.If(n > 0):
                    with dve.Fori(0, n) as k:
                        dve.wait_ge(s_xs, done + k + 1)
                        dve.wait_ge(s_xd, done + k + 1)
                        dve.tensor_scalar(xdf[:, :], xdst[:, :], base[:, ds(t, 1)], None, ALU.subtract)
                        dve.drain()
                        dve.tensor_scalar(xhot[:, :], lane[:, :], xdf[:, 0:1], None, ALU.is_equal).then_inc(s_xh, 1)

            def neighbours(t, par):
                dve.wait_ge(s_agg, t + 1)
                dve.tensor_scalar(sc[:, 34:35], AG[:, C:C + 1], 1.0, None, ALU.max)
                link()
                dve.reciprocal(sc[:, 35:36], sc[:, 34:35])
                link()
                dve.tensor_scalar(neigh[:, par, :], AG[:, 0:C], sc[:, 35:36], 1.0 / XS, ALU.mult, ALU.mult)\
                    .then_inc(s_nei, 1)

            def key_bias(n, k):
                dve.wait_ge(s_kx, n - 1 if k > 2 else n - k + 1)
                dve.wait_ge(s_kp, n + 1)
                dve.tensor_tensor(keyb[k % 3], bank[2 + k % 3][:, 0:C], bk_b[:, :], ALU.add).then_inc(s_kb, 1)

            def key_divide(n, k):
                dve.wait_ge(s_k2, n + 1)
                c = 32 + k % 3
                dve.tensor_scalar(sc[:, c + 4:c + 5], sc[:, c:c + 1], EPS_DIV, None, ALU.add)
                link()
                dve.reciprocal(sc[:, c + 8:c + 9], sc[:, c + 4:c + 5])
                link()
                dve.tensor_scalar(key2[k % 3], key2[k % 3], sc[:, c + 8:c + 9], None, ALU.mult).then_inc(s_k2n, 1)

            weight_scales()
            window(0, 0, 1)
            window(1, 1, 1)
            dve.drain()
            with dve.Fori(0, 2) as turn:
                for k in range(24 + 1):
                    if k < 24:
                        key_bias(24 * turn + k, k)
                    if k:
                        key_divide(24 * turn + k - 1, k - 1)
                    if k % 2 and 5 <= k <= 21:
                        i = (k - 5) // 2
                        dve.wait_ge(s_used, GROUPS * turn + i + 1)
                        dve.tensor_tensor(hot[:, i % RG, :, :], lane[:, None, :].broadcast_to((P, WG, P)),
                                          dstf[:, :, :].rearrange("p a w -> p (a w)")[:, ds(turn * W + WG * i, WG)]
                                          [:, :, None].broadcast_to((P, WG, P)), ALU.is_equal).then_inc(s_hot, 1)
                        if i == 0:
                            one_hots_extra(turn)
                dve.wait_ge(s_agg, turn + 1)
                dve.tensor_scalar(sc[:, 10:11], AG[:, C:C + 1], 1.0, None, ALU.max)
                link()
                dve.reciprocal(sc[:, 11:12], sc[:, 10:11])
                link()
                dve.tensor_scalar(neigh[:, :, :].rearrange("p a c -> p (a c)")[:, ds(turn * C, C)], AG[:, 0:C],
                                  sc[:, 11:12], 1.0 / XS, ALU.mult, ALU.mult).then_inc(s_nei, 1)
            key_bias(48, 0)
            key_divide(48, 0)

            dve.wait_ge(s_kx, TILES + 1)
            dve.tensor_copy(kxs.rearrange("p k c -> p (k c)"), Y[0][:, :]).then_inc(s_kxs, 1)
            dve.tensor_copy(sc[:, 0:4], Y[1][:, 0:4])
            link()
            dve.tensor_scalar(sc[:, 4:6], sc[:, 2:4], TINY, None, ALU.max)
            rsqrt(sc[:, 8:10], sc[:, 4:6], sc[:, 12:14])
            dve.tensor_tensor(sc[:, 4:6], sc[:, 4:6], sc[:, 8:10], ALU.mult)
            link()
            dve.tensor_scalar(sc[:, 4:6], sc[:, 4:6], EPS_NORM, None, ALU.max)
            link()
            dve.reciprocal(sc[:, 8:10], sc[:, 4:6])
            dve.wait_ge(s_wvo, 1)
            dve.wait_ge(s_bo, 16)
            dve.tensor_copy(sbv, bank[3][:, 0:C])
            link()
            dve.tensor_tensor(co_b[:, :], sbv, bo_b, ALU.add)
            dve.wait_ge(s_mp, 1)
            for k in range(KC):
                dve.scalar_tensor_tensor(out=mix[:, k, :], in0=sbv, scalar=sc[:, k:k + 1],
                                         in1=bank[4][:, k * C:(k + 1) * C], op0=ALU.mult, op1=ALU.add)
            link()
            for k in range(KC):
                last = dve.tensor_scalar(mix[:, k, :], mix[:, k, :], sc[:, 8 + k:9 + k], float(NODES) ** -0.5,
                                         ALU.mult, ALU.mult)
            dve.drain().then_inc(s_mix, 1)

            def update(t, q, stage_, b=None):
                par = q % 2
                if stage_ == "A":
                    dve.wait_ge(s_pA, t + 1)
                    dve.tensor_copy(tmp[:, 0, :], PB[:, 0:C])
                    dve.tensor_tensor(tmp[:, 1, :], PB[:, C:2 * C], bq_b[:, :], ALU.add)
                    dve.drain().then_inc(s_dA, 1)
                if stage_ == "B":
                    dve.wait_ge(s_aA, t + 1)
                    dve.tensor_scalar(sc[:, 3:4], sc[:, 0:1], EPS_DIV, None, ALU.add)
                    dve.tensor_scalar(sc[:, 4:5], sc[:, 1:2], TINY, None, ALU.max)
                    link()
                    dve.reciprocal(sc[:, 5:6], sc[:, 3:4])
                    rsqrt1(sc[:, 6:7], sc[:, 4:5], sc[:, 7:8])
                    dve.tensor_tensor(sc[:, 7:8], sc[:, 4:5], sc[:, 6:7], ALU.mult)
                    link()
                    dve.tensor_scalar(sc[:, 6:7], sc[:, 7:8], sc[:, 5:6], EPS_NORM, ALU.mult, ALU.max)
                    link()
                    dve.reciprocal(sc[:, 7:8], sc[:, 6:7])
                    link()
                    dve.tensor_scalar(tmp[:, 3, :], tmp[:, 1, :], sc[:, 5:6], sc[:, 7:8], ALU.mult, ALU.mult)\
                        .then_inc(s_dB, 1)
                if stage_ == "C":
                    dve.wait_ge(s_pB, t + 1)
                    dve.tensor_copy(tmp[:, 4, :], PB[:, 0:C])
                    dve.tensor_tensor(tmp[:, 1, :], PB[:, C:2 * C], bg_b[:, :], ALU.add)
                    dve.drain().then_inc(s_dC, 1)
                if stage_ == "D":
                    dve.wait_ge(s_aC, t + 1)
                    dve.tensor_scalar(sc[:, 4:5], sc[:, 2:3], TINY, None, ALU.max)
                    rsqrt1(sc[:, 6:7], sc[:, 4:5], sc[:, 7:8])
                    dve.tensor_tensor(sc[:, 7:8], sc[:, 4:5], sc[:, 6:7], ALU.mult)
                    link()
                    dve.tensor_scalar(sc[:, 6:7], sc[:, 7:8], EPS_NORM, None, ALU.max)
                    link()
                    dve.reciprocal(sc[:, 7:8], sc[:, 6:7])
                    link()
                    dve.scalar_tensor_tensor(out=xt[:, par, :], in0=tmp[:, 1, :], scalar=sc[:, 7:8],
                                             in1=xt[:, par, :], op0=ALU.mult, op1=ALU.add)
                    link()
                    dve.tensor_tensor(xt[:, par, :], xt[:, par, :], co_b[:, :], ALU.add)
                    link()
                    dve.wait_ge(s_pC, t + 1)
                    dve.tensor_tensor(xt[:, par, :], PB[:, 0:C], xt[:, par, :], ALU.add)
                    link()
                if stage_ == "E":
                    dve.bn_stats(sc[:, 8:14], xt[:, par, :])
                    link()
                    dve.bn_aggr(sc[:, 14:16], sc[:, 8:14])
                    link()
                    dve.tensor_scalar(sc[:, 4:5], sc[:, 15:16], EPS_LN, None, ALU.add)
                    rsqrt1(sc[:, 6:7], sc[:, 4:5], sc[:, 7:8])
                    dve.tensor_scalar(tmp[:, 3, :], xt[:, par, :], sc[:, 14:15], sc[:, 6:7],
                                      ALU.subtract, ALU.mult).then_inc(s_dE, 1)
                if stage_ == "F":
                    dve.wait_ge(s_pD, t + 1)
                    if b is not None:
                        dve.wait_ge(s_x1, b + 1)
                    dve.tensor_copy(x1s[:, :].rearrange("p (k n) -> p k n", k=KC)[:, :, q * P:(q + 1) * P],
                                    PB[:, 0:C].rearrange("p (k n) -> p k n", k=KC))
                    dve.tensor_scalar(tmp[:, 0, :], PB[:, C:2 * C], XS, None, ALU.mult)
                    dve.drain().then_inc(s_dF, 1)
                if stage_ == "G":
                    dve.wait_ge(s_aF, t + 1)
                    dve.tensor_tensor(x2s[:, KC:2 * KC, q * P:(q + 1) * P],
                                      tmp[:, 0, :].rearrange("p (k n) -> p k n", k=KC),
                                      x2s[:, 0:KC, q * P:(q + 1) * P], ALU.subtract).then_inc(s_dG, 1)
                    dve.wait_ge(s_pE, t + 1)
                    dve.tensor_scalar(sc[:, 40:48], PB[:, 0:EXP], 1.0 / XS, None, ALU.mult)
                    link()
                    dve.max(sc[:, 48:56], sc[:, 40:48])
                    link()
                    dve.max_index(idx8[:, :], sc[:, 48:56], sc[:, 40:48])
                    dve.tensor_scalar(sc[:, 64:72], sc[:, 48:56], sc[:, 48:49], None, ALU.subtract)
                    dve.drain().then_inc(s_dH, 1)
                if stage_ == "H":
                    dve.wait_ge(s_aH, t + 1)
                    ex, de = sc[:, 80:88], sc[:, 88:96]
                    dve.tensor_scalar(ex, sc[:, 72:80], 1.0, None, ALU.add)
                    dve.tensor_scalar(de, sc[:, 72:80], -1.0, 1.0, ALU.mult, ALU.add)
                    link()
                    dve.reciprocal(sc[:, 64:72], de)
                    link()
                    dve.tensor_tensor(ex, ex, sc[:, 64:72], ALU.mult)
                    for _ in range(3):
                        link()
                        dve.tensor_tensor(ex, ex, ex, ALU.mult)
                    link()
                    dve.tensor_reduce(sc[:, 3:4], ex, AX.X, ALU.add)
                    dve.tensor_copy(sc[:, 72:74], idx8[:, 0:2])
                    link()
                    dve.reciprocal(sc[:, 4:5], sc[:, 3:4])
                    link()
                    dve.tensor_scalar(sc[:, 88:90], ex[:, 0:2], sc[:, 4:5], None, ALU.mult)
                    link()
                    dve.tensor_scalar(sc[:, 5:6], sc[:, 88:89], sc[:, 89:90], 1e-9, ALU.add, ALU.add)
                    link()
                    dve.reciprocal(sc[:, 6:7], sc[:, 5:6])
                    link()
                    dve.tensor_scalar(sc[:, 90:92], sc[:, 88:90], sc[:, 6:7], None, ALU.mult)
                    link()
                    dve.tensor_scalar(sc[:, 40:48], lane8[:, :], sc[:, 72:73], sc[:, 90:91], ALU.is_equal, ALU.mult)
                    dve.tensor_scalar(sc[:, 48:56], lane8[:, :], sc[:, 73:74], sc[:, 91:92], ALU.is_equal, ALU.mult)
                    link()
                    dve.tensor_tensor(sc[:, 56:64], sc[:, 40:48], sc[:, 48:56], ALU.add).then_inc(s_dI, 1)
                if stage_ == "I":
                    if some(t):
                        dve.wait_ge(s_gst, t * 16)
                    dve.wait_ge(s_pF, t + 1)
                    dve.tensor_copy(gts[:, :], PB[0:EXP, 0:P]).then_inc(s_dJ, 1)

            def split_low(c):
                dve.wait_ge(s_whi, c + 1)
                dve.scalar_tensor_tensor(out=split_to(c, 1), in0=stage[c % 2],
                                         scalar=cst[:, c // SPLITS:c // SPLITS + 1], in1=split_to(c, 0),
                                         op0=ALU.mult, op1=ALU.subtract).then_inc(s_wlo, 1)

            for p in range(BT):
                for k in range(POST):
                    if p < BT - 1 and k < GROUPS:
                        if k == 0:
                            window(p + 2, p % 2, (p + 2) // 2 + 1)
                        one_hots(p + 2, k, p % 2)
                    if k in STAGES:
                        update(p, p, STAGES[k])
                    if k < 6:
                        split_low(6 * p + k)
                    if p < BT - 1 and k == 9:
                        neighbours(p + 2, p % 2)

            def take_input(b, n):
                dve.drain()
                dve.wait_ge(s_aF, n)
                dve.wait_ge(s_h3, HT * b)
                dve.tensor_copy(x2a[:, :, :], x2s[:, :, :]).then_inc(s_x2, 1)

            take_input(0, BT)

            def low(b, j, cols):
                dve.wait_ge(s_hi, HT * b + j + 1)
                dve.tensor_tensor(hh[:, 2 * (j % 3) + 1, 0:cols], hid[:, (j % 2) * NB:(j % 2) * NB + cols],
                                  hh[:, 2 * (j % 3), 0:cols], ALU.subtract).then_inc(s_lo, 1)

            def ffn_block(b, agg, tiles, cols, nxt):
                for j in range(HT):
                    if agg:
                        for q, i in (GROUP_AT[0] if j == 0 else []) + (GROUP_AT[j + 1] if j + 1 < HT else []):
                            t, par = BT * b + AHEAD + q, (AHEAD + q) % 2
                            if i == 0:
                                window(t, par, 2 * b + (AHEAD + q) // 2 + 1)
                            one_hots(t, i, par)
                    s, h = (sig[:, (j % 2) * NB:(j % 2) * NB + cols], hid[:, (j % 2) * NB:(j % 2) * NB + cols])
                    dve.wait_ge(s_h3, HT * b + j + 1)
                    dve.wait_ge(s_sig, HT * b + j + 1)
                    dve.scalar_tensor_tensor(out=h, in0=H3[j % 2][:, 0:cols], scalar=cst[:, 4:5], in1=s,
                                             op0=ALU.mult, op1=ALU.mult).then_inc(s_u, 1)
                    if j:
                        low(b, j - 1, cols)
                    i = j // FULL if j < HT_FULL else EXP + j - HT_FULL
                    if j % FULL == 0 or j >= HT_FULL:
                        dve.wait_ge(s_gld[i % GSLOTS], gate_count(b, i))
                    dve.wait_ge(s_u, HT * b + j + 2)
                    g = gate[:, (i % GSLOTS) * NB:(i % GSLOTS) * NB + cols]
                    dve.tensor_tensor(h, h, g, ALU.mult).then_inc(s_t, 1)
                    for q, st in stages_at(j, tiles):
                        update(BT * b + BT + q, q, st, b)
                    if agg:
                        for q, i in GROUP_AT[j]:
                            if i == GROUPS - 1:
                                neighbours(BT * b + AHEAD + q, (AHEAD + q) % 2)
                low(b, HT - 1, cols)
                if nxt:
                    take_input(b + 1, BT * b + BT + len(tiles))
                dve.wait_ge(s_x1, b + 1)
                dve.wait_ge(s_f2, HT * b + HT + 1)
                for k in range(KC):
                    o = x1a[:, k * NB:k * NB + cols]
                    dve.scalar_tensor_tensor(out=o, in0=Y[k][:, 0:cols], scalar=cst[:, 5:6], in1=o,
                                             op0=ALU.mult, op1=ALU.add).then_inc(s_y, 1)

            with dve.Fori(0, BLOCKS - 1) as b:
                ffn_block(b, True, range(BT), NB, True)
            ffn_block(BLOCKS - 1, False, range(1), NB, True)
            ffn_block(BLOCKS, False, (), P, False)


def gate_count(b, i):
    def dmas(k):
        return 1 if k < EXP else len(segments(HT_FULL + k - EXP))

    slot = [k for k in range(GLOADS) if k % GSLOTS == i % GSLOTS]
    return b * (16 * sum(map(dmas, slot))) + 16 * sum(dmas(k) for k in slot if k <= i)


def kernel(x, src, dst, L0_gnn_W, L0_gnn_b, L0_mix_W_qkv, L0_mix_b_qkv, L0_mix_W_out, L0_mix_b_out,
           L0_ffn_router_w, L0_ffn_w1, L0_ffn_w2, L0_ffn_w3):
    import numpy as np
    import concourse.bacc as bacc
    from concourse.bass_utils import run_bass_kernel_spmd

    def pad(a, n, value=0):
        out = np.full((n,) + a.shape[1:], value, a.dtype)
        out[:a.shape[0]] = a
        return out

    def hidden_rows(w):
        a = np.concatenate([w[:, :FULL * P].reshape(-1, C), w[:, FULL * P:].reshape(-1, C)])
        return pad(a, HPAD)

    x, src, dst = np.asarray(x), np.asarray(src), np.asarray(dst)
    w1, w2, w3 = np.asarray(L0_ffn_w1), np.asarray(L0_ffn_w2), np.asarray(L0_ffn_w3)
    wqkv, bqkv = np.asarray(L0_mix_W_qkv), np.asarray(L0_mix_b_qkv)
    nowhere = 1 << 20
    w13T = [hidden_rows(w).T.reshape(KC, P, HPAD).transpose(1, 0, 2).reshape(P, KC * HPAD) for w in (w1, w3)]
    arrays = {
        "x": pad(x, NPAD),
        "srcT": pad(src, ETW * P).reshape(ETW, P).T,
        "dstT": pad(dst, ETW * P, nowhere).reshape(ETW, P).T,
        "dst_rows": pad(dst, EJ * P * P, nowhere).reshape(EJ * P, P),
        "Wg": np.asarray(L0_gnn_W), "bg": np.asarray(L0_gnn_b)[None, :],
        "Wq": wqkv[:, 0:C], "Wk": wqkv[:, C:2 * C], "WvT": wqkv[:, 2 * C:].T,
        "bq": bqkv[None, 0:C], "bk": bqkv[None, C:2 * C], "bv": bqkv[2 * C:, None],
        "Wo": np.asarray(L0_mix_W_out), "bo": np.asarray(L0_mix_b_out)[None, :],
        "rwT": np.asarray(L0_ffn_router_w).T,
        "w1n": pad(w1.reshape(-1, C), NW13 * P), "w3n": pad(w3.reshape(-1, C), NW13 * P),
        "w2n": w2.reshape(-1, HID),
        "w13T": np.stack(w13T),
        "w2T": hidden_rows(w2.transpose(0, 2, 1)).reshape(HT, P, C).transpose(1, 0, 2).reshape(P, HT * C),
    }
    arrays = {f"in_{k}": np.ascontiguousarray(v) for k, v in arrays.items()}
    nc = bacc.Bacc("TRN2", target_bir_lowering=False, num_devices=1, dynamic_dma_scratch_size=14336)
    args = [nc.dram_tensor(k, v.shape, mybir.dt.from_np(v.dtype), kind="ExternalInput").ap() for k, v in arrays.items()]
    out = nc.dram_tensor("out_t", (C, NODES), F32, kind="ExternalOutput").ap()
    gnn_mix_moe(nc, *args, out)
    r = run_bass_kernel_spmd(nc, [arrays], core_ids=[0])
    return np.ascontiguousarray(r.results[0]["out_t"].T)
```

```python
import concourse.bass as bass
from concourse import mybir
from contextlib import ExitStack

P = 128
F32 = mybir.dt.float32
F16 = mybir.dt.float16
I32 = mybir.dt.int32
U32 = mybir.dt.uint32
ALU = mybir.AluOpType
ACT = mybir.ActivationFunctionType
AX = mybir.AxisListType
RMAX = bass.bass_isa.ReduceOp.max

NODES = 6250
C = 256
KC = C // P
TILES = -(-NODES // P)
NPAD = TILES * P
LAST = NODES - (TILES - 1) * P
EDGES = 200000
ET = -(-EDGES // P)
W = 36
WG = 4
GROUPS = W // WG
RG = 3
ETW = ET + W + 1
EJ = -(-ET // P)
EXP = 8
HID = 682
FULL = HID // P
HT_FULL = EXP * FULL
REST = HID - FULL * P
HT = HT_FULL + -(-EXP * REST // P)
HPAD = HT * P
BT = 4
NB = BT * P
BLOCKS = TILES // BT
GLOADS = EXP + HT - HT_FULL
GSLOTS = 3
XS = 1024.0
TROW = 64
NODE_GROUPS = -(-TILES // BT)
UNITS = KC * HT
WU = 11
SPLITS = -(-UNITS // WU)
LOADS = 8
LCOL = UNITS * P // LOADS
EPS_LN, EPS_DIV, EPS_NORM = 1e-5, 1e-7, 1e-12
TINY = 1e-30
RSQRT_MAGIC = float(0x5F3759DF)

AHEAD = BT + 1

GROUP_AT = [[] for _ in range(HT)]
for _g in range(BT * GROUPS):
    GROUP_AT[int((_g + 0.5) * (HT - BT) / (BT * GROUPS))].append((_g // GROUPS, _g % GROUPS))
POST = 10
STAGES = dict(enumerate("ABCDEFGHI", 1))


def stages_at(step, tiles):
    q, k = divmod(step, POST)
    return [(q, STAGES[k])] if q in tiles and k in STAGES else []


def splits_at(p, k):
    slots = (0, 1, 3, 6, 9)
    c = len(slots) * (p + 1) + slots.index(k) if k in slots else 3 * SPLITS
    return [c] if c < 3 * SPLITS else []


def some(n):
    return not (isinstance(n, int) and n == 0)


def segments(tile):
    first = (tile - HT_FULL) * P
    out, r = [], first
    while r < min(first + P, EXP * REST):
        e = r // REST
        end = min((e + 1) * REST, first + P, EXP * REST)
        out.append((r - first, end - first, e))
        r = end
    return out


def gnn_mix_moe(nc, x, srcT, dstT, dst_rows, Wg, bg, Wq, Wk, WvT, bq, bk, bv, Wo, bo, rwT, wT, outT):
    with ExitStack() as ctx:
        def sb(name, shape, dt=F32):
            return ctx.enter_context(nc.sbuf_tensor(name, shape, dt))

        def sem(name):
            return ctx.enter_context(nc.semaphore(name))

        def sems(name, n):
            return [sem(f"{name}_{i}") for i in range(n)]

        def dram(name, shape, dt=F32):
            return nc.dram_tensor(name, shape, dt).ap()

        XH = dram("xn_split", (NPAD, 2 * C), F16)
        XT = dram("xn_cols", (NPAD, C))
        GT = dram("gates_t", (EXP, NPAD))

        wts = sb("wts", [P, 3, UNITS, 2, P], F16)
        x2s = sb("x2s", [P, 2 * KC, NB], F16)
        x2a = sb("x2a", [P, 2 * KC, NB], F16)
        x1s = sb("x1s", [P, KC * NB])
        x1a = sb("x1a", [P, KC * NB])
        gate = sb("gate", [P, GSLOTS * NB])
        sig = sb("sig", [P, 2 * NB])
        hid = sb("hid", [P, 2 * NB])
        hh = sb("hh", [P, 3 * 2, NB], F16)
        rows = sb("rows", [P, RG * WG, 2 * C + 2], F16)
        hot = sb("hot", [P, RG, WG, P], F16)
        wq_s = sb("wq_s", [P, KC, C])
        wg_s = sb("wg_s", [P, 2 * KC, C])
        mix = sb("mix", [P, KC, C])
        wvo = sb("wvo", [P, KC, C])
        bq_b = sb("bq_b", [P, C])
        bg_b = sb("bg_b", [P, C])
        co_b = sb("co_b", [P, C])
        rw_s = sb("rw_s", [P, KC, EXP])
        ident = sb("ident", [P, P])
        lane = sb("lane", [P, P], F16)
        xt = sb("xt", [P, 2, C])
        xnt = sb("xnt", [P, 2, C])
        neigh = sb("neigh", [P, 2, C])
        tmp = sb("tmp", [P, 5, C])
        srcw = sb("srcw", [P, 2, W], I32)
        dstw = sb("dstw", [P, 2, W], I32)
        dstf = sb("dstf", [P, 2, W])
        base = sb("base", [P, TILES])
        tab = sb("tab", [P, 3, TROW], I32)
        xsrc = sb("xsrc", [P, 1], I32)
        xdst = sb("xdst", [P, 1], I32)
        xdf = sb("xdf", [P, 1])
        xrow = sb("xrow", [P, 2 * C + 2], F16)
        xhot = sb("xhot", [P, P], F16)
        sc = sb("sc", [P, 96])
        cst = sb("cst", [P, 8])
        lane8 = sb("lane8", [P, EXP])
        idx8 = sb("idx8", [P, EXP], U32)
        gts = sb("gts", [EXP, P])
        one = sb("one", [P, 1])
        wmx = sb("wmx", [P, 3 * LOADS])

        def tiles4(a):
            return a.rearrange("p (t c) -> p t c", c=C)

        rflat = rows[:, :, :].rearrange("p a n -> p (a n)").bitcast(F32)
        hflat = hh[:, :, :].rearrange("p a n -> p (a n)").bitcast(F32)
        gflat = gate[:, :]
        xin = [tiles4(a[:, :]) for a in (x1s, x1a, sig, hid)]
        xtb = [tiles4(rflat[:, 1024 * h:1024 * (h + 1)]) for h in range(2)]
        xhb = [x2s[:, :, :], x2a[:, :, :]]
        key2 = [a[:, i, :] for a in (xt, xnt, neigh, wvo) for i in range(2)]
        key4 = [tmp[:, i, :] for i in range(BT)]
        wk_s, bk_b = mix, co_b
        stage = [gflat, hflat]
        wvt_s = gflat[:, 0:512].rearrange("p (k c) -> p k c", c=C)
        wo_s = gflat[:, 512:1024].rearrange("p (k c) -> p k c", c=C)
        bv_s = gflat[:, 1024:1024 + KC]
        bvr = gflat[:, 1040:1040 + KC * P].rearrange("p (k c) -> p k c", c=P)
        kxs = tmp[:, 0:2, :]
        sbv, bo_b = tmp[:, 2, :], tmp[:, 3, :]
        wflat = wts[:, :, :, :, :].rearrange("p n u h c -> p (n u h c)").bitcast(F32)
        rng = wflat[:, 2 * UNITS * P:]
        drow = rng[:, 0:EJ * P].bitcast(I32).rearrange("p (j e) -> p j e", e=P)
        rng = rng[:, EJ * P:]
        kidx, dmin, dmax = rng[:, 0:EJ], rng[:, 20:20 + EJ], rng[:, 40:40 + EJ]
        ra = rng[:, 100:100 + TILES * EJ].rearrange("p (t j) -> p t j", j=EJ)
        rb = rng[:, 800:800 + TILES * EJ].rearrange("p (t j) -> p t j", j=EJ)
        rloc, rall = rng[:, 2800:2800 + 2 * TILES], rng[:, 3000:3000 + 2 * TILES]
        run = [rng[:, 3200 + 64 * i:3200 + 64 * i + TILES] for i in range(2)]

        bank = [ctx.enter_context(nc.psum_tensor(f"bank{i}", [P, 512], F32)) for i in range(8)]
        Y, H1, H3, AG, PB = bank[0:2], bank[2:4], bank[4:6], bank[6], bank[7]

        s_wld = sem("s_wld")
        s_bo = sem("s_bo")
        s_rng = sem("s_rng")
        s_x = sems("s_x", BT)
        s_xst = sems("s_xst", 2)
        s_w = sems("s_w", 4)
        s_wk = sem("s_wk")
        s_win = sems("s_win", 2)
        s_row = sems("s_row", RG)
        s_tile = sems("s_tile", 2)
        s_gst = sem("s_gst")
        s_gld = sems("s_gld", GSLOTS)
        s_out = sem("s_out")
        s_xi = sem("s_xi")
        s_xr = sem("s_xr")
        s_const, s_ident, s_rloc, s_rall, s_tab = map(sem, ("s_const", "s_ident", "s_rloc", "s_rall", "s_tab"))
        s_nloc, s_nall, s_wm, s_cst = map(sem, ("s_nloc", "s_nall", "s_wm", "s_cst"))
        s_zero = sem("s_zero")
        s_lnr = sem("s_lnr")
        s_lnx = sem("s_lnx")
        s_lnh = sem("s_lnh")
        s_lnl = sem("s_lnl")
        s_lnt = sem("s_lnt")
        s_lnc = sem("s_lnc")
        s_ck = sem("s_ck")
        s_cent = sem("s_cent")
        s_kp = sem("s_kp")
        s_k2 = sem("s_k2")
        s_k2n = sem("s_k2n")
        s_k4 = sem("s_k4")
        s_kx = sem("s_kx")
        s_wvo, s_wvc, s_kxs, s_mp, s_mix = map(sem, ("s_wvo", "s_wvc", "s_kxs", "s_mp", "s_mix"))
        s_stg = sem("s_stg")
        s_whi = sem("s_whi")
        s_wlo = sem("s_wlo")
        s_dst = sem("s_dst")
        s_hot = sem("s_hot")
        s_used = sem("s_used")
        s_agg = sem("s_agg")
        s_nei = sem("s_nei")
        s_pool = sem("s_pool")
        s_sp = sem("s_sp")
        s_xs = sem("s_xs")
        s_xh = sem("s_xh")
        s_xd = sem("s_xd")
        (s_pA, s_dA, s_aA, s_dB, s_pB, s_dC, s_aC, s_dD, s_pC, s_dE, s_pD, s_dF, s_aF, s_dG, s_pE, s_dH, s_aH, s_dI,
         s_pF, s_dJ) = (sem(f"s_{n}") for n in "pA dA aA dB pB dC aC dD pC dE pD dF aF dG pE dH aH dI pF dJ".split())
        s_h1 = sem("s_h1")
        s_h3 = sem("s_h3")
        s_sig = sem("s_sig")
        s_u = sem("s_u")
        s_t = sem("s_t")
        s_hi = sem("s_hi")
        s_lo = sem("s_lo")
        s_f2 = sem("s_f2")
        s_x2 = sem("s_x2")
        s_x1 = sem("s_x1")
        s_y = sem("s_y")

        block = ctx.enter_context(nc.Block())
        ds = bass.ds

        def rows_of(t, first, n):
            return t[ds(first * P, n * P), :].rearrange("(t p) c -> p t c", p=P)

        def load_piece(c):
            return wflat[:, c * LCOL:(c + 1) * LCOL]

        def split_chunk(c):
            n, k = divmod(c, SPLITS)
            u0, u1 = WU * k, min(WU * (k + 1), UNITS)
            whole = wflat[:, (n * UNITS + u0) * P:(n * UNITS + u1) * P]
            aside = stage[c % 2][:, 0:(u1 - u0) * P]
            return whole, wts[:, n, u0:u1, 0, :], wts[:, n, u0:u1, 1, :], aside

        def unit(n, u):
            return wts[:, n, u, 0, :], wts[:, n, u, 1, :]

        def pairs(n):
            return [(i, range(2 * i, min(2 * i + 2, n))) for i in range((n + 1) // 2)]

        FIRST, TURNS = 3, 2

        def first_pass(engine, step):
            def sizes(s):
                return {i: 0 if not 0 <= s + i < NODE_GROUPS else min(BT, TILES - BT * (s + i)) for i in range(-2, 3)}

            for s in range(FIRST):
                step(s, s % BT, sizes(s))
            with engine.Fori(0, TURNS) as turn:
                for k in range(BT):
                    step(BT * turn + (FIRST + k), (FIRST + k) % BT, sizes(FIRST + k))
            for s in range(FIRST + BT * TURNS, NODE_GROUPS + 2):
                step(s, s % BT, sizes(s))

        @block.sync
        def _(sp):
            def load_group(g, k):
                if not (isinstance(g, int) and g < BT):
                    sp.wait_ge(s_kx, BT * (g - BT) + BT)
                    sp.sem_inc(s_sp, 1)
                    sp.wait_ge(s_lnl, g - BT + 1)
                sp.dma_start(xin[k], rows_of(x, BT * g, BT)).then_inc(s_x[k], 16)

            load_group(0, 0)
            for dst_, src_ in ((wk_s[:, :, :], Wk.rearrange("(k p) c -> p k c", p=P)), (bk_b[:, :], bk.broadcast_to((P, C)))):
                sp.dma_start(dst_, src_).then_inc(s_wk, 16)
            load_group(1, 1)
            sp.dma_start(drow, dst_rows.rearrange("(p j) e -> p j e", j=EJ)).then_inc(s_rng, 16)
            for k in range(2, BT):
                load_group(k, k)
            for dst_, src_ in ((wq_s[:, :, :], Wq), (wvt_s, WvT), (wo_s, Wo), (rw_s[:, :, :], rwT), (wg_s[:, :, :], Wg)):
                sp.dma_start(dst_, src_.rearrange("(k p) c -> p k c", p=P)).then_inc(s_wld, 16)
            for dst_, src_ in ((bq_b, bq), (bg_b, bg)):
                sp.dma_start(dst_[:, :], src_.broadcast_to((P, C))).then_inc(s_wld, 16)
            for k in range(KC):
                sp.dma_start(bv_s[:, k:k + 1], bv[k * P:(k + 1) * P, :]).then_inc(s_wld, 16)

            def step(s, k, sizes):
                if n := sizes[0]:
                    sp.wait_ge(s_lnl, s + 1)
                    sp.dma_start(rows_of(XH, BT * s, n), xhb[k % 2][:, 0:n, :]).then_inc(s_xst[k % 2], 16)
                    sp.wait_ge(s_lnc, s + 1)
                    sp.dma_start(rows_of(XT, BT * s, n), xtb[k % 2][:, 0:n, :]).then_inc(s_xst[k % 2], 16)
                if sizes[2] and not (isinstance(s, int) and s < 2):
                    load_group(s + 2, (k + 2) % BT)

            first_pass(sp, step)

            def load_window(t, par, n):
                if some(n):
                    sp.wait_ge(s_agg, n)
                first = sp.value_load(tab[0:1, 0, ds(t, 1)], min_val=0, max_val=ET - 1)
                sp.dma_start(srcw[:, par, :], srcT[:, ds(first, W)]).then_inc(s_win[par], 16)
                sp.dma_start(dstw[:, par, :], dstT[:, ds(first, W)]).then_inc(s_win[par], 16)

            def load_tile(t, par, n):
                if some(n):
                    sp.wait_ge(s_pD, n)
                sp.dma_start(xt[:, par, :], x[ds(t * P, P), :]).then_inc(s_tile[par], 16)
                sp.dma_start(xnt[:, par, :], XT[ds(t * P, P), :]).then_inc(s_tile[par], 16)

            sp.wait_ge(s_tab, 1)
            load_window(0, 0, 0)
            load_window(1, 1, 0)
            sp.wait_ge(s_kx, TILES)
            sp.dma_start(bo_b, bo.broadcast_to((P, C))).then_inc(s_bo, 16)
            sp.wait_ge(s_xst[0], 32 * 7)
            sp.wait_ge(s_xst[1], 32 * 6)
            load_tile(0, 0, 0)
            load_tile(1, 1, 0)

            def store_gates(t, n):
                sp.wait_ge(s_dJ, n)
                sp.sem_inc(s_sp, 1)
                sp.dma_start(GT[:, ds(t * P, P)], gts[:, :]).then_inc(s_gst, 16)

            def load_gate(b, i, cols):
                slot = i % GSLOTS
                to = gate[:, slot * NB:slot * NB + cols]
                if i < EXP:
                    sp.dma_start(to, GT[i:i + 1, ds(b * NB, cols)].broadcast_to((P, cols))).then_inc(s_gld[slot], 16)
                    return
                for r0, r1, e in segments(HT_FULL + i - EXP):
                    sp.dma_start(to[r0:r1, :], GT[e:e + 1, ds(b * NB, cols)].broadcast_to((r1 - r0, cols)))\
                        .then_inc(s_gld[slot], 16)

            load_window(2, 0, 1)
            for p in range(BT):
                if p < BT - 1:
                    load_tile(p + 2, p % 2, p + 1)
                store_gates(p, p + 1)
                if p < BT - 1:
                    load_window(p + 3, (p + 3) % 2, p + 2)
            sp.wait_ge(s_gst, 16 * BT)
            sp.wait_ge(s_wlo, 3 * SPLITS)
            for i in range(GSLOTS):
                load_gate(0, i, NB)

            def ffn_block(b, agg, tiles, cols, nxt):
                t0 = BT * b + BT
                for j in range(HT):
                    if agg and j % POST == 1 and j // POST in tiles:
                        q = j // POST
                        load_window(t0 + q + 2, q % 2, t0 + q + 1)
                        load_tile(t0 + q + 1, (q + 1) % 2, t0 + q)
                    if j and j % FULL == 0:
                        sp.wait_ge(s_t, HT * b + j)
                        sp.sem_inc(s_sp, 1)
                        load_gate(b, j // FULL - 1 + GSLOTS, cols)
                    if j % POST == 9 and j // POST in tiles:
                        store_gates(t0 + j // POST, t0 + j // POST + 1)
                if nxt:
                    sp.wait_ge(s_gst, 16 * (t0 + len(tiles)))
                    sp.sem_inc(s_sp, 1)
                    sp.wait_ge(s_t, HT * b + HT)
                    sp.sem_inc(s_sp, 1)
                    for i in range(GSLOTS):
                        load_gate(b + 1, i, nxt)
                for k in range(KC):
                    n = min(cols, NODES - NB * b) if isinstance(b, int) else cols
                    sp.wait_ge(s_y, KC * b + k + 2)
                    sp.dma_start(outT[k * P:(k + 1) * P, ds(b * NB, n)], x1a[:, k * NB:k * NB + n]).then_inc(s_out, 16)

            with sp.Fori(0, BLOCKS - 1) as b:
                ffn_block(b, True, range(BT), NB, NB)
            ffn_block(BLOCKS - 1, False, range(1), NB, P)
            ffn_block(BLOCKS, False, (), P, 0)
            sp.wait_ge(s_out, 16 * KC * (BLOCKS + 1) + 1)

        @block.gpsimd
        def _(pool):
            pool.iota(lane[:, :], [[1, P]], base=0, channel_multiplier=0, allow_small_or_imprecise_dtypes=True)\
                .then_inc(s_const, 1)
            pool.iota(lane8[:, :], [[1, EXP]], base=0, channel_multiplier=0, allow_small_or_imprecise_dtypes=True)\
                .then_inc(s_const, 1)
            pool.iota(base[:, :], [[P, TILES]], base=0, channel_multiplier=0, allow_small_or_imprecise_dtypes=True)\
                .then_inc(s_const, 1)
            pool.iota(kidx, [[1, EJ]], base=0, channel_multiplier=EJ, allow_small_or_imprecise_dtypes=True)\
                .then_inc(s_const, 1)
            pool.memset(one[:, :], 1.0).then_inc(s_const, 1)
            pool.memset(gts[:, :], 1.0).then_inc(s_const, 1)
            pool.memset(xrow[:, 2 * C:2 * C + 2], 1.0).then_inc(s_const, 1)
            pool.memset(ident[:, :], 0.0).then_inc(s_ident, 1)
            pool.wait_ge(s_ident, 1)
            pool.affine_select(out=ident[:, :], in_=ident[:, :], compare_op=ALU.not_equal, fill=1.0,
                               base=0, pattern=[[-1, P]], channel_multiplier=1).then_inc(s_ident, 1)
            def load_weights(c):
                if c >= 4:
                    pool.wait_ge(s_wm, c - 3)
                if c == 2 * LOADS:
                    pool.wait_ge(s_tab, 1)
                n, k = divmod(c, LOADS)
                pool.dma_start(load_piece(c), wT[n, :, k * LCOL:(k + 1) * LCOL]).then_inc(s_w[c % 4], 16)

            for c in range(4):
                load_weights(c)
            pool.wait_ge(s_rloc, 1)
            pool.partition_all_reduce(rall, rloc, P, RMAX).then_inc(s_rall, 1)

            def gather_group(t, i, par):
                pool.wait_ge(s_used, GROUPS * t + i + 1)
                pool.sem_inc(s_pool, 1)
                g = i % RG
                for m in range(WG):
                    e = WG * i + m
                    pool.indirect_dma_start(rows[:, g * WG + m, 0:2 * C], None, XH,
                                            bass.IndirectOffsetOnAxis(ap=srcw[:, par, e:e + 1], axis=0))\
                        .then_inc(s_row[g], 16)

            def gather_extra(t):
                first = pool.value_load(tab[0:1, 0, ds(t, 1)], min_val=0, max_val=ET - 1)
                n = pool.value_load(tab[0:1, 1, ds(t, 1)], min_val=0, max_val=ET)
                done = pool.value_load(tab[0:1, 2, ds(t, 1)], min_val=0, max_val=ET * TILES)
                with pool.If(n > 0):
                    with pool.Fori(0, n) as i:
                        pool.wait_ge(s_xd, done + i + 1)
                        col = nc.s_assert_within(first + i + W, 0, ETW - 1,
                                                 skip_runtime_bounds_check_because="the table's counts end at the last edge tile")
                        pool.dma_start(xsrc[:, :], srcT[:, ds(col, 1)], allow_slow_non_contiguous=True).then_inc(s_xi, 16)
                        pool.dma_start(xdst[:, :], dstT[:, ds(col, 1)], allow_slow_non_contiguous=True).then_inc(s_xi, 16)
                        pool.wait_ge(s_xi, (done + i) * 32 + 32)
                        pool.sem_inc(s_xs, 1)
                        pool.indirect_dma_start(xrow[:, 0:2 * C], None, XH,
                                                bass.IndirectOffsetOnAxis(ap=xsrc[:, 0:1], axis=0)).then_inc(s_xr, 16)

            def gather_tile(t, par, use):
                pool.wait_ge(s_win[par], 32 * use)
                gather_group(t, 0, par)
                gather_extra(t)
                for i in range(1, GROUPS):
                    gather_group(t, i, par)

            for c in range(4, 3 * LOADS):
                load_weights(c)
            pool.wait_ge(s_nloc, 1)
            pool.partition_all_reduce(sc[:, 4:7], sc[:, 0:3], P, RMAX).then_inc(s_nall, 1)
            pool.wait_ge(s_xst[0], 32 * 7)
            pool.wait_ge(s_xst[1], 32 * 6)
            pool.wait_ge(s_kx, TILES)
            pool.memset(rows[:, :, 2 * C:2 * C + 2], 1.0).then_inc(s_const, 1)
            pool.wait_ge(s_const, 8)
            for t in range(AHEAD):
                gather_tile(t, t % 2, t // 2 + 1)
            with pool.Fori(0, BLOCKS - 1) as b:
                for q in range(BT):
                    gather_tile(BT * b + AHEAD + q, (AHEAD + q) % 2, 2 * b + (AHEAD + q) // 2 + 1)

        @block.scalar
        def _(act):
            def step(s, k, sizes):
                if n := sizes[0]:
                    h = k % 2
                    act.wait_ge(s_lnr, s + 1)
                    for i in range(n):
                        last = act.activation(xin[k][:, i, :], xin[k][:, i, :], ACT.Identity,
                                              scale=sc[:, 16 + 8 * h + i:17 + 8 * h + i],
                                              bias=sc[:, 20 + 8 * h + i:21 + 8 * h + i])
                    last.then_inc(s_lnx, 1)
                    if not (isinstance(s, int) and s < 2):
                        act.wait_ge(s_xst[h], 32 * (s // 2) if isinstance(s, int) else 16 * (s - k % 2))
                    act.wait_ge(s_lnx, s + 1)
                    act.activation(xhb[h][:, 0:n, 0:C], xin[k][:, 0:n, :], ACT.Copy, scale=XS).then_inc(s_lnh, 1)
                if n := sizes[-2]:
                    for i, tiles in pairs(n):
                        act.wait_ge(s_k2n, 2 * (s - 2) + i + 1)
                        if not (isinstance(s, int) and s < 3):
                            act.wait_ge(s_kx, BT * (s - 3) + 2 * i + 2)
                        for m in tiles:
                            last = act.activation(key4[m], key2[BT * (k % 2) + m], ACT.Square)
                        last.then_inc(s_k4, 1)
                if n := sizes[0]:
                    act.wait_ge(s_lnt, s + 1)
                    if not (isinstance(s, int) and s < 2):
                        act.wait_ge(s_kp, 2 * (s - 2) + 2)
                    for i, tiles in pairs(n):
                        m = len(tiles)
                        last = act.activation(xtb[h][:, 2 * i:2 * i + m, :].rearrange("p t c -> p (t c)"),
                                              bank[2 + 2 * h + i][:, 0:m * C], ACT.Copy)
                    last.then_inc(s_lnc, 1)
                if n := sizes[-1]:
                    o = BT * ((k - 1) % 2)
                    for i, tiles in pairs(n):
                        act.wait_ge(s_kp, 2 * (s - 1) + i + 1)
                        if not (isinstance(s, int) and s < 3):
                            act.wait_ge(s_kx, BT * (s - 3) + 2 * i + 2)
                        for m in tiles:
                            last = act.activation(key2[o + m], bank[6 + i][:, (m % 2) * C:(m % 2) * C + C], ACT.Square,
                                                  accum_out=sc[:, 80 + o + m:81 + o + m])
                        last.then_inc(s_k2, 1)

            first_pass(act, step)
            act.wait_ge(s_wvo, 1)
            act.activation(wvo[:, :, :].rearrange("p k c -> p (k c)"), bank[2][:, :], ACT.Copy).then_inc(s_wvc, 1)

            def split_high(c):
                whole, high, _, aside = split_chunk(c)
                if c < 2:
                    act.wait_ge(s_mix, 1)
                else:
                    act.wait_ge(s_wlo, c - 1)
                n = c // SPLITS
                act.activation(aside, whole, ACT.Copy, scale=cst[:, n:n + 1]).then_inc(s_stg, 1)
                act.wait_ge(s_stg, c + 1)
                act.activation(high, aside.rearrange("p (u c) -> p u c", c=P), ACT.Copy).then_inc(s_whi, 1)

            def update(t, q, stage_):
                if stage_ == "A":
                    act.wait_ge(s_dA, t + 1)
                    act.activation(tmp[:, 1, :], tmp[:, 1, :], ACT.Square, accum_out=sc[:, 0:1])
                    act.drain()
                    act.activation(tmp[:, 2, :], tmp[:, 1, :], ACT.Square, accum_out=sc[:, 1:2]).then_inc(s_aA, 1)
                if stage_ == "C":
                    act.wait_ge(s_dC, t + 1)
                    act.activation(tmp[:, 1, :], tmp[:, 1, :], ACT.Relu)
                    act.drain()
                    act.activation(tmp[:, 2, :], tmp[:, 1, :], ACT.Square, accum_out=sc[:, 2:3]).then_inc(s_aC, 1)
                if stage_ == "F":
                    act.wait_ge(s_dF, t + 1)
                    act.activation(x2s[:, 0:KC, q * P:(q + 1) * P],
                                   tmp[:, 0, :].rearrange("p (k n) -> p k n", k=KC), ACT.Copy).then_inc(s_aF, 1)
                if stage_ == "G":
                    act.wait_ge(s_dH, t + 1)
                    act.activation(sc[:, 72:80], sc[:, 64:72], ACT.Tanh, scale=1.0 / 16.0).then_inc(s_aH, 1)

            act.wait_ge(s_cst, 1)
            for p in range(-1, BT):
                for k in range(POST):
                    for c in splits_at(p, k):
                        split_high(c)
                    if p >= 0 and k in STAGES:
                        update(p, p, STAGES[k])

            def ffn_block(b, tiles, cols):
                for j in range(HT):
                    act.wait_ge(s_u, HT * b + max(j - 1, 0) + 1)
                    act.wait_ge(s_h1, HT * b + j + 1)
                    act.activation(sig[:, (j % 2) * NB:(j % 2) * NB + cols], H1[j % 2][:, 0:cols], ACT.Silu,
                                   scale=cst[:, 3:4]).then_inc(s_sig, 1)
                    act.wait_ge(s_f2, HT * b + max(j - 2, 0) + 1)
                    act.wait_ge(s_t, HT * b + j + 1)
                    act.activation(hh[:, 2 * (j % 3), 0:cols], hid[:, (j % 2) * NB:(j % 2) * NB + cols], ACT.Copy)\
                        .then_inc(s_hi, 1)
                    if j == 3:
                        act.wait_ge(s_out, 16 * KC * b + 1)
                        act.activation(x1a[:, :], x1s[:, :], ACT.Copy).then_inc(s_x1, 1)
                    for q, s in stages_at(j, tiles):
                        update(BT * b + BT + q, q, s)

            with act.Fori(0, BLOCKS - 1) as b:
                ffn_block(b, range(BT), NB)
            ffn_block(BLOCKS - 1, range(1), NB)
            ffn_block(BLOCKS, (), P)

        @block.tensor
        def _(pe):
            pe.sem_inc(s_used, RG)
            for free in (s_xd, s_nei, s_y, s_u, s_f2, s_out):
                pe.sem_inc(free, 1)

            def open_sum(bank_):
                pe.matmul(bank_[:, :], hot[:, 0, 0, :], hot[:, 0, :, :].rearrange("p a n -> p (a n)"),
                          start=True, stop=False, skip_group_check=True)

            def sum_group(t, i, turn=None):
                g = i % RG
                if i == 0:
                    pe.wait_ge(s_nei, t + 1)
                pe.wait_ge(s_row[g], (3 * t + i // RG) * 64 + 64)
                pe.wait_ge(s_hot, GROUPS * t + i + 1)
                for m in range(WG):
                    r = rows[:, g * WG + m, :]
                    pe.matmul(AG[:, 0:C], hot[:, g, m, :], r[:, 0:C], start=(i == 0 and m == 0), stop=False,
                              skip_group_check=True)
                    last = pe.matmul(AG[:, 0:C + 1], hot[:, g, m, :], r[:, C:2 * C + 1], start=False,
                                     stop=(i == GROUPS - 1 and m == WG - 1), skip_group_check=True)
                last.then_inc(s_used, 1)
                if i == 0:
                    n = pe.value_load(tab[0:1, 1, ds(t, 1)], min_val=0, max_val=ET)
                    done = pe.value_load(tab[0:1, 2, ds(t, 1)], min_val=0, max_val=ET * TILES)
                    with pe.If(n > 0):
                        with pe.Fori(0, n) as k:
                            pe.wait_ge(s_xr, (done + k) * 16 + 16)
                            pe.wait_ge(s_xh, done + k + 1)
                            pe.matmul(AG[:, 0:C], xhot[:, :], xrow[:, 0:C], start=False, stop=False,
                                      skip_group_check=True)
                            pe.matmul(AG[:, 0:C + 1], xhot[:, :], xrow[:, C:2 * C + 1], start=False, stop=False,
                                      skip_group_check=True).then_inc(s_xd, 1)
                if i == GROUPS - 1:
                    pe.drain().then_inc(s_agg, 1)

            def step(s, k, sizes):
                if n := sizes[0]:
                    h = k % 2
                    if not (isinstance(s, int) and s < 2):
                        pe.wait_ge(s_lnc, s - 1)
                    pe.wait_ge(s_lnx, s + 1)
                    for i in range(n):
                        for c in range(KC):
                            o = (i % 2) * C + c * P
                            last = pe.transpose(bank[2 + 2 * h + i // 2][:, o:o + P],
                                                xin[k][:, i, c * P:(c + 1) * P], ident[:, :])
                    last.then_inc(s_lnt, 1)
                if n := sizes[-1]:
                    pe.wait_ge(s_lnc, s)
                    for i, tiles in pairs(n):
                        if not (isinstance(s, int) and s < 2):
                            pe.wait_ge(s_k2, 2 * (s - 2) + i + 1)
                        for m in tiles:
                            o = bank[6 + i][:, (m % 2) * C:(m % 2) * C + C]
                            for c in range(KC):
                                pe.matmul(o, xtb[(k - 1) % 2][:, m, c * P:(c + 1) * P], wk_s[:, c, :],
                                          start=(c == 0), stop=False)
                            last = pe.matmul(o, gts[0:1, :], bk_b[0:1, :], start=False, stop=True)
                        last.then_inc(s_kp, 1)
                if n := sizes[-2]:
                    for i, tiles in pairs(n):
                        pe.wait_ge(s_k4, 2 * (s - 2) + i + 1)
                        for m in tiles:
                            rows_ = P if n == BT else LAST
                            k2, k4 = key2[BT * (k % 2) + m], key4[m]
                            for c in range(KC):
                                pe.matmul(Y[0][:, c * C:(c + 1) * C], xin[(k - 2) % BT][0:rows_, m, c * P:(c + 1) * P],
                                          k2[0:rows_, :], start=False, stop=False, skip_group_check=True)
                            for a, kk in enumerate((k2, k4)):
                                for c in range(KC):
                                    last = pe.matmul(Y[1][:, 2 * a + c:2 * a + c + 1], kk[0:rows_, c * P:(c + 1) * P],
                                                     one[0:rows_, :], start=False, stop=False, skip_group_check=True)
                            last.then_inc(s_kx, 1)

            pe.wait_ge(s_ident, 2)
            pe.wait_ge(s_const, 7)
            pe.wait_ge(s_zero, 1)
            open_sum(Y[0])
            open_sum(Y[1])
            pe.drain().then_inc(s_zero, 1)
            pe.wait_ge(s_ck, 1)
            first_pass(pe, step)
            pe.wait_ge(s_cent, 1)
            pe.wait_ge(s_lnc, NODE_GROUPS)
            pe.wait_ge(s_k2, 2 * NODE_GROUPS - 1)
            for k in range(KC):
                for d in range(KC):
                    pe.matmul(bank[2][:, k * C:(k + 1) * C], wvt_s[:, d, k * P:(k + 1) * P], wo_s[:, d, :],
                              start=(d == 0), stop=(d == KC - 1))
            for d in range(KC):
                last = pe.matmul(bank[3][:, 0:C], bvr[:, d, :], wo_s[:, d, :], start=(d == 0), stop=(d == KC - 1))
            last.then_inc(s_wvo, 1)
            pe.wait_ge(s_wvc, 1)
            pe.wait_ge(s_kxs, 1)
            for k in range(KC):
                for d in range(KC):
                    last = pe.matmul(bank[4][:, k * C:(k + 1) * C], kxs[:, d, k * P:(k + 1) * P], wvo[:, d, :],
                                     start=(d == 0), stop=(d == KC - 1))
            last.then_inc(s_mp, 1)

            def update(t, q, stage_):
                par = q % 2
                if stage_ == "A":
                    pe.wait_ge(s_nei, t + 2)
                    if some(t):
                        pe.wait_ge(s_dJ, t)
                    for c in range(KC):
                        pe.transpose(PB[:, c * P:(c + 1) * P], neigh[:, par, c * P:(c + 1) * P], ident[:, :])
                    pe.wait_ge(s_tile[par], 32 * ((t - q) // 2 + q // 2) + 32 if isinstance(t, int)
                               else (t - q) * 16 + 32 * (q // 2) + 32)
                    for c in range(KC):
                        last = pe.matmul(PB[:, C:2 * C], xnt[:, par, c * P:(c + 1) * P], wq_s[:, c, :],
                                         start=(c == 0), stop=(c == KC - 1))
                    last.then_inc(s_pA, 1)
                if stage_ == "C":
                    pe.wait_ge(s_dB, t + 1)
                    for c in range(KC):
                        pe.transpose(PB[:, c * P:(c + 1) * P], tmp[:, 3, c * P:(c + 1) * P], ident[:, :])
                    for c in range(2 * KC):
                        lhs = xnt[:, par, c * P:(c + 1) * P] if c < KC else tmp[:, 0, (c - KC) * P:(c - KC + 1) * P]
                        last = pe.matmul(PB[:, C:2 * C], lhs, wg_s[:, c, :], start=(c == 0), stop=(c == 2 * KC - 1))
                    last.then_inc(s_pB, 1)
                if stage_ == "D":
                    pe.wait_ge(s_dC, t + 1)
                    for c in range(2 * KC):
                        lhs = xnt[:, par, c * P:(c + 1) * P] if c < KC else tmp[:, 4, (c - KC) * P:(c - KC + 1) * P]
                        last = pe.matmul(PB[:, 0:C], lhs, (wvo if c < KC else mix)[:, c % KC, :],
                                         start=(c == 0), stop=(c == 2 * KC - 1))
                    last.then_inc(s_pC, 1)
                if stage_ == "F":
                    pe.wait_ge(s_dE, t + 1)
                    for c in range(KC):
                        pe.transpose(PB[:, c * P:(c + 1) * P], xt[:, par, c * P:(c + 1) * P], ident[:, :])
                        last = pe.transpose(PB[:, C + c * P:C + (c + 1) * P], tmp[:, 3, c * P:(c + 1) * P], ident[:, :])
                    last.then_inc(s_pD, 1)
                if stage_ == "G":
                    pe.wait_ge(s_dF, t + 1)
                    for c in range(KC):
                        last = pe.matmul(PB[:, 0:EXP], tmp[:, 0, c * P:(c + 1) * P], rw_s[:, c, :],
                                         start=(c == 0), stop=(c == KC - 1))
                    last.then_inc(s_pE, 1)
                if stage_ == "I":
                    pe.wait_ge(s_dI, t + 1)
                    pe.transpose(PB[0:EXP, 0:P], sc[:, 56:64], ident[:, :]).then_inc(s_pF, 1)

            for k in range(GROUPS):
                sum_group(0, k)
            pe.wait_ge(s_mix, 1)
            for p in range(BT):
                for k in range(POST):
                    if k < GROUPS:
                        sum_group(p + 1, k)
                    if k in STAGES:
                        update(p, p, STAGES[k])

            def second(b, j, cols):
                pe.wait_ge(s_lo, HT * b + j + 1)
                if j == 0:
                    pe.wait_ge(s_y, KC * b + 1)
                hi, lo = hh[:, 2 * (j % 3), 0:cols], hh[:, 2 * (j % 3) + 1, 0:cols]
                for c in range(KC):
                    whi, wlo = unit(2, KC * j + c)
                    o = Y[c][:, 0:cols]
                    pe.matmul(o, whi, hi, start=(j == 0), stop=False)
                    pe.matmul(o, whi, lo, start=False, stop=False)
                    last = pe.matmul(o, wlo, hi, start=False, stop=(j == HT - 1))
                last.then_inc(s_f2, 1)

            def ffn_block(b, agg, tiles, cols):
                pe.wait_ge(s_x2, b + 1)
                for j in range(HT):
                    pe.wait_ge(s_u, HT * b + max(j - 1, 0) + 1)
                    for n, (H, done) in enumerate(((H1, s_h1), (H3, s_h3))):
                        o = H[j % 2][:, 0:cols]
                        for c in range(KC):
                            whi, wlo = unit(n, HT * c + j)
                            xhi, xlo = x2a[:, c, 0:cols], x2a[:, KC + c, 0:cols]
                            pe.matmul(o, whi, xhi, start=(c == 0), stop=False)
                            pe.matmul(o, whi, xlo, start=False, stop=False)
                            last = pe.matmul(o, wlo, xhi, start=False, stop=(c == KC - 1))
                        last.then_inc(done, 1)
                    if j >= 2:
                        second(b, j - 2, cols)
                    if agg:
                        for q, i in GROUP_AT[j]:
                            sum_group(BT * b + AHEAD + q, i)
                    for q, s in stages_at(j, tiles):
                        update(BT * b + BT + q, q, s)
                second(b, HT - 2, cols)
                second(b, HT - 1, cols)

            pe.wait_ge(s_wlo, 3 * SPLITS)
            with pe.Fori(0, BLOCKS - 1) as b:
                ffn_block(b, True, range(BT), NB)
            ffn_block(BLOCKS - 1, False, range(1), NB)
            ffn_block(BLOCKS, False, (), P)

        @block.vector
        def _(dve):
            def link(_=None):
                dve.drain()

            def rsqrt(y, v, t):
                link()
                dve.tensor_scalar(t.bitcast(I32), v.bitcast(I32), 1, None, ALU.logical_shift_right)
                link()
                dve.tensor_scalar(y.bitcast(I32), t.bitcast(I32), -1.0, RSQRT_MAGIC, ALU.mult, ALU.add)
                for _ in range(3):
                    link()
                    dve.tensor_tensor(t, y, y, ALU.mult)
                    link()
                    dve.tensor_tensor(t, t, v, ALU.mult)
                    link()
                    dve.tensor_scalar(t, t, -0.5, 1.5, ALU.mult, ALU.add)
                    link()
                    dve.tensor_tensor(y, y, t, ALU.mult)
                link()

            def rsqrt1(y, v, t):
                link()
                dve.tensor_scalar(t.bitcast(I32), v.bitcast(I32), 1, None, ALU.logical_shift_right)
                link()
                dve.tensor_scalar(y.bitcast(I32), t.bitcast(I32), -1.0, RSQRT_MAGIC, ALU.mult, ALU.add)
                for _ in range(3):
                    link()
                    dve.tensor_scalar(t, y, v, y, ALU.mult, ALU.mult)
                    link()
                    dve.tensor_scalar(t, t, -0.5, 1.5, ALU.mult, ALU.add)
                    link()
                    dve.tensor_tensor(y, y, t, ALU.mult)
                link()

            dve.memset(hot[:, :, :, :], 0.0).then_inc(s_zero, 1)
            dve.memset(tab[:, :, :], 0)
            dve.wait_ge(s_const, 7)

            def ranges():
                dve.wait_ge(s_rng, 16)
                dve.tensor_reduce(dmin, drow, AX.X, ALU.min)
                dve.tensor_reduce(dmax, drow, AX.X, ALU.max)
                link()
                by_tile = (P, TILES, EJ)
                thr = base[:, :, None].broadcast_to(by_tile)
                kk = kidx[:, None, :].broadcast_to(by_tile)
                dve.tensor_tensor(ra, dmax[:, None, :].broadcast_to(by_tile), thr, ALU.subtract)
                link()
                dve.tensor_scalar(rb, ra, 0.0, 1.0e6, ALU.is_lt, ALU.mult)
                link()
                dve.tensor_tensor(ra, rb, kk, ALU.add)
                link()
                dve.tensor_reduce(rall[:, 0:TILES], ra, AX.X, ALU.min)
                link()
                dve.tensor_scalar(rloc[:, 0:TILES], rall[:, 0:TILES], -1.0, None, ALU.mult)
                dve.tensor_tensor(ra, dmin[:, None, :].broadcast_to(by_tile), thr, ALU.subtract)
                link()
                dve.tensor_scalar(rb, ra, float(P), None, ALU.is_lt)
                link()
                dve.tensor_tensor(ra, rb, kk, ALU.mult)
                link()
                dve.tensor_tensor(ra, ra, rb, ALU.add)
                link()
                dve.tensor_reduce(rloc[:, TILES:2 * TILES], ra, AX.X, ALU.max)
                dve.drain().then_inc(s_rloc, 1)

            def node_scales(g, k, n):
                h = k % 2
                dve.wait_ge(s_x[k], 16 * (g // BT) + 16 if isinstance(g, int) else BT * (g - k) + 16)
                if not (isinstance(g, int) and g < 2):
                    dve.wait_ge(s_lnx, g - 1)
                st = sc[:, 40:64].rearrange("p (t s) -> p t s", s=6)
                mv = sc[:, 64:72].rearrange("p (t s) -> p t s", s=2)
                for m in range(n):
                    dve.bn_stats(st[:, m, :], xin[k][:, m, :])
                link()
                for m in range(n):
                    dve.bn_aggr(mv[:, m, :], st[:, m, :])
                link()
                v, t = sc[:, 72:72 + n], sc[:, 76:76 + n]
                y, sh = sc[:, 16 + 8 * h:16 + 8 * h + n], sc[:, 20 + 8 * h:20 + 8 * h + n]
                dve.tensor_scalar(v, mv[:, 0:n, 1], EPS_LN, None, ALU.add)
                rsqrt(y, v, t)
                dve.tensor_tensor(t, mv[:, 0:n, 0], y, ALU.mult)
                link()
                dve.tensor_scalar(sh, t, -1.0, None, ALU.mult).then_inc(s_lnr, 1)

            def node_low(g, k, n):
                dve.wait_ge(s_lnh, g + 1)
                dve.scalar_tensor_tensor(out=xhb[k % 2][:, 0:n, C:2 * C], in0=xin[k][:, 0:n, :], scalar=XS,
                                         in1=xhb[k % 2][:, 0:n, 0:C], op0=ALU.mult, op1=ALU.subtract).then_inc(s_lnl, 1)

            def key_divide(g, k, n):
                o = BT * (k % 2)
                for i, tiles in pairs(n):
                    dve.wait_ge(s_k2, 2 * g + i + 1)
                    a, b_ = tiles[0], tiles[-1] + 1
                    dve.tensor_scalar(sc[:, 0 + a:0 + b_], sc[:, 80 + o + a:80 + o + b_], EPS_DIV, None, ALU.add)
                    link()
                    dve.reciprocal(sc[:, 4 + a:4 + b_], sc[:, 0 + a:0 + b_])
                    link()
                    for m in tiles:
                        last = dve.tensor_scalar(key2[o + m], key2[o + m], sc[:, 4 + m:5 + m], None, ALU.mult)
                    last.then_inc(s_k2n, 1)

            def greatest(c, m):
                dve.wait_ge(s_w[m], 16 * (c // 4) + 16 if isinstance(c, int) else 4 * (c - m) + 16)
                dve.tensor_reduce(wmx[:, ds(c, 1)], wflat[:, ds(c * LCOL, LCOL)], AX.X, ALU.max, apply_absolute_value=True).then_inc(s_wm, 1)

            def centre(weights, cols):
                for i, wgt in enumerate(weights):
                    dve.tensor_reduce(cols[:, i:i + 1], wgt, AX.X, ALU.add)
                link()
                dve.tensor_scalar(cols[:, 3:6], cols[:, 0:3], 1.0 / C, None, ALU.mult)
                link()
                for i, wgt in enumerate(weights):
                    dve.tensor_scalar(wgt, wgt, cols[:, 3 + i:4 + i], None, ALU.subtract)

            def range_table():
                dve.wait_ge(s_rall, 1)
                dve.tensor_scalar(rall[:, 0:TILES], rall[:, 0:TILES], -1.0, float(ET - 1), ALU.mult, ALU.min)
                link()
                dve.tensor_copy(tab[:, 0, 0:TILES], rall[:, 0:TILES])
                dve.tensor_tensor(run[0], rall[:, TILES:2 * TILES], rall[:, 0:TILES], ALU.subtract)
                link()
                dve.tensor_scalar(run[0], run[0], -float(W), 0.0, ALU.add, ALU.max)
                link()
                dve.tensor_copy(tab[:, 1, 0:TILES], run[0])
                dve.tensor_copy(rall[:, 0:TILES], run[0])
                a, b_ = run
                for step in (1, 2, 4, 8, 16, 32):
                    link()
                    dve.tensor_copy(b_[:, 0:step], a[:, 0:step])
                    dve.tensor_tensor(b_[:, step:TILES], a[:, step:TILES], a[:, 0:TILES - step], ALU.add)
                    a, b_ = b_, a
                link()
                dve.tensor_tensor(a, a, rall[:, 0:TILES], ALU.subtract)
                link()
                dve.tensor_copy(tab[:, 2, 0:TILES], a)
                dve.drain().then_inc(s_tab, 1)

            def step(s, k, sizes):
                if sizes[-2]:
                    key_divide(s - 2, k, sizes[-2])
                if sizes[0]:
                    node_low(s, k, sizes[0])
                if not isinstance(s, int) or 2 * s < 3 * LOADS:
                    for m in range(2):
                        greatest(2 * s + m, (2 * k + m) % 4)
                if sizes[1]:
                    node_scales(s + 1, (k + 1) % BT, sizes[1])
                if isinstance(s, int) and s == 0:
                    ranges()
                if isinstance(s, int) and s == 1:
                    range_table()

            node_scales(0, 0, BT)
            dve.wait_ge(s_wk, 32)
            centre((wk_s[:, 0, :], wk_s[:, 1, :], bk_b[:, :]), sc[:, 88:94])
            dve.drain().then_inc(s_ck, 1)
            first_pass(dve, step)

            dve.wait_ge(s_wld, 16 * 9)
            centre((wq_s[:, 0, :], wq_s[:, 1, :], bq_b[:, :]), sc[:, 88:94])
            for k in range(KC):
                dve.tensor_scalar(bvr[:, k, :], ident[:, :], 0.0, bv_s[:, k:k + 1], ALU.mult, ALU.add)
            dve.drain().then_inc(s_cent, 1)

            dve.tensor_reduce(sc[:, 0:3], wmx[:, :].rearrange("p (n t) -> p n t", n=3), AX.X, ALU.max)
            dve.drain().then_inc(s_nloc, 1)

            def weight_scales():
                dve.wait_ge(s_nall, 1)
                dve.tensor_scalar(sc[:, 8:11], sc[:, 4:7], TINY, None, ALU.max)
                link()
                p = sc[:, 12:15]
                dve.tensor_scalar(p.bitcast(I32), sc[:, 8:11].bitcast(I32), 0x7F800000, None, ALU.bitwise_and)
                link()
                dve.tensor_scalar(cst[:, 0:3].bitcast(I32), p.bitcast(I32), -1.0, float((127 + 127 + 13) << 23),
                                  ALU.mult, ALU.add)
                dve.tensor_scalar(cst[:, 3:4], p[:, 0:1], 2.0 ** -23, None, ALU.mult)
                dve.tensor_tensor(cst[:, 5:6], p[:, 0:1], p[:, 1:2], ALU.mult)
                link()
                dve.tensor_scalar(cst[:, 4:5], cst[:, 0:1], 2.0 ** -39, None, ALU.mult)
                dve.tensor_scalar(cst[:, 5:6], cst[:, 5:6], p[:, 2:3], 2.0 ** -10, ALU.mult, ALU.mult)
                dve.drain().then_inc(s_cst, 1)

            def window(t, par, use, col=None):
                dve.wait_ge(s_win[par], 32 * use)
                dve.tensor_scalar(dstf[:, par, :], dstw[:, par, :], base[:, ds(t, 1)], None, ALU.subtract)
                link()

            def one_hots(t, i, par):
                dve.wait_ge(s_used, GROUPS * t + i + 1)
                dve.tensor_tensor(hot[:, i % RG, :, :], lane[:, None, :].broadcast_to((P, WG, P)),
                                  par_dst(par)[:, WG * i:WG * i + WG, None].broadcast_to((P, WG, P)), ALU.is_equal)\
                    .then_inc(s_hot, 1)
                if i == 0:
                    one_hots_extra(t)

            def par_dst(par):
                return dstf[:, par, :]

            def one_hots_extra(t):
                n = dve.value_load(tab[0:1, 1, ds(t, 1)], min_val=0, max_val=ET)
                done = dve.value_load(tab[0:1, 2, ds(t, 1)], min_val=0, max_val=ET * TILES)
                with dve.If(n > 0):
                    with dve.Fori(0, n) as k:
                        dve.wait_ge(s_xs, done + k + 1)
                        dve.wait_ge(s_xd, done + k + 1)
                        dve.tensor_scalar(xdf[:, :], xdst[:, :], base[:, ds(t, 1)], None, ALU.subtract)
                        dve.drain()
                        dve.tensor_scalar(xhot[:, :], lane[:, :], xdf[:, 0:1], None, ALU.is_equal).then_inc(s_xh, 1)

            def neighbours(t, par):
                dve.wait_ge(s_agg, t + 1)
                dve.tensor_scalar(sc[:, 34:35], AG[:, C:C + 1], 1.0, None, ALU.max)
                link()
                dve.reciprocal(sc[:, 35:36], sc[:, 34:35])
                link()
                dve.tensor_scalar(neigh[:, par, :], AG[:, 0:C], sc[:, 35:36], 1.0 / XS, ALU.mult, ALU.mult)\
                    .then_inc(s_nei, 1)

            weight_scales()

            dve.wait_ge(s_kx, TILES)
            dve.tensor_copy(kxs.rearrange("p k c -> p (k c)"), Y[0][:, :]).then_inc(s_kxs, 1)
            dve.tensor_copy(sc[:, 0:4], Y[1][:, 0:4])
            link()
            dve.tensor_scalar(sc[:, 4:6], sc[:, 2:4], TINY, None, ALU.max)
            rsqrt(sc[:, 8:10], sc[:, 4:6], sc[:, 12:14])
            dve.tensor_tensor(sc[:, 4:6], sc[:, 4:6], sc[:, 8:10], ALU.mult)
            link()
            dve.tensor_scalar(sc[:, 4:6], sc[:, 4:6], EPS_NORM, None, ALU.max)
            link()
            dve.reciprocal(sc[:, 8:10], sc[:, 4:6])
            dve.wait_ge(s_wvo, 1)
            dve.wait_ge(s_bo, 16)
            dve.tensor_copy(sbv, bank[3][:, 0:C])
            link()
            dve.tensor_tensor(co_b[:, :], sbv, bo_b, ALU.add)
            dve.wait_ge(s_mp, 1)
            for k in range(KC):
                dve.scalar_tensor_tensor(out=mix[:, k, :], in0=sbv, scalar=sc[:, k:k + 1],
                                         in1=bank[4][:, k * C:(k + 1) * C], op0=ALU.mult, op1=ALU.add)
            link()
            for k in range(KC):
                last = dve.tensor_scalar(mix[:, k, :], mix[:, k, :], sc[:, 8 + k:9 + k], float(NODES) ** -0.5,
                                         ALU.mult, ALU.mult)
            dve.drain().then_inc(s_mix, 1)

            def update(t, q, stage_, b=None):
                par = q % 2
                if stage_ == "A":
                    dve.wait_ge(s_pA, t + 1)
                    dve.tensor_copy(tmp[:, 0, :], PB[:, 0:C])
                    dve.tensor_tensor(tmp[:, 1, :], PB[:, C:2 * C], bq_b[:, :], ALU.add)
                    dve.drain().then_inc(s_dA, 1)
                if stage_ == "B":
                    dve.wait_ge(s_aA, t + 1)
                    dve.tensor_scalar(sc[:, 3:4], sc[:, 0:1], EPS_DIV, None, ALU.add)
                    dve.tensor_scalar(sc[:, 4:5], sc[:, 1:2], TINY, None, ALU.max)
                    link()
                    dve.reciprocal(sc[:, 5:6], sc[:, 3:4])
                    rsqrt1(sc[:, 6:7], sc[:, 4:5], sc[:, 7:8])
                    dve.tensor_tensor(sc[:, 7:8], sc[:, 4:5], sc[:, 6:7], ALU.mult)
                    link()
                    dve.tensor_scalar(sc[:, 6:7], sc[:, 7:8], sc[:, 5:6], EPS_NORM, ALU.mult, ALU.max)
                    link()
                    dve.reciprocal(sc[:, 7:8], sc[:, 6:7])
                    link()
                    dve.tensor_scalar(tmp[:, 3, :], tmp[:, 1, :], sc[:, 5:6], sc[:, 7:8], ALU.mult, ALU.mult)\
                        .then_inc(s_dB, 1)
                if stage_ == "C":
                    dve.wait_ge(s_pB, t + 1)
                    dve.tensor_copy(tmp[:, 4, :], PB[:, 0:C])
                    dve.tensor_tensor(tmp[:, 1, :], PB[:, C:2 * C], bg_b[:, :], ALU.add)
                    dve.drain().then_inc(s_dC, 1)
                if stage_ == "D":
                    dve.wait_ge(s_aC, t + 1)
                    dve.tensor_scalar(sc[:, 4:5], sc[:, 2:3], TINY, None, ALU.max)
                    rsqrt1(sc[:, 6:7], sc[:, 4:5], sc[:, 7:8])
                    dve.tensor_tensor(sc[:, 7:8], sc[:, 4:5], sc[:, 6:7], ALU.mult)
                    link()
                    dve.tensor_scalar(sc[:, 6:7], sc[:, 7:8], EPS_NORM, None, ALU.max)
                    link()
                    dve.reciprocal(sc[:, 7:8], sc[:, 6:7])
                    link()
                    dve.scalar_tensor_tensor(out=xt[:, par, :], in0=tmp[:, 1, :], scalar=sc[:, 7:8],
                                             in1=xt[:, par, :], op0=ALU.mult, op1=ALU.add)
                    link()
                    dve.tensor_tensor(xt[:, par, :], xt[:, par, :], co_b[:, :], ALU.add)
                    link()
                    dve.wait_ge(s_pC, t + 1)
                    dve.tensor_tensor(xt[:, par, :], PB[:, 0:C], xt[:, par, :], ALU.add)
                    link()
                if stage_ == "E":
                    dve.bn_stats(sc[:, 8:14], xt[:, par, :])
                    link()
                    dve.bn_aggr(sc[:, 14:16], sc[:, 8:14])
                    link()
                    dve.tensor_scalar(sc[:, 4:5], sc[:, 15:16], EPS_LN, None, ALU.add)
                    rsqrt1(sc[:, 6:7], sc[:, 4:5], sc[:, 7:8])
                    dve.tensor_scalar(tmp[:, 3, :], xt[:, par, :], sc[:, 14:15], sc[:, 6:7],
                                      ALU.subtract, ALU.mult).then_inc(s_dE, 1)
                if stage_ == "F":
                    dve.wait_ge(s_pD, t + 1)
                    if b is not None:
                        dve.wait_ge(s_x1, b + 1)
                    dve.tensor_copy(x1s[:, :].rearrange("p (k n) -> p k n", k=KC)[:, :, q * P:(q + 1) * P],
                                    PB[:, 0:C].rearrange("p (k n) -> p k n", k=KC))
                    dve.tensor_scalar(tmp[:, 0, :], PB[:, C:2 * C], XS, None, ALU.mult)
                    dve.drain().then_inc(s_dF, 1)
                if stage_ == "G":
                    dve.wait_ge(s_aF, t + 1)
                    dve.tensor_tensor(x2s[:, KC:2 * KC, q * P:(q + 1) * P],
                                      tmp[:, 0, :].rearrange("p (k n) -> p k n", k=KC),
                                      x2s[:, 0:KC, q * P:(q + 1) * P], ALU.subtract).then_inc(s_dG, 1)
                    dve.wait_ge(s_pE, t + 1)
                    dve.tensor_scalar(sc[:, 40:48], PB[:, 0:EXP], 1.0 / XS, None, ALU.mult)
                    link()
                    dve.max(sc[:, 48:56], sc[:, 40:48])
                    link()
                    dve.max_index(idx8[:, :], sc[:, 48:56], sc[:, 40:48])
                    dve.tensor_scalar(sc[:, 64:72], sc[:, 48:56], sc[:, 48:49], None, ALU.subtract)
                    dve.drain().then_inc(s_dH, 1)
                if stage_ == "H":
                    dve.wait_ge(s_aH, t + 1)
                    ex, de = sc[:, 80:88], sc[:, 88:96]
                    dve.tensor_scalar(ex, sc[:, 72:80], 1.0, None, ALU.add)
                    dve.tensor_scalar(de, sc[:, 72:80], -1.0, 1.0, ALU.mult, ALU.add)
                    link()
                    dve.reciprocal(sc[:, 64:72], de)
                    link()
                    dve.tensor_tensor(ex, ex, sc[:, 64:72], ALU.mult)
                    for _ in range(3):
                        link()
                        dve.tensor_tensor(ex, ex, ex, ALU.mult)
                    link()
                    dve.tensor_reduce(sc[:, 3:4], ex, AX.X, ALU.add)
                    dve.tensor_copy(sc[:, 72:74], idx8[:, 0:2])
                    link()
                    dve.reciprocal(sc[:, 4:5], sc[:, 3:4])
                    link()
                    dve.tensor_scalar(sc[:, 88:90], ex[:, 0:2], sc[:, 4:5], None, ALU.mult)
                    link()
                    dve.tensor_scalar(sc[:, 5:6], sc[:, 88:89], sc[:, 89:90], 1e-9, ALU.add, ALU.add)
                    link()
                    dve.reciprocal(sc[:, 6:7], sc[:, 5:6])
                    link()
                    dve.tensor_scalar(sc[:, 90:92], sc[:, 88:90], sc[:, 6:7], None, ALU.mult)
                    link()
                    dve.tensor_scalar(sc[:, 40:48], lane8[:, :], sc[:, 72:73], sc[:, 90:91], ALU.is_equal, ALU.mult)
                    dve.tensor_scalar(sc[:, 48:56], lane8[:, :], sc[:, 73:74], sc[:, 91:92], ALU.is_equal, ALU.mult)
                    link()
                    dve.tensor_tensor(sc[:, 56:64], sc[:, 40:48], sc[:, 48:56], ALU.add).then_inc(s_dI, 1)
                if stage_ == "I":
                    if some(t):
                        dve.wait_ge(s_gst, t * 16)
                    dve.wait_ge(s_pF, t + 1)
                    dve.tensor_copy(gts[:, :], PB[0:EXP, 0:P]).then_inc(s_dJ, 1)

            def split_low(c):
                _, high, low_, aside = split_chunk(c)
                dve.wait_ge(s_whi, c + 1)
                dve.tensor_tensor(low_, aside.rearrange("p (u c) -> p u c", c=P), high, ALU.subtract).then_inc(s_wlo, 1)

            for p in range(-1, BT):
                for k in range(POST):
                    if k == 0:
                        window(p + 1, (p + 1) % 2, (p + 1) // 2 + 1)
                    if k < GROUPS:
                        one_hots(p + 1, k, (p + 1) % 2)
                    for c in splits_at(p, k):
                        split_low(c)
                    if p >= 0 and k in STAGES:
                        update(p, p, STAGES[k])
                neighbours(p + 1, (p + 1) % 2)

            def take_input(b, n):
                dve.drain()
                dve.wait_ge(s_aF, n)
                if some(b):
                    dve.wait_ge(s_h3, HT * b)
                dve.tensor_copy(x2a[:, :, :], x2s[:, :, :]).then_inc(s_x2, 1)

            take_input(0, BT)

            def low(b, j, cols):
                dve.wait_ge(s_hi, HT * b + j + 1)
                dve.tensor_tensor(hh[:, 2 * (j % 3) + 1, 0:cols], hid[:, (j % 2) * NB:(j % 2) * NB + cols],
                                  hh[:, 2 * (j % 3), 0:cols], ALU.subtract).then_inc(s_lo, 1)

            def ffn_block(b, agg, tiles, cols, nxt):
                for j in range(HT):
                    if agg:
                        for q, i in (GROUP_AT[0] if j == 0 else []) + (GROUP_AT[j + 1] if j + 1 < HT else []):
                            t, par = BT * b + AHEAD + q, (AHEAD + q) % 2
                            if i == 0:
                                window(t, par, 2 * b + (AHEAD + q) // 2 + 1)
                            one_hots(t, i, par)
                    s, h = (sig[:, (j % 2) * NB:(j % 2) * NB + cols], hid[:, (j % 2) * NB:(j % 2) * NB + cols])
                    dve.wait_ge(s_h3, HT * b + j + 1)
                    dve.wait_ge(s_sig, HT * b + j + 1)
                    dve.scalar_tensor_tensor(out=h, in0=H3[j % 2][:, 0:cols], scalar=cst[:, 4:5], in1=s,
                                             op0=ALU.mult, op1=ALU.mult).then_inc(s_u, 1)
                    if j:
                        low(b, j - 1, cols)
                    i = j // FULL if j < HT_FULL else EXP + j - HT_FULL
                    if j % FULL == 0 or j >= HT_FULL:
                        dve.wait_ge(s_gld[i % GSLOTS], gate_count(b, i))
                    dve.wait_ge(s_u, HT * b + j + 2)
                    g = gate[:, (i % GSLOTS) * NB:(i % GSLOTS) * NB + cols]
                    dve.tensor_tensor(h, h, g, ALU.mult).then_inc(s_t, 1)
                    for q, st in stages_at(j, tiles):
                        update(BT * b + BT + q, q, st, b)
                    if agg:
                        for q, i in GROUP_AT[j]:
                            if i == GROUPS - 1:
                                neighbours(BT * b + AHEAD + q, (AHEAD + q) % 2)
                low(b, HT - 1, cols)
                if nxt:
                    take_input(b + 1, BT * b + BT + len(tiles))
                dve.wait_ge(s_x1, b + 1)
                dve.wait_ge(s_f2, HT * b + HT + 1)
                for k in range(KC):
                    o = x1a[:, k * NB:k * NB + cols]
                    dve.scalar_tensor_tensor(out=o, in0=Y[k][:, 0:cols], scalar=cst[:, 5:6], in1=o,
                                             op0=ALU.mult, op1=ALU.add).then_inc(s_y, 1)

            with dve.Fori(0, BLOCKS - 1) as b:
                ffn_block(b, True, range(BT), NB, True)
            ffn_block(BLOCKS - 1, False, range(1), NB, True)
            ffn_block(BLOCKS, False, (), P, False)


def gate_count(b, i):
    def dmas(k):
        return 1 if k < EXP else len(segments(HT_FULL + k - EXP))

    slot = [k for k in range(GLOADS) if k % GSLOTS == i % GSLOTS]
    return b * (16 * sum(map(dmas, slot))) + 16 * sum(dmas(k) for k in slot if k <= i)


def kernel(x, src, dst, L0_gnn_W, L0_gnn_b, L0_mix_W_qkv, L0_mix_b_qkv, L0_mix_W_out, L0_mix_b_out,
           L0_ffn_router_w, L0_ffn_w1, L0_ffn_w2, L0_ffn_w3):
    import numpy as np
    import concourse.bacc as bacc
    from concourse.bass_utils import run_bass_kernel_spmd

    def pad(a, n, value=0):
        out = np.full((n,) + a.shape[1:], value, a.dtype)
        out[:a.shape[0]] = a
        return out

    def hidden_rows(w):
        a = np.concatenate([w[:, :FULL * P].reshape(-1, C), w[:, FULL * P:].reshape(-1, C)])
        return pad(a, HPAD)

    x, src, dst = np.asarray(x), np.asarray(src), np.asarray(dst)
    w1, w2, w3 = np.asarray(L0_ffn_w1), np.asarray(L0_ffn_w2), np.asarray(L0_ffn_w3)
    wqkv, bqkv = np.asarray(L0_mix_W_qkv), np.asarray(L0_mix_b_qkv)
    nowhere = 1 << 20
    w13T = [hidden_rows(w).T.reshape(KC, P, HPAD).transpose(1, 0, 2).reshape(P, KC * HPAD) for w in (w1, w3)]
    w2T = hidden_rows(w2.transpose(0, 2, 1)).reshape(HT, P, C).transpose(1, 0, 2).reshape(P, HT * C)
    arrays = {
        "x": pad(x, NODE_GROUPS * NB),
        "srcT": pad(src, ETW * P).reshape(ETW, P).T,
        "dstT": pad(dst, ETW * P, nowhere).reshape(ETW, P).T,
        "dst_rows": pad(dst, EJ * P * P, nowhere).reshape(EJ * P, P),
        "Wg": np.asarray(L0_gnn_W), "bg": np.asarray(L0_gnn_b)[None, :],
        "Wq": wqkv[:, 0:C], "Wk": wqkv[:, C:2 * C], "WvT": wqkv[:, 2 * C:].T,
        "bq": bqkv[None, 0:C], "bk": bqkv[None, C:2 * C], "bv": bqkv[2 * C:, None],
        "Wo": np.asarray(L0_mix_W_out), "bo": np.asarray(L0_mix_b_out)[None, :],
        "rwT": np.asarray(L0_ffn_router_w).T,
        "wT": np.stack(w13T + [w2T]),
    }
    arrays = {f"in_{k}": np.ascontiguousarray(v) for k, v in arrays.items()}
    nc = bacc.Bacc("TRN2", target_bir_lowering=False, num_devices=1, dynamic_dma_scratch_size=14336)
    args = [nc.dram_tensor(k, v.shape, mybir.dt.from_np(v.dtype), kind="ExternalInput").ap() for k, v in arrays.items()]
    out = nc.dram_tensor("out_t", (C, NODES), F32, kind="ExternalOutput").ap()
    gnn_mix_moe(nc, *args, out)
    r = run_bass_kernel_spmd(nc, [arrays], core_ids=[0])
    return np.ascontiguousarray(r.results[0]["out_t"].T)
```

```python
import concourse.bass as bass
from concourse import mybir
from contextlib import ExitStack

P = 128
F32 = mybir.dt.float32
F16 = mybir.dt.float16
I32 = mybir.dt.int32
U32 = mybir.dt.uint32
ALU = mybir.AluOpType
ACT = mybir.ActivationFunctionType
AX = mybir.AxisListType
RMAX = bass.bass_isa.ReduceOp.max

NODES = 6250
C = 256
KC = C // P
TILES = -(-NODES // P)
NPAD = TILES * P
LAST = NODES - (TILES - 1) * P
EDGES = 200000
ET = -(-EDGES // P)
W = 34
WG = 4
GROUPS = -(-W // WG)
RG = 3
ETW = ET + W + 1
EJ = -(-ET // P)
EXP = 8
HID = 682
FULL = HID // P
HT_FULL = EXP * FULL
REST = HID - FULL * P
HT = HT_FULL + -(-EXP * REST // P)
HPAD = HT * P
BT = 4
NB = BT * P
BLOCKS = -(-(TILES - 1) // BT)
GLOADS = EXP + HT - HT_FULL
GSLOTS = 3
XS = 1024.0
TROW = 64
NODE_GROUPS = -(-TILES // BT)
UNITS = KC * HT
WU = 11
SPLITS = -(-UNITS // WU)
LOADS = 8
LCOL = UNITS * P // LOADS
EPS_LN, EPS_DIV, EPS_NORM = 1e-5, 1e-7, 1e-12
TINY = 1e-30
RSQRT_MAGIC = float(0x5F3759DF)



def first_node(b):
    return P * (BT * b - (BT - 1)) if not isinstance(b, int) or b else 0


GROUP_AT = [[] for _ in range(HT)]
for _g in range(BT * GROUPS):
    GROUP_AT[int((_g + 0.5) * (HT - BT - 1) / (BT * GROUPS))].append((_g // GROUPS, _g % GROUPS))
POST = 10
STAGES = dict(zip((1, 2, 3, 4, 6, 7, 8, 9, 10), "ABCDEFGHI"))


def stages_at(step, tiles):
    return [(q, STAGES[step - POST * q]) for q in tiles if step - POST * q in STAGES]


def splits_at(p, k):
    first, double = (0, range(1, 8)) if p < 0 else (POST + 7, ())
    at = [i for i in range(POST) for _ in range(2 if i in double else 1)]
    return [first + n for n, i in enumerate(at) if i == k and first + n < 3 * SPLITS]


def some(n):
    return not (isinstance(n, int) and n == 0)


def group_size(i):
    return min(WG, W - WG * i)


def rows_count(t, i):
    mine = [k for k in range(GROUPS) if k % RG == i % RG]
    return 16 * sum(map(group_size, mine)) * t + 16 * sum(group_size(k) for k in mine if k <= i)


def segments(tile):
    first = (tile - HT_FULL) * P
    out, r = [], first
    while r < min(first + P, EXP * REST):
        e = r // REST
        end = min((e + 1) * REST, first + P, EXP * REST)
        out.append((r - first, end - first, e))
        r = end
    return out


def gnn_mix_moe(nc, x, srcT, dstT, dst_rows, Wg, bg, Wq, Wk, WvT, bq, bk, bv, Wo, bo, rwT, wT, outT):
    with ExitStack() as ctx:
        def sb(name, shape, dt=F32):
            return ctx.enter_context(nc.sbuf_tensor(name, shape, dt))

        def sem(name):
            return ctx.enter_context(nc.semaphore(name))

        def sems(name, n):
            return [sem(f"{name}_{i}") for i in range(n)]

        def dram(name, shape, dt=F32):
            return nc.dram_tensor(name, shape, dt).ap()

        XH = dram("xn_split", (NPAD, 2 * C), F16)
        XT = dram("xn_cols", (NPAD, C))
        GT = dram("gates_t", (EXP, NPAD))

        wts = sb("wts", [P, 3, UNITS, 2, P], F16)
        x2s = sb("x2s", [P, 2 * KC, NB], F16)
        x2a = sb("x2a", [P, 2 * KC, NB], F16)
        x1s = sb("x1s", [P, KC * NB])
        x1a = sb("x1a", [P, KC * NB])
        gate = sb("gate", [P, GSLOTS * NB])
        sig = sb("sig", [P, 2 * NB])
        hid = sb("hid", [P, 2 * NB])
        hh = sb("hh", [P, 3 * 2, NB], F16)
        rows = sb("rows", [P, RG * WG, 2 * C + 2], F16)
        hot = sb("hot", [P, RG, WG, P], F16)
        wq_s = sb("wq_s", [P, KC, C])
        wg_s = sb("wg_s", [P, 2 * KC, C])
        mix = sb("mix", [P, KC, C])
        wvo = sb("wvo", [P, KC, C])
        bq_b = sb("bq_b", [P, C])
        bg_b = sb("bg_b", [P, C])
        co_b = sb("co_b", [P, C])
        rw_s = sb("rw_s", [P, KC, EXP])
        ident = sb("ident", [P, P])
        lane = sb("lane", [P, P], F16)
        xt = sb("xt", [P, 2, C])
        xnt = sb("xnt", [P, 2, C])
        neigh = sb("neigh", [P, 2, C])
        tmp = sb("tmp", [P, 5, C])
        srcw = sb("srcw", [P, 2, W], I32)
        dstw = sb("dstw", [P, 2, W], I32)
        dstf = sb("dstf", [P, 2, W])
        base = sb("base", [P, TILES])
        tab = sb("tab", [P, 3, TROW], I32)
        xsrc = sb("xsrc", [P, 1], I32)
        xdst = sb("xdst", [P, 1], I32)
        xdf = sb("xdf", [P, 1])
        xrow = sb("xrow", [P, 2 * C + 2], F16)
        xhot = sb("xhot", [P, P], F16)
        sc = sb("sc", [P, 96])
        cst = sb("cst", [P, 8])
        lane8 = sb("lane8", [P, EXP])
        idx8 = sb("idx8", [P, EXP], U32)
        gts = sb("gts", [EXP, P])
        one = sb("one", [P, 1])
        wmx = sb("wmx", [P, 3 * LOADS])

        def tiles4(a):
            return a.rearrange("p (t c) -> p t c", c=C)

        rflat = rows[:, :, :].rearrange("p a n -> p (a n)").bitcast(F32)
        hflat = hh[:, :, :].rearrange("p a n -> p (a n)").bitcast(F32)
        gflat = gate[:, :]
        xin = [tiles4(a[:, :]) for a in (x1s, x1a, sig, hid)]
        xtb = [tiles4(rflat[:, 1024 * h:1024 * (h + 1)]) for h in range(2)]
        xhb = [x2s[:, :, :], x2a[:, :, :]]
        key2 = [a[:, i, :] for a in (xt, xnt, neigh, wvo) for i in range(2)]
        key4 = [tmp[:, i, :] for i in range(BT)]
        wk_s, bk_b = mix, co_b
        stage = [hflat, gflat]
        wvt_s = gflat[:, 0:512].rearrange("p (k c) -> p k c", c=C)
        wo_s = gflat[:, 512:1024].rearrange("p (k c) -> p k c", c=C)
        bv_s = gflat[:, 1024:1024 + KC]
        bvr = gflat[:, 1040:1040 + KC * P].rearrange("p (k c) -> p k c", c=P)
        kxs = tmp[:, 0:2, :]
        sbv, bo_b = tmp[:, 2, :], tmp[:, 3, :]
        wflat = wts[:, :, :, :, :].rearrange("p n u h c -> p (n u h c)").bitcast(F32)
        rng = wflat[:, 2 * UNITS * P:]
        drow = rng[:, 0:EJ * P].bitcast(I32).rearrange("p (j e) -> p j e", e=P)
        rng = rng[:, EJ * P:]
        kidx, dmin, dmax = rng[:, 0:EJ], rng[:, 20:20 + EJ], rng[:, 40:40 + EJ]
        ra = rng[:, 100:100 + TILES * EJ].rearrange("p (t j) -> p t j", j=EJ)
        rb = rng[:, 800:800 + TILES * EJ].rearrange("p (t j) -> p t j", j=EJ)
        rloc, rall = rng[:, 2800:2800 + 2 * TILES], rng[:, 3000:3000 + 2 * TILES]
        run = [rng[:, 3200 + 64 * i:3200 + 64 * i + TILES] for i in range(2)]

        bank = [ctx.enter_context(nc.psum_tensor(f"bank{i}", [P, 512], F32)) for i in range(8)]
        Y, H1, H3, AG, PB = bank[0:2], bank[2:4], bank[4:6], bank[6], bank[7]

        s_wld = sem("s_wld")
        s_bo = sem("s_bo")
        s_rng = sem("s_rng")
        s_x = sems("s_x", BT)
        s_xst = sems("s_xst", 2)
        s_w = sems("s_w", 4)
        s_wk = sem("s_wk")
        s_win = sems("s_win", 2)
        s_row = sems("s_row", RG)
        s_tile = sems("s_tile", 2)
        s_gst = sem("s_gst")
        s_gld = sems("s_gld", GSLOTS)
        s_out = sem("s_out")
        s_xi = sem("s_xi")
        s_xr = sem("s_xr")
        s_const = sem("s_const")
        s_ident = sem("s_ident")
        s_rloc = sem("s_rloc")
        s_rall = sem("s_rall")
        s_tab = sem("s_tab")
        s_wm = sem("s_wm")
        s_nloc = sem("s_nloc")
        s_nall = sem("s_nall")
        s_cst = sem("s_cst")
        s_zero = sem("s_zero")
        s_lnr = sem("s_lnr")
        s_lnx = sem("s_lnx")
        s_lnh = sem("s_lnh")
        s_lnl = sem("s_lnl")
        s_lnt = sem("s_lnt")
        s_lnc = sem("s_lnc")
        s_ck = sem("s_ck")
        s_cent = sem("s_cent")
        s_kp = sem("s_kp")
        s_k2 = sem("s_k2")
        s_k2n = sem("s_k2n")
        s_k4 = sem("s_k4")
        s_kx = sem("s_kx")
        s_wvo = sem("s_wvo")
        s_wvc = sem("s_wvc")
        s_kxs = sem("s_kxs")
        s_mp = sem("s_mp")
        s_mix = sem("s_mix")
        s_stg = sem("s_stg")
        s_stgd = sem("s_stgd")
        s_whi = sem("s_whi")
        s_wlo = sem("s_wlo")
        s_hot = sem("s_hot")
        s_used = sem("s_used")
        s_agg = sem("s_agg")
        s_nei = sem("s_nei")
        s_pool = sem("s_pool")
        s_sp = sem("s_sp")
        s_xs = sem("s_xs")
        s_xh = sem("s_xh")
        s_xd = sem("s_xd")
        s_query_psum = sem("s_query_psum")
        s_query = sem("s_query")
        s_query_norm = sem("s_query_norm")
        s_query_unit = sem("s_query_unit")
        s_graph_psum = sem("s_graph_psum")
        s_graph = sem("s_graph")
        s_graph_norm = sem("s_graph_norm")
        s_attn_psum = sem("s_attn_psum")
        s_norm2 = sem("s_norm2")
        s_norm2_t = sem("s_norm2_t")
        s_ffn_in = sem("s_ffn_in")
        s_ffn_high = sem("s_ffn_high")
        s_logits = sem("s_logits")
        s_logits_less = sem("s_logits_less")
        s_tanh = sem("s_tanh")
        s_gates = sem("s_gates")
        s_gates_psum = sem("s_gates_psum")
        s_gates_t = sem("s_gates_t")
        s_h1 = sem("s_h1")
        s_h3 = sem("s_h3")
        s_sig = sem("s_sig")
        s_u = sem("s_u")
        s_t = sem("s_t")
        s_hi = sem("s_hi")
        s_lo = sem("s_lo")
        s_f2 = sem("s_f2")
        s_x2 = sem("s_x2")
        s_x1 = sem("s_x1")
        s_y = sem("s_y")

        block = ctx.enter_context(nc.Block())
        ds = bass.ds

        def rows_of(t, first, n):
            return t[ds(first * P, n * P), :].rearrange("(t p) c -> p t c", p=P)

        def load_piece(c):
            return wflat[:, c * LCOL:(c + 1) * LCOL]

        def split_chunk(c):
            n, k = divmod(c, SPLITS)
            u0, u1 = WU * k, min(WU * (k + 1), UNITS)
            whole = wflat[:, (n * UNITS + u0) * P:(n * UNITS + u1) * P]
            aside = stage[c % 2][:, 0:(u1 - u0) * P]
            return whole, wts[:, n, u0:u1, 0, :], wts[:, n, u0:u1, 1, :], aside

        def unit(n, u):
            return wts[:, n, u, 0, :], wts[:, n, u, 1, :]

        def pairs(n):
            return [(i, range(2 * i, min(2 * i + 2, n))) for i in range((n + 1) // 2)]

        FIRST, TURNS = 3, 2

        def first_pass(engine, step):
            def sizes(s):
                return {i: 0 if not 0 <= s + i < NODE_GROUPS else min(BT, TILES - BT * (s + i)) for i in range(-2, 3)}

            for s in range(FIRST):
                step(s, s % BT, sizes(s))
            with engine.Fori(0, TURNS) as turn:
                for k in range(BT):
                    step(BT * turn + (FIRST + k), (FIRST + k) % BT, sizes(FIRST + k))
            for s in range(FIRST + BT * TURNS, NODE_GROUPS + 2):
                step(s, s % BT, sizes(s))

        @block.sync
        def _(sp):
            def load_group(g, k):
                if not (isinstance(g, int) and g < BT):
                    sp.wait_ge(s_kx, BT * (g - BT) + BT)
                    sp.sem_inc(s_sp, 1)
                    sp.wait_ge(s_lnl, g - BT + 1)
                sp.dma_start(xin[k], rows_of(x, BT * g, BT)).then_inc(s_x[k], 16)

            load_group(0, 0)
            for dst_, src_ in ((wk_s[:, :, :], Wk.rearrange("(k p) c -> p k c", p=P)), (bk_b[:, :], bk.broadcast_to((P, C)))):
                sp.dma_start(dst_, src_).then_inc(s_wk, 16)
            load_group(1, 1)
            sp.dma_start(drow, dst_rows.rearrange("(p j) e -> p j e", j=EJ)).then_inc(s_rng, 16)
            for k in range(2, BT):
                load_group(k, k)
            for dst_, src_ in ((wq_s[:, :, :], Wq), (wvt_s, WvT), (wo_s, Wo), (rw_s[:, :, :], rwT), (wg_s[:, :, :], Wg)):
                sp.dma_start(dst_, src_.rearrange("(k p) c -> p k c", p=P)).then_inc(s_wld, 16)
            for dst_, src_ in ((bq_b, bq), (bg_b, bg)):
                sp.dma_start(dst_[:, :], src_.broadcast_to((P, C))).then_inc(s_wld, 16)
            for k in range(KC):
                sp.dma_start(bv_s[:, k:k + 1], bv[k * P:(k + 1) * P, :]).then_inc(s_wld, 16)

            def step(s, k, sizes):
                if n := sizes[0]:
                    sp.wait_ge(s_lnl, s + 1)
                    sp.dma_start(rows_of(XH, BT * s, n), xhb[k % 2][:, 0:n, :]).then_inc(s_xst[k % 2], 16)
                    sp.wait_ge(s_lnc, s + 1)
                    sp.dma_start(rows_of(XT, BT * s, n), xtb[k % 2][:, 0:n, :]).then_inc(s_xst[k % 2], 16)
                if sizes[2] and not (isinstance(s, int) and s < 2):
                    load_group(s + 2, (k + 2) % BT)

            first_pass(sp, step)

            def load_window(t, par):
                if not isinstance(t, int) or t > 1:
                    sp.wait_ge(s_agg, t - 1)
                first = sp.value_load(tab[0:1, 0, ds(t, 1)], min_val=0, max_val=ET - 1)
                sp.dma_start(srcw[:, par, :], srcT[:, ds(first, W)]).then_inc(s_win[par], 16)
                sp.dma_start(dstw[:, par, :], dstT[:, ds(first, W)]).then_inc(s_win[par], 16)

            def load_tile(t, par):
                if not isinstance(t, int) or t > 1:
                    sp.wait_ge(s_norm2_t, t - 1)
                sp.dma_start(xt[:, par, :], x[ds(t * P, P), :]).then_inc(s_tile[par], 16)
                sp.dma_start(xnt[:, par, :], XT[ds(t * P, P), :]).then_inc(s_tile[par], 16)

            sp.wait_ge(s_tab, 1)
            load_window(0, 0)
            load_window(1, 1)
            sp.wait_ge(s_kx, TILES)
            sp.dma_start(bo_b, bo.broadcast_to((P, C))).then_inc(s_bo, 16)
            sp.wait_ge(s_xst[0], 32 * 7)
            sp.wait_ge(s_xst[1], 32 * 6)
            load_tile(0, 0)
            load_tile(1, 1)

            def store_gates(t, n):
                sp.wait_ge(s_gates_t, n)
                sp.sem_inc(s_sp, 1)
                sp.dma_start(GT[:, ds(t * P, P)], gts[:, :]).then_inc(s_gst, 16)

            def load_gate(b, i, cols):
                slot = i % GSLOTS
                to = gate[:, slot * NB:slot * NB + cols]
                if i < EXP:
                    sp.dma_start(to, GT[i:i + 1, ds(first_node(b), cols)].broadcast_to((P, cols))).then_inc(s_gld[slot], 16)
                    return
                for r0, r1, e in segments(HT_FULL + i - EXP):
                    sp.dma_start(to[r0:r1, :], GT[e:e + 1, ds(first_node(b), cols)].broadcast_to((r1 - r0, cols)))\
                        .then_inc(s_gld[slot], 16)

            load_window(2, 0)
            store_gates(0, 1)
            sp.wait_ge(s_gst, 16)
            sp.wait_ge(s_wlo, 3 * SPLITS)
            for i in range(GSLOTS):
                load_gate(0, i, P)

            def ffn_block(b, windows, tiles, cols, nxt):
                for j in range(HT):
                    q = j // POST
                    if j % POST == 1:
                        if q in windows:
                            load_window(BT * b + 3 + q, (q + 1) % 2)
                        if q in tiles and not (isinstance(b, int) and BT * b + 2 + q >= TILES):
                            load_tile(BT * b + 2 + q, q % 2)
                    if j and j % FULL == 0:
                        sp.wait_ge(s_t, HT * b + j)
                        sp.sem_inc(s_sp, 1)
                        load_gate(b, j // FULL - 1 + GSLOTS, cols)
                    if j and j % POST == 0 and q - 1 in tiles:
                        store_gates(BT * b + q, BT * b + 1 + q)
                if nxt:
                    sp.wait_ge(s_gst, 16 * (BT * b + BT + 1))
                    sp.sem_inc(s_sp, 1)
                    sp.wait_ge(s_t, HT * b + HT)
                    sp.sem_inc(s_sp, 1)
                    for i in range(GSLOTS):
                        load_gate(b + 1, i, nxt)
                for k in range(KC):
                    n = min(cols, NODES - first_node(b)) if isinstance(b, int) else cols
                    sp.wait_ge(s_y, KC * b + k + 2)
                    sp.dma_start(outT[k * P:(k + 1) * P, ds(first_node(b), n)], x1a[:, k * NB:k * NB + n]).then_inc(s_out, 16)

            ffn_block(0, range(BT), range(BT), P, NB)
            with sp.Fori(1, BLOCKS - 1) as b:
                ffn_block(b, range(BT), range(BT), NB, NB)
            ffn_block(BLOCKS - 1, range(BT - 2), range(BT), NB, NB)
            ffn_block(BLOCKS, (), (), NB, 0)
            sp.wait_ge(s_out, 16 * KC * (BLOCKS + 1) + 1)

        @block.gpsimd
        def _(pool):
            pool.iota(lane[:, :], [[1, P]], base=0, channel_multiplier=0, allow_small_or_imprecise_dtypes=True)\
                .then_inc(s_const, 1)
            pool.iota(lane8[:, :], [[1, EXP]], base=0, channel_multiplier=0, allow_small_or_imprecise_dtypes=True)\
                .then_inc(s_const, 1)
            pool.iota(base[:, :], [[P, TILES]], base=0, channel_multiplier=0, allow_small_or_imprecise_dtypes=True)\
                .then_inc(s_const, 1)
            pool.iota(kidx, [[1, EJ]], base=0, channel_multiplier=EJ, allow_small_or_imprecise_dtypes=True)\
                .then_inc(s_const, 1)
            pool.memset(one[:, :], 1.0).then_inc(s_const, 1)
            pool.memset(gts[:, :], 1.0).then_inc(s_const, 1)
            pool.memset(xrow[:, 2 * C:2 * C + 2], 1.0).then_inc(s_const, 1)
            pool.memset(ident[:, :], 0.0).then_inc(s_ident, 1)
            pool.wait_ge(s_ident, 1)
            pool.affine_select(out=ident[:, :], in_=ident[:, :], compare_op=ALU.not_equal, fill=1.0,
                               base=0, pattern=[[-1, P]], channel_multiplier=1).then_inc(s_ident, 1)
            def load_weights(c):
                if c >= 4:
                    pool.wait_ge(s_wm, c - 3)
                if c == 2 * LOADS:
                    pool.wait_ge(s_tab, 1)
                n, k = divmod(c, LOADS)
                pool.dma_start(load_piece(c), wT[n, :, k * LCOL:(k + 1) * LCOL]).then_inc(s_w[c % 4], 16)

            for c in range(8):
                load_weights(c)
            pool.wait_ge(s_rloc, 1)
            pool.partition_all_reduce(rall, rloc, P, RMAX).then_inc(s_rall, 1)

            def gather_group(t, i, par):
                pool.wait_ge(s_used, GROUPS * t + i + 1)
                pool.sem_inc(s_pool, 1)
                g = i % RG
                for m in range(group_size(i)):
                    e = WG * i + m
                    pool.indirect_dma_start(rows[:, g * WG + m, 0:2 * C], None, XH,
                                            bass.IndirectOffsetOnAxis(ap=srcw[:, par, e:e + 1], axis=0))\
                        .then_inc(s_row[g], 16)

            def gather_extra(t):
                first = pool.value_load(tab[0:1, 0, ds(t, 1)], min_val=0, max_val=ET - 1)
                n = pool.value_load(tab[0:1, 1, ds(t, 1)], min_val=0, max_val=ET)
                done = pool.value_load(tab[0:1, 2, ds(t, 1)], min_val=0, max_val=ET * TILES)
                with pool.If(n > 0):
                    with pool.Fori(0, n) as i:
                        pool.wait_ge(s_xd, done + i + 1)
                        col = nc.s_assert_within(first + i + W, 0, ETW - 1,
                                                 skip_runtime_bounds_check_because="the table's counts end at the last edge tile")
                        pool.dma_start(xsrc[:, :], srcT[:, ds(col, 1)], allow_slow_non_contiguous=True).then_inc(s_xi, 16)
                        pool.dma_start(xdst[:, :], dstT[:, ds(col, 1)], allow_slow_non_contiguous=True).then_inc(s_xi, 16)
                        pool.wait_ge(s_xi, (done + i) * 32 + 32)
                        pool.sem_inc(s_xs, 1)
                        pool.indirect_dma_start(xrow[:, 0:2 * C], None, XH,
                                                bass.IndirectOffsetOnAxis(ap=xsrc[:, 0:1], axis=0)).then_inc(s_xr, 16)

            def gather_tile(t, par, use):
                pool.wait_ge(s_win[par], 32 * use)
                gather_group(t, 0, par)
                gather_extra(t)
                for i in range(1, GROUPS):
                    gather_group(t, i, par)

            for c in range(8, 3 * LOADS):
                load_weights(c)
            pool.wait_ge(s_nloc, 1)
            pool.partition_all_reduce(sc[:, 4:7], sc[:, 0:3], P, RMAX).then_inc(s_nall, 1)
            pool.wait_ge(s_xst[0], 32 * 7)
            pool.wait_ge(s_xst[1], 32 * 6)
            pool.wait_ge(s_kx, TILES)
            pool.memset(rows[:, :, 2 * C:2 * C + 2], 1.0).then_inc(s_const, 1)
            pool.wait_ge(s_const, 8)
            with pool.Fori(0, TILES // 2) as i:
                for par in range(2):
                    gather_tile(2 * i + par, par, i + 1)
            gather_tile(TILES - 1, 0, TILES // 2 + 1)

        @block.scalar
        def _(act):
            def step(s, k, sizes):
                if n := sizes[0]:
                    h = k % 2
                    act.wait_ge(s_lnr, s + 1)
                    for i in range(n):
                        last = act.activation(xin[k][:, i, :], xin[k][:, i, :], ACT.Identity,
                                              scale=sc[:, 16 + 8 * h + i:17 + 8 * h + i],
                                              bias=sc[:, 20 + 8 * h + i:21 + 8 * h + i])
                    last.then_inc(s_lnx, 1)
                    if not (isinstance(s, int) and s < 2):
                        act.wait_ge(s_xst[h], 32 * (s // 2) if isinstance(s, int) else 16 * (s - k % 2))
                    act.wait_ge(s_lnx, s + 1)
                    act.activation(xhb[h][:, 0:n, 0:C], xin[k][:, 0:n, :], ACT.Copy, scale=XS).then_inc(s_lnh, 1)
                if n := sizes[-2]:
                    for i, tiles in pairs(n):
                        act.wait_ge(s_k2n, 2 * (s - 2) + i + 1)
                        if not (isinstance(s, int) and s < 3):
                            act.wait_ge(s_kx, BT * (s - 3) + 2 * i + 2)
                        for m in tiles:
                            last = act.activation(key4[m], key2[BT * (k % 2) + m], ACT.Square)
                        last.then_inc(s_k4, 1)
                if n := sizes[0]:
                    act.wait_ge(s_lnt, s + 1)
                    if not (isinstance(s, int) and s < 2):
                        act.wait_ge(s_kp, 2 * (s - 2) + 2)
                    for i, tiles in pairs(n):
                        m = len(tiles)
                        last = act.activation(xtb[h][:, 2 * i:2 * i + m, :].rearrange("p t c -> p (t c)"),
                                              bank[2 + 2 * h + i][:, 0:m * C], ACT.Copy)
                    last.then_inc(s_lnc, 1)
                if n := sizes[-1]:
                    o = BT * ((k - 1) % 2)
                    for i, tiles in pairs(n):
                        act.wait_ge(s_kp, 2 * (s - 1) + i + 1)
                        if not (isinstance(s, int) and s < 3):
                            act.wait_ge(s_kx, BT * (s - 3) + 2 * i + 2)
                        for m in tiles:
                            last = act.activation(key2[o + m], bank[6 + i][:, (m % 2) * C:(m % 2) * C + C], ACT.Square,
                                                  accum_out=sc[:, 80 + o + m:81 + o + m])
                        last.then_inc(s_k2, 1)

            first_pass(act, step)
            act.wait_ge(s_wvo, 1)
            act.activation(wvo[:, :, :].rearrange("p k c -> p (k c)"), bank[2][:, :], ACT.Copy).then_inc(s_wvc, 1)

            def split_high(c):
                whole, high, _, aside = split_chunk(c)
                if c > 1 and c % 2 == 0:
                    act.wait_ge(s_wlo, c - 1)
                n = c // SPLITS
                if c % 2:
                    act.wait_ge(s_stgd, c // 2 + 1)
                else:
                    act.activation(aside, whole, ACT.Copy, scale=cst[:, n:n + 1]).then_inc(s_stg, 1)
                    act.wait_ge(s_stg, c // 2 + 1)
                act.activation(high, aside.rearrange("p (u c) -> p u c", c=P), ACT.Copy).then_inc(s_whi, 1)

            def update(t, q, stage_):
                if stage_ == "A":
                    act.wait_ge(s_query, t + 1)
                    act.activation(tmp[:, 1, :], tmp[:, 1, :], ACT.Square, accum_out=sc[:, 0:1])
                    act.drain()
                    act.activation(tmp[:, 2, :], tmp[:, 1, :], ACT.Square, accum_out=sc[:, 1:2]).then_inc(s_query_norm, 1)
                if stage_ == "C":
                    act.wait_ge(s_graph, t + 1)
                    act.activation(tmp[:, 1, :], tmp[:, 1, :], ACT.Relu)
                    act.drain()
                    act.activation(tmp[:, 2, :], tmp[:, 1, :], ACT.Square, accum_out=sc[:, 2:3]).then_inc(s_graph_norm, 1)
                if stage_ == "F":
                    act.wait_ge(s_ffn_in, t + 1)
                    act.activation(x2s[:, 0:KC, q * P:(q + 1) * P],
                                   tmp[:, 0, :].rearrange("p (k n) -> p k n", k=KC), ACT.Copy).then_inc(s_ffn_high, 1)
                if stage_ == "G":
                    act.wait_ge(s_logits_less, t + 1)
                    act.activation(sc[:, 72:80], sc[:, 64:72], ACT.Tanh, scale=1.0 / 16.0).then_inc(s_tanh, 1)

            act.wait_ge(s_cst, 1)
            for p in range(-1, 1):
                for k in range(POST + 1):
                    for c in splits_at(p, k):
                        split_high(c)
                    if p >= 0 and k in STAGES:
                        update(p, p, STAGES[k])

            def ffn_block(b, tiles, cols):
                for j in range(HT):
                    act.wait_ge(s_u, HT * b + max(j - 1, 0) + 1)
                    act.wait_ge(s_h1, HT * b + j + 1)
                    act.activation(sig[:, (j % 2) * NB:(j % 2) * NB + cols], H1[j % 2][:, 0:cols], ACT.Silu,
                                   scale=cst[:, 3:4]).then_inc(s_sig, 1)
                    act.wait_ge(s_f2, HT * b + max(j - 2, 0) + 1)
                    act.wait_ge(s_t, HT * b + j + 1)
                    act.activation(hh[:, 2 * (j % 3), 0:cols], hid[:, (j % 2) * NB:(j % 2) * NB + cols], ACT.Copy)\
                        .then_inc(s_hi, 1)
                    if j == 3:
                        act.wait_ge(s_out, 16 * KC * b + 1)
                        act.activation(x1a[:, :], x1s[:, :], ACT.Copy).then_inc(s_x1, 1)
                    for q, s in stages_at(j, tiles):
                        update(BT * b + 1 + q, q, s)

            ffn_block(0, range(BT), P)
            with act.Fori(1, BLOCKS - 1) as b:
                ffn_block(b, range(BT), NB)
            ffn_block(BLOCKS - 1, range(BT), NB)
            ffn_block(BLOCKS, (), NB)

        @block.tensor
        def _(pe):
            pe.sem_inc(s_used, RG)
            for free in (s_xd, s_nei, s_y, s_u, s_f2, s_out):
                pe.sem_inc(free, 1)

            def open_sum(bank_):
                pe.matmul(bank_[:, :], hot[:, 0, 0, :], hot[:, 0, :, :].rearrange("p a n -> p (a n)"),
                          start=True, stop=False, skip_group_check=True)

            def sum_group(t, i, turn=None):
                g = i % RG
                if i == 0:
                    pe.wait_ge(s_nei, t + 1)
                pe.wait_ge(s_row[g], rows_count(t, i))
                pe.wait_ge(s_hot, GROUPS * t + i + 1)
                size = group_size(i)
                for m in range(size):
                    r = rows[:, g * WG + m, :]
                    pe.matmul(AG[:, 0:C], hot[:, g, m, :], r[:, 0:C], start=(i == 0 and m == 0), stop=False,
                              skip_group_check=True)
                    last = pe.matmul(AG[:, 0:C + 1], hot[:, g, m, :], r[:, C:2 * C + 1], start=False,
                                     stop=(i == GROUPS - 1 and m == size - 1), skip_group_check=True)
                last.then_inc(s_used, 1)
                if i == 0:
                    n = pe.value_load(tab[0:1, 1, ds(t, 1)], min_val=0, max_val=ET)
                    done = pe.value_load(tab[0:1, 2, ds(t, 1)], min_val=0, max_val=ET * TILES)
                    with pe.If(n > 0):
                        with pe.Fori(0, n) as k:
                            pe.wait_ge(s_xr, (done + k) * 16 + 16)
                            pe.wait_ge(s_xh, done + k + 1)
                            pe.matmul(AG[:, 0:C], xhot[:, :], xrow[:, 0:C], start=False, stop=False,
                                      skip_group_check=True)
                            pe.matmul(AG[:, 0:C + 1], xhot[:, :], xrow[:, C:2 * C + 1], start=False, stop=False,
                                      skip_group_check=True).then_inc(s_xd, 1)
                if i == GROUPS - 1:
                    pe.drain().then_inc(s_agg, 1)

            def step(s, k, sizes):
                if n := sizes[0]:
                    h = k % 2
                    if not (isinstance(s, int) and s < 2):
                        pe.wait_ge(s_lnc, s - 1)
                    pe.wait_ge(s_lnx, s + 1)
                    for i in range(n):
                        for c in range(KC):
                            o = (i % 2) * C + c * P
                            last = pe.transpose(bank[2 + 2 * h + i // 2][:, o:o + P],
                                                xin[k][:, i, c * P:(c + 1) * P], ident[:, :])
                    last.then_inc(s_lnt, 1)
                if n := sizes[-1]:
                    pe.wait_ge(s_lnc, s)
                    for i, tiles in pairs(n):
                        if not (isinstance(s, int) and s < 2):
                            pe.wait_ge(s_k2, 2 * (s - 2) + i + 1)
                        for m in tiles:
                            o = bank[6 + i][:, (m % 2) * C:(m % 2) * C + C]
                            for c in range(KC):
                                pe.matmul(o, xtb[(k - 1) % 2][:, m, c * P:(c + 1) * P], wk_s[:, c, :],
                                          start=(c == 0), stop=False)
                            last = pe.matmul(o, gts[0:1, :], bk_b[0:1, :], start=False, stop=True)
                        last.then_inc(s_kp, 1)
                if n := sizes[-2]:
                    for i, tiles in pairs(n):
                        pe.wait_ge(s_k4, 2 * (s - 2) + i + 1)
                        for m in tiles:
                            rows_ = P if n == BT else LAST
                            k2, k4 = key2[BT * (k % 2) + m], key4[m]
                            for c in range(KC):
                                pe.matmul(Y[0][:, c * C:(c + 1) * C], xin[(k - 2) % BT][0:rows_, m, c * P:(c + 1) * P],
                                          k2[0:rows_, :], start=False, stop=False, skip_group_check=True)
                            for a, kk in enumerate((k2, k4)):
                                for c in range(KC):
                                    last = pe.matmul(Y[1][:, 2 * a + c:2 * a + c + 1], kk[0:rows_, c * P:(c + 1) * P],
                                                     one[0:rows_, :], start=False, stop=False, skip_group_check=True)
                            last.then_inc(s_kx, 1)

            pe.wait_ge(s_ident, 2)
            pe.wait_ge(s_const, 7)
            pe.wait_ge(s_zero, 1)
            open_sum(Y[0])
            open_sum(Y[1])
            pe.drain().then_inc(s_zero, 1)
            pe.wait_ge(s_ck, 1)
            first_pass(pe, step)
            pe.wait_ge(s_cent, 1)
            pe.wait_ge(s_lnc, NODE_GROUPS)
            pe.wait_ge(s_k2, 2 * NODE_GROUPS - 1)
            for k in range(KC):
                for d in range(KC):
                    pe.matmul(bank[2][:, k * C:(k + 1) * C], wvt_s[:, d, k * P:(k + 1) * P], wo_s[:, d, :],
                              start=(d == 0), stop=(d == KC - 1))
            for d in range(KC):
                last = pe.matmul(bank[3][:, 0:C], bvr[:, d, :], wo_s[:, d, :], start=(d == 0), stop=(d == KC - 1))
            last.then_inc(s_wvo, 1)
            pe.wait_ge(s_wvc, 1)
            pe.wait_ge(s_kxs, 1)
            for k in range(KC):
                for d in range(KC):
                    last = pe.matmul(bank[4][:, k * C:(k + 1) * C], kxs[:, d, k * P:(k + 1) * P], wvo[:, d, :],
                                     start=(d == 0), stop=(d == KC - 1))
            last.then_inc(s_mp, 1)

            def update(t, par, stage_):
                if stage_ == "A":
                    pe.wait_ge(s_nei, t + 2)
                    if some(t):
                        pe.wait_ge(s_gates_t, t)
                    for c in range(KC):
                        pe.transpose(PB[:, c * P:(c + 1) * P], neigh[:, par, c * P:(c + 1) * P], ident[:, :])
                    pe.wait_ge(s_tile[par], 16 * (t - par) + 32)
                    for c in range(KC):
                        last = pe.matmul(PB[:, C:2 * C], xnt[:, par, c * P:(c + 1) * P], wq_s[:, c, :],
                                         start=(c == 0), stop=(c == KC - 1))
                    last.then_inc(s_query_psum, 1)
                if stage_ == "C":
                    pe.wait_ge(s_query_unit, t + 1)
                    for c in range(KC):
                        pe.transpose(PB[:, c * P:(c + 1) * P], tmp[:, 3, c * P:(c + 1) * P], ident[:, :])
                    for c in range(2 * KC):
                        lhs = xnt[:, par, c * P:(c + 1) * P] if c < KC else tmp[:, 0, (c - KC) * P:(c - KC + 1) * P]
                        last = pe.matmul(PB[:, C:2 * C], lhs, wg_s[:, c, :], start=(c == 0), stop=(c == 2 * KC - 1))
                    last.then_inc(s_graph_psum, 1)
                if stage_ == "D":
                    pe.wait_ge(s_graph, t + 1)
                    for c in range(2 * KC):
                        lhs = xnt[:, par, c * P:(c + 1) * P] if c < KC else tmp[:, 4, (c - KC) * P:(c - KC + 1) * P]
                        last = pe.matmul(PB[:, 0:C], lhs, (wvo if c < KC else mix)[:, c % KC, :],
                                         start=(c == 0), stop=(c == 2 * KC - 1))
                    last.then_inc(s_attn_psum, 1)
                if stage_ == "F":
                    pe.wait_ge(s_norm2, t + 1)
                    for c in range(KC):
                        pe.transpose(PB[:, c * P:(c + 1) * P], xt[:, par, c * P:(c + 1) * P], ident[:, :])
                        last = pe.transpose(PB[:, C + c * P:C + (c + 1) * P], tmp[:, 3, c * P:(c + 1) * P], ident[:, :])
                    last.then_inc(s_norm2_t, 1)
                if stage_ == "G":
                    pe.wait_ge(s_ffn_in, t + 1)
                    for c in range(KC):
                        last = pe.matmul(PB[:, 0:EXP], tmp[:, 0, c * P:(c + 1) * P], rw_s[:, c, :],
                                         start=(c == 0), stop=(c == KC - 1))
                    last.then_inc(s_logits, 1)
                if stage_ == "I":
                    pe.wait_ge(s_gates, t + 1)
                    pe.transpose(PB[0:EXP, 0:P], sc[:, 56:64], ident[:, :]).then_inc(s_gates_psum, 1)

            for k in range(GROUPS):
                sum_group(0, k)
            pe.wait_ge(s_mix, 1)
            for k in range(POST + 1):
                if k < GROUPS:
                    sum_group(1, k)
                if k in STAGES:
                    update(0, 0, STAGES[k])

            def second(b, j, cols):
                pe.wait_ge(s_lo, HT * b + j + 1)
                if j == 0:
                    pe.wait_ge(s_y, KC * b + 1)
                hi, lo = hh[:, 2 * (j % 3), 0:cols], hh[:, 2 * (j % 3) + 1, 0:cols]
                for c in range(KC):
                    whi, wlo = unit(2, KC * j + c)
                    o = Y[c][:, 0:cols]
                    pe.matmul(o, whi, hi, start=(j == 0), stop=False)
                    pe.matmul(o, whi, lo, start=False, stop=False)
                    last = pe.matmul(o, wlo, hi, start=False, stop=(j == HT - 1))
                last.then_inc(s_f2, 1)

            def ffn_block(b, summed, tiles, cols):
                pe.wait_ge(s_x2, b + 1)
                for j in range(HT):
                    pe.wait_ge(s_u, HT * b + max(j - 1, 0) + 1)
                    for n, (H, done) in enumerate(((H1, s_h1), (H3, s_h3))):
                        o = H[j % 2][:, 0:cols]
                        for c in range(KC):
                            whi, wlo = unit(n, HT * c + j)
                            xhi, xlo = x2a[:, c, 0:cols], x2a[:, KC + c, 0:cols]
                            pe.matmul(o, whi, xhi, start=(c == 0), stop=False)
                            pe.matmul(o, whi, xlo, start=False, stop=False)
                            last = pe.matmul(o, wlo, xhi, start=False, stop=(c == KC - 1))
                        last.then_inc(done, 1)
                    if j >= 2:
                        second(b, j - 2, cols)
                    for q, i in GROUP_AT[j]:
                        if q in summed:
                            sum_group(BT * b + 2 + q, i)
                    for q, s in stages_at(j, tiles):
                        update(BT * b + 1 + q, (q + 1) % 2, s)
                second(b, HT - 2, cols)
                second(b, HT - 1, cols)

            pe.wait_ge(s_wlo, 3 * SPLITS)
            ffn_block(0, range(BT), range(BT), P)
            with pe.Fori(1, BLOCKS - 1) as b:
                ffn_block(b, range(BT), range(BT), NB)
            ffn_block(BLOCKS - 1, range(BT - 1), range(BT), NB)
            ffn_block(BLOCKS, (), (), NB)

        @block.vector
        def _(dve):
            def link(_=None):
                dve.drain()

            def rsqrt(y, v, t):
                link()
                dve.tensor_scalar(y.bitcast(I32), v.bitcast(I32), -0.5, RSQRT_MAGIC, ALU.mult, ALU.add)
                for _ in range(3):
                    link()
                    dve.tensor_tensor(t, y, y, ALU.mult)
                    link()
                    dve.tensor_tensor(t, t, v, ALU.mult)
                    link()
                    dve.tensor_scalar(t, t, -0.5, 1.5, ALU.mult, ALU.add)
                    link()
                    dve.tensor_tensor(y, y, t, ALU.mult)
                link()

            def rsqrt8(y, v, t, w):
                link()
                dve.tensor_scalar(y.bitcast(I32), v.bitcast(I32), -0.5, RSQRT_MAGIC, ALU.mult, ALU.add)
                for i in range(2):
                    dve.tensor_scalar(w[:, i:i + 1], v, 0.25 ** (i + 1), None, ALU.mult)
                for scaled in (v, w[:, 0:1], w[:, 1:2]):
                    link()
                    dve.tensor_scalar(t, y, scaled, y, ALU.mult, ALU.mult)
                    link()
                    dve.tensor_scalar(y, t, 3.0, y, ALU.subtract, ALU.mult)
                link()

            dve.memset(hot[:, :, :, :], 0.0).then_inc(s_zero, 1)
            dve.memset(tab[:, :, :], 0)
            dve.wait_ge(s_const, 7)

            def ranges():
                dve.wait_ge(s_rng, 16)
                dve.tensor_reduce(dmin, drow, AX.X, ALU.min)
                dve.tensor_reduce(dmax, drow, AX.X, ALU.max)
                link()
                by_tile = (P, TILES, EJ)
                thr = base[:, :, None].broadcast_to(by_tile)
                kk = kidx[:, None, :].broadcast_to(by_tile)
                dve.tensor_tensor(ra, dmax[:, None, :].broadcast_to(by_tile), thr, ALU.subtract)
                link()
                dve.tensor_scalar(rb, ra, 0.0, 1.0e6, ALU.is_lt, ALU.mult)
                link()
                dve.tensor_tensor(ra, rb, kk, ALU.add)
                link()
                dve.tensor_reduce(rall[:, 0:TILES], ra, AX.X, ALU.min)
                link()
                dve.tensor_scalar(rloc[:, 0:TILES], rall[:, 0:TILES], -1.0, None, ALU.mult)
                dve.tensor_tensor(ra, dmin[:, None, :].broadcast_to(by_tile), thr, ALU.subtract)
                link()
                dve.tensor_scalar(rb, ra, float(P), None, ALU.is_lt)
                link()
                dve.tensor_tensor(ra, rb, kk, ALU.mult)
                link()
                dve.tensor_tensor(ra, ra, rb, ALU.add)
                link()
                dve.tensor_reduce(rloc[:, TILES:2 * TILES], ra, AX.X, ALU.max)
                dve.drain().then_inc(s_rloc, 1)

            def node_scales(g, k, n):
                h = k % 2
                dve.wait_ge(s_x[k], 16 * (g // BT) + 16 if isinstance(g, int) else BT * (g - k) + 16)
                if not (isinstance(g, int) and g < 2):
                    dve.wait_ge(s_lnx, g - 1)
                st = sc[:, 40:64].rearrange("p (t s) -> p t s", s=6)
                mv = sc[:, 64:72].rearrange("p (t s) -> p t s", s=2)
                for m in range(n):
                    dve.bn_stats(st[:, m, :], xin[k][:, m, :])
                link()
                for m in range(n):
                    dve.bn_aggr(mv[:, m, :], st[:, m, :])
                link()
                v, t = sc[:, 72:72 + n], sc[:, 76:76 + n]
                y, sh = sc[:, 16 + 8 * h:16 + 8 * h + n], sc[:, 20 + 8 * h:20 + 8 * h + n]
                dve.tensor_scalar(v, mv[:, 0:n, 1], EPS_LN, None, ALU.add)
                rsqrt(y, v, t)
                dve.tensor_tensor(t, mv[:, 0:n, 0], y, ALU.mult)
                link()
                dve.tensor_scalar(sh, t, -1.0, None, ALU.mult).then_inc(s_lnr, 1)

            def node_low(g, k, n):
                dve.wait_ge(s_lnh, g + 1)
                dve.scalar_tensor_tensor(out=xhb[k % 2][:, 0:n, C:2 * C], in0=xin[k][:, 0:n, :], scalar=XS,
                                         in1=xhb[k % 2][:, 0:n, 0:C], op0=ALU.mult, op1=ALU.subtract).then_inc(s_lnl, 1)

            def key_divide(g, k, n):
                o = BT * (k % 2)
                for i, tiles in pairs(n):
                    dve.wait_ge(s_k2, 2 * g + i + 1)
                    a, b_ = tiles[0], tiles[-1] + 1
                    dve.tensor_scalar(sc[:, 0 + a:0 + b_], sc[:, 80 + o + a:80 + o + b_], EPS_DIV, None, ALU.add)
                    link()
                    dve.reciprocal(sc[:, 4 + a:4 + b_], sc[:, 0 + a:0 + b_])
                    link()
                    for m in tiles:
                        last = dve.tensor_scalar(key2[o + m], key2[o + m], sc[:, 4 + m:5 + m], None, ALU.mult)
                    last.then_inc(s_k2n, 1)

            def greatest(c, m):
                dve.wait_ge(s_w[m], 16 * (c // 4) + 16 if isinstance(c, int) else 4 * (c - m) + 16)
                dve.tensor_reduce(wmx[:, ds(c, 1)], wflat[:, ds(c * LCOL, LCOL)], AX.X, ALU.max, apply_absolute_value=True).then_inc(s_wm, 1)

            def centre(weights, cols):
                for i, wgt in enumerate(weights):
                    dve.tensor_reduce(cols[:, i:i + 1], wgt, AX.X, ALU.add)
                link()
                dve.tensor_scalar(cols[:, 3:6], cols[:, 0:3], 1.0 / C, None, ALU.mult)
                link()
                for i, wgt in enumerate(weights):
                    dve.tensor_scalar(wgt, wgt, cols[:, 3 + i:4 + i], None, ALU.subtract)

            def range_table():
                dve.wait_ge(s_rall, 1)
                dve.tensor_scalar(rall[:, 0:TILES], rall[:, 0:TILES], -1.0, float(ET - 1), ALU.mult, ALU.min)
                link()
                dve.tensor_copy(tab[:, 0, 0:TILES], rall[:, 0:TILES])
                dve.tensor_tensor(run[0], rall[:, TILES:2 * TILES], rall[:, 0:TILES], ALU.subtract)
                link()
                dve.tensor_scalar(run[0], run[0], -float(W), 0.0, ALU.add, ALU.max)
                link()
                dve.tensor_copy(tab[:, 1, 0:TILES], run[0])
                dve.tensor_copy(rall[:, 0:TILES], run[0])
                a, b_ = run
                for step in (1, 2, 4, 8, 16, 32):
                    link()
                    dve.tensor_copy(b_[:, 0:step], a[:, 0:step])
                    dve.tensor_tensor(b_[:, step:TILES], a[:, step:TILES], a[:, 0:TILES - step], ALU.add)
                    a, b_ = b_, a
                link()
                dve.tensor_tensor(a, a, rall[:, 0:TILES], ALU.subtract)
                link()
                dve.tensor_copy(tab[:, 2, 0:TILES], a)
                dve.drain().then_inc(s_tab, 1)

            def step(s, k, sizes):
                loads = not isinstance(s, int) or 2 * s < 3 * LOADS
                if loads:
                    greatest(2 * s, 2 * k % 4)
                if sizes[-2]:
                    key_divide(s - 2, k, sizes[-2])
                if loads:
                    greatest(2 * s + 1, (2 * k + 1) % 4)
                if sizes[0]:
                    node_low(s, k, sizes[0])
                if sizes[1]:
                    node_scales(s + 1, (k + 1) % BT, sizes[1])
                if isinstance(s, int) and s == 1:
                    ranges()
                if isinstance(s, int) and s == 2:
                    range_table()

            node_scales(0, 0, BT)
            dve.wait_ge(s_wk, 32)
            centre((wk_s[:, 0, :], wk_s[:, 1, :], bk_b[:, :]), sc[:, 88:94])
            dve.drain().then_inc(s_ck, 1)
            first_pass(dve, step)

            dve.wait_ge(s_wld, 16 * 9)
            centre((wq_s[:, 0, :], wq_s[:, 1, :], bq_b[:, :]), sc[:, 88:94])
            for k in range(KC):
                dve.tensor_scalar(bvr[:, k, :], ident[:, :], 0.0, bv_s[:, k:k + 1], ALU.mult, ALU.add)
            dve.drain().then_inc(s_cent, 1)

            dve.tensor_reduce(sc[:, 0:3], wmx[:, :].rearrange("p (n t) -> p n t", n=3), AX.X, ALU.max)
            dve.drain().then_inc(s_nloc, 1)

            def weight_scales():
                dve.wait_ge(s_nall, 1)
                dve.tensor_scalar(sc[:, 8:11], sc[:, 4:7], TINY, None, ALU.max)
                link()
                p = sc[:, 12:15]
                dve.tensor_scalar(p.bitcast(I32), sc[:, 8:11].bitcast(I32), 0x7F800000, None, ALU.bitwise_and)
                link()
                dve.tensor_scalar(cst[:, 0:3].bitcast(I32), p.bitcast(I32), -1.0, float((127 + 127 + 13) << 23),
                                  ALU.mult, ALU.add)
                dve.tensor_scalar(cst[:, 3:4], p[:, 0:1], 2.0 ** -23, None, ALU.mult)
                dve.tensor_tensor(cst[:, 5:6], p[:, 0:1], p[:, 1:2], ALU.mult)
                link()
                dve.tensor_scalar(cst[:, 4:5], cst[:, 0:1], 2.0 ** -39, None, ALU.mult)
                dve.tensor_scalar(cst[:, 5:6], cst[:, 5:6], p[:, 2:3], 2.0 ** -10, ALU.mult, ALU.mult)
                dve.drain().then_inc(s_cst, 1)

            def window(t, par):
                dve.wait_ge(s_win[par], 16 * (t - par) + 32)
                dve.tensor_scalar(dstf[:, par, :], dstw[:, par, :], base[:, ds(t, 1)], None, ALU.subtract)
                link()

            def one_hots(t, i, par):
                dve.wait_ge(s_used, GROUPS * t + i + 1)
                n = group_size(i)
                dve.tensor_tensor(hot[:, i % RG, 0:n, :], lane[:, None, :].broadcast_to((P, n, P)),
                                  dstf[:, par, WG * i:WG * i + n, None].broadcast_to((P, n, P)), ALU.is_equal)\
                    .then_inc(s_hot, 1)

            def one_hots_extra(t):
                n = dve.value_load(tab[0:1, 1, ds(t, 1)], min_val=0, max_val=ET)
                done = dve.value_load(tab[0:1, 2, ds(t, 1)], min_val=0, max_val=ET * TILES)
                with dve.If(n > 0):
                    with dve.Fori(0, n) as k:
                        dve.wait_ge(s_xs, done + k + 1)
                        dve.wait_ge(s_xd, done + k + 1)
                        dve.tensor_scalar(xdf[:, :], xdst[:, :], base[:, ds(t, 1)], None, ALU.subtract)
                        dve.drain()
                        dve.tensor_scalar(xhot[:, :], lane[:, :], xdf[:, 0:1], None, ALU.is_equal).then_inc(s_xh, 1)

            def neighbours(t, par):
                dve.wait_ge(s_agg, t + 1)
                dve.tensor_scalar(sc[:, 34:35], AG[:, C:C + 1], 1.0, None, ALU.max)
                link()
                dve.reciprocal(sc[:, 35:36], sc[:, 34:35])
                link()
                dve.tensor_scalar(neigh[:, par, :], AG[:, 0:C], sc[:, 35:36], 1.0 / XS, ALU.mult, ALU.mult)\
                    .then_inc(s_nei, 1)

            weight_scales()

            dve.wait_ge(s_kx, TILES)
            dve.tensor_copy(kxs.rearrange("p k c -> p (k c)"), Y[0][:, :]).then_inc(s_kxs, 1)
            dve.tensor_copy(sc[:, 0:4], Y[1][:, 0:4])
            link()
            dve.tensor_scalar(sc[:, 4:6], sc[:, 2:4], TINY, None, ALU.max)
            rsqrt(sc[:, 8:10], sc[:, 4:6], sc[:, 12:14])
            dve.tensor_tensor(sc[:, 4:6], sc[:, 4:6], sc[:, 8:10], ALU.mult)
            link()
            dve.tensor_scalar(sc[:, 4:6], sc[:, 4:6], EPS_NORM, None, ALU.max)
            link()
            dve.reciprocal(sc[:, 8:10], sc[:, 4:6])
            dve.wait_ge(s_wvo, 1)
            dve.wait_ge(s_bo, 16)
            dve.tensor_copy(sbv, bank[3][:, 0:C])
            link()
            dve.tensor_tensor(co_b[:, :], sbv, bo_b, ALU.add)
            dve.wait_ge(s_mp, 1)
            for k in range(KC):
                dve.scalar_tensor_tensor(out=mix[:, k, :], in0=sbv, scalar=sc[:, k:k + 1],
                                         in1=bank[4][:, k * C:(k + 1) * C], op0=ALU.mult, op1=ALU.add)
            link()
            for k in range(KC):
                last = dve.tensor_scalar(mix[:, k, :], mix[:, k, :], sc[:, 8 + k:9 + k], float(NODES) ** -0.5,
                                         ALU.mult, ALU.mult)
            dve.drain().then_inc(s_mix, 1)

            def update(t, q, par, stage_, b=None):
                if stage_ == "A":
                    dve.wait_ge(s_query_psum, t + 1)
                    dve.tensor_copy(tmp[:, 0, :], PB[:, 0:C])
                    dve.tensor_tensor(tmp[:, 1, :], PB[:, C:2 * C], bq_b[:, :], ALU.add)
                    dve.drain().then_inc(s_query, 1)
                if stage_ == "B":
                    dve.wait_ge(s_query_norm, t + 1)
                    dve.tensor_scalar(sc[:, 3:4], sc[:, 0:1], EPS_DIV, None, ALU.add)
                    dve.tensor_scalar(sc[:, 4:5], sc[:, 1:2], TINY, None, ALU.max)
                    link()
                    dve.reciprocal(sc[:, 5:6], sc[:, 3:4])
                    rsqrt8(sc[:, 6:7], sc[:, 4:5], sc[:, 7:8], sc[:, 36:38])
                    dve.tensor_scalar(sc[:, 7:8], sc[:, 4:5], sc[:, 6:7], -0.125, ALU.mult, ALU.mult)
                    link()
                    dve.tensor_scalar(sc[:, 6:7], sc[:, 7:8], sc[:, 5:6], EPS_NORM, ALU.mult, ALU.max)
                    link()
                    dve.reciprocal(sc[:, 7:8], sc[:, 6:7])
                    link()
                    dve.tensor_scalar(tmp[:, 3, :], tmp[:, 1, :], sc[:, 5:6], sc[:, 7:8], ALU.mult, ALU.mult)\
                        .then_inc(s_query_unit, 1)
                if stage_ == "C":
                    dve.wait_ge(s_graph_psum, t + 1)
                    dve.tensor_copy(tmp[:, 4, :], PB[:, 0:C])
                    dve.tensor_tensor(tmp[:, 1, :], PB[:, C:2 * C], bg_b[:, :], ALU.add)
                    dve.drain().then_inc(s_graph, 1)
                if stage_ == "D":
                    dve.wait_ge(s_graph_norm, t + 1)
                    dve.tensor_scalar(sc[:, 4:5], sc[:, 2:3], TINY, None, ALU.max)
                    rsqrt8(sc[:, 6:7], sc[:, 4:5], sc[:, 7:8], sc[:, 36:38])
                    dve.tensor_scalar(sc[:, 7:8], sc[:, 4:5], sc[:, 6:7], -0.125, ALU.mult, ALU.mult)
                    link()
                    dve.tensor_scalar(sc[:, 6:7], sc[:, 7:8], EPS_NORM, None, ALU.max)
                    link()
                    dve.reciprocal(sc[:, 7:8], sc[:, 6:7])
                    link()
                    dve.scalar_tensor_tensor(out=xt[:, par, :], in0=tmp[:, 1, :], scalar=sc[:, 7:8],
                                             in1=xt[:, par, :], op0=ALU.mult, op1=ALU.add)
                    link()
                    dve.tensor_tensor(xt[:, par, :], xt[:, par, :], co_b[:, :], ALU.add)
                    link()
                    dve.wait_ge(s_attn_psum, t + 1)
                    dve.tensor_tensor(xt[:, par, :], PB[:, 0:C], xt[:, par, :], ALU.add)
                    link()
                if stage_ == "E":
                    dve.bn_stats(sc[:, 8:14], xt[:, par, :])
                    link()
                    dve.bn_aggr(sc[:, 14:16], sc[:, 8:14])
                    link()
                    dve.tensor_scalar(sc[:, 4:5], sc[:, 15:16], EPS_LN, None, ALU.add)
                    rsqrt8(sc[:, 6:7], sc[:, 4:5], sc[:, 7:8], sc[:, 36:38])
                    dve.tensor_scalar(tmp[:, 3, :], xt[:, par, :], sc[:, 14:15], sc[:, 6:7],
                                      ALU.subtract, ALU.mult).then_inc(s_norm2, 1)
                if stage_ == "F":
                    dve.wait_ge(s_norm2_t, t + 1)
                    if b is not None:
                        dve.wait_ge(s_x1, b + 1)
                    dve.tensor_copy(x1s[:, :].rearrange("p (k n) -> p k n", k=KC)[:, :, q * P:(q + 1) * P],
                                    PB[:, 0:C].rearrange("p (k n) -> p k n", k=KC))
                    dve.tensor_scalar(tmp[:, 0, :], PB[:, C:2 * C], -XS / 8, None, ALU.mult)
                    dve.drain().then_inc(s_ffn_in, 1)
                if stage_ == "G":
                    dve.wait_ge(s_ffn_high, t + 1)
                    dve.tensor_tensor(x2s[:, KC:2 * KC, q * P:(q + 1) * P],
                                      tmp[:, 0, :].rearrange("p (k n) -> p k n", k=KC),
                                      x2s[:, 0:KC, q * P:(q + 1) * P], ALU.subtract)
                    dve.wait_ge(s_logits, t + 1)
                    dve.tensor_scalar(sc[:, 40:48], PB[:, 0:EXP], 1.0 / XS, None, ALU.mult)
                    link()
                    dve.max(sc[:, 48:56], sc[:, 40:48])
                    link()
                    dve.max_index(idx8[:, :], sc[:, 48:56], sc[:, 40:48])
                    dve.tensor_scalar(sc[:, 64:72], sc[:, 48:56], sc[:, 48:49], None, ALU.subtract)
                    dve.drain().then_inc(s_logits_less, 1)
                    dve.tensor_copy(sc[:, 4:6], idx8[:, 0:2])
                if stage_ == "H":
                    dve.wait_ge(s_tanh, t + 1)
                    ex, de = sc[:, 80:88], sc[:, 88:96]
                    dve.tensor_scalar(ex, sc[:, 72:80], 1.0, None, ALU.add)
                    dve.tensor_scalar(de, sc[:, 72:80], -1.0, 1.0, ALU.mult, ALU.add)
                    link()
                    dve.reciprocal(sc[:, 64:72], de)
                    link()
                    dve.tensor_tensor(ex, ex, sc[:, 64:72], ALU.mult)
                    for _ in range(3):
                        link()
                        dve.tensor_tensor(ex, ex, ex, ALU.mult)
                    link()
                    dve.tensor_reduce(sc[:, 3:4], ex, AX.X, ALU.add)
                    dve.tensor_tensor(sc[:, 6:7], ex[:, 0:1], ex[:, 1:2], ALU.add)
                    dve.tensor_scalar(sc[:, 40:48], lane8[:, :], sc[:, 4:5], ex[:, 0:1], ALU.is_equal, ALU.mult)
                    dve.tensor_scalar(sc[:, 48:56], lane8[:, :], sc[:, 5:6], ex[:, 1:2], ALU.is_equal, ALU.mult)
                    link()
                    dve.tensor_scalar(sc[:, 7:8], sc[:, 3:4], 1e-9, sc[:, 6:7], ALU.mult, ALU.add)
                    dve.tensor_tensor(sc[:, 40:48], sc[:, 40:48], sc[:, 48:56], ALU.add)
                    link()
                    dve.reciprocal(sc[:, 36:37], sc[:, 7:8])
                    link()
                    dve.tensor_scalar(sc[:, 56:64], sc[:, 40:48], sc[:, 36:37], None, ALU.mult).then_inc(s_gates, 1)
                if stage_ == "I":
                    if some(t):
                        dve.wait_ge(s_gst, t * 16)
                    dve.wait_ge(s_gates_psum, t + 1)
                    dve.tensor_copy(gts[:, :], PB[0:EXP, 0:P]).then_inc(s_gates_t, 1)

            def split_low(c):
                if c % 2 == 0:
                    n = (c + 1) // SPLITS
                    whole, _, _, aside = split_chunk(c + 1)
                    link()
                    dve.tensor_scalar(aside, whole, cst[:, n:n + 1], None, ALU.mult).then_inc(s_stgd, 1)
                _, high, low_, aside = split_chunk(c)
                dve.wait_ge(s_whi, c + 1)
                dve.tensor_tensor(low_, aside.rearrange("p (u c) -> p u c", c=P), high, ALU.subtract).then_inc(s_wlo, 1)

            for p in range(-1, 1):
                window(p + 1, p + 1)
                for k in range(POST + 1):
                    if k < GROUPS:
                        one_hots(p + 1, k, p + 1)
                    if k == 0:
                        one_hots_extra(p + 1)
                    for c in splits_at(p, k):
                        split_low(c)
                    if p >= 0 and k in STAGES:
                        update(0, 0, 0, STAGES[k])
                neighbours(p + 1, p + 1)

            def take_input(b, n):
                dve.drain()
                dve.wait_ge(s_ffn_high, n)
                if some(b):
                    dve.wait_ge(s_h3, HT * b)
                dve.tensor_copy(x2a[:, :, :], x2s[:, :, :]).then_inc(s_x2, 1)

            take_input(0, 1)

            def low(b, j, cols):
                dve.wait_ge(s_hi, HT * b + j + 1)
                dve.tensor_tensor(hh[:, 2 * (j % 3) + 1, 0:cols], hid[:, (j % 2) * NB:(j % 2) * NB + cols],
                                  hh[:, 2 * (j % 3), 0:cols], ALU.subtract).then_inc(s_lo, 1)

            def ffn_block(b, summed, tiles, cols, nxt):
                for j in range(HT):
                    if summed:
                        for q, i in (GROUP_AT[0] if j == 0 else []) + (GROUP_AT[j + 1] if j + 1 < HT else []):
                            t, par = BT * b + 2 + q, q % 2
                            if i == 0 and q in summed:
                                window(t, par)
                            if q in summed:
                                one_hots(t, i, par)
                    for q, i in GROUP_AT[j]:
                        if i == 0 and q in summed:
                            one_hots_extra(BT * b + 2 + q)
                    s, h = (sig[:, (j % 2) * NB:(j % 2) * NB + cols], hid[:, (j % 2) * NB:(j % 2) * NB + cols])
                    dve.wait_ge(s_h3, HT * b + j + 1)
                    dve.wait_ge(s_sig, HT * b + j + 1)
                    dve.scalar_tensor_tensor(out=h, in0=H3[j % 2][:, 0:cols], scalar=cst[:, 4:5], in1=s,
                                             op0=ALU.mult, op1=ALU.mult).then_inc(s_u, 1)
                    if j:
                        low(b, j - 1, cols)
                    i = j // FULL if j < HT_FULL else EXP + j - HT_FULL
                    if j % FULL == 0 or j >= HT_FULL:
                        dve.wait_ge(s_gld[i % GSLOTS], gate_count(b, i))
                    dve.wait_ge(s_u, HT * b + j + 2)
                    g = gate[:, (i % GSLOTS) * NB:(i % GSLOTS) * NB + cols]
                    dve.tensor_tensor(h, h, g, ALU.mult).then_inc(s_t, 1)
                    for q, st in stages_at(j, tiles):
                        update(BT * b + 1 + q, q, (q + 1) % 2, st, b)
                    for q, i in GROUP_AT[j]:
                        if i == GROUPS - 1 and q in summed:
                            neighbours(BT * b + 2 + q, q % 2)
                low(b, HT - 1, cols)
                if nxt:
                    take_input(b + 1, BT * b + BT + 1)
                dve.wait_ge(s_x1, b + 1)
                dve.wait_ge(s_f2, HT * b + HT + 1)
                for k in range(KC):
                    o = x1a[:, k * NB:k * NB + cols]
                    dve.scalar_tensor_tensor(out=o, in0=Y[k][:, 0:cols], scalar=cst[:, 5:6], in1=o,
                                             op0=ALU.mult, op1=ALU.add).then_inc(s_y, 1)

            ffn_block(0, range(BT), range(BT), P, True)
            with dve.Fori(1, BLOCKS - 1) as b:
                ffn_block(b, range(BT), range(BT), NB, True)
            ffn_block(BLOCKS - 1, range(BT - 1), range(BT), NB, True)
            ffn_block(BLOCKS, (), (), NB, False)


def gate_count(b, i):
    def dmas(k):
        return 1 if k < EXP else len(segments(HT_FULL + k - EXP))

    slot = [k for k in range(GLOADS) if k % GSLOTS == i % GSLOTS]
    return b * (16 * sum(map(dmas, slot))) + 16 * sum(dmas(k) for k in slot if k <= i)


def kernel(x, src, dst, L0_gnn_W, L0_gnn_b, L0_mix_W_qkv, L0_mix_b_qkv, L0_mix_W_out, L0_mix_b_out,
           L0_ffn_router_w, L0_ffn_w1, L0_ffn_w2, L0_ffn_w3):
    import numpy as np
    import concourse.bacc as bacc
    from concourse.bass_utils import run_bass_kernel_spmd

    def pad(a, n, value=0):
        out = np.full((n,) + a.shape[1:], value, a.dtype)
        out[:a.shape[0]] = a
        return out

    def hidden_rows(w):
        a = np.concatenate([w[:, :FULL * P].reshape(-1, C), w[:, FULL * P:].reshape(-1, C)])
        return pad(a, HPAD)

    x, src, dst = np.asarray(x), np.asarray(src), np.asarray(dst)
    w1, w2, w3 = np.asarray(L0_ffn_w1), np.asarray(L0_ffn_w2), np.asarray(L0_ffn_w3)
    wqkv, bqkv = np.asarray(L0_mix_W_qkv), np.asarray(L0_mix_b_qkv)
    nowhere = 1 << 20
    w13T = [hidden_rows(w).T.reshape(KC, P, HPAD).transpose(1, 0, 2).reshape(P, KC * HPAD) for w in (w1, w3)]
    w2T = hidden_rows(w2.transpose(0, 2, 1)).reshape(HT, P, C).transpose(1, 0, 2).reshape(P, HT * C)
    arrays = {
        "x": pad(x, NODE_GROUPS * NB),
        "srcT": pad(src, ETW * P).reshape(ETW, P).T,
        "dstT": pad(dst, ETW * P, nowhere).reshape(ETW, P).T,
        "dst_rows": pad(dst, EJ * P * P, nowhere).reshape(EJ * P, P),
        "Wg": np.asarray(L0_gnn_W), "bg": np.asarray(L0_gnn_b)[None, :],
        "Wq": wqkv[:, 0:C], "Wk": wqkv[:, C:2 * C], "WvT": wqkv[:, 2 * C:].T,
        "bq": bqkv[None, 0:C], "bk": bqkv[None, C:2 * C], "bv": bqkv[2 * C:, None],
        "Wo": np.asarray(L0_mix_W_out), "bo": np.asarray(L0_mix_b_out)[None, :],
        "rwT": np.asarray(L0_ffn_router_w).T,
        "wT": np.stack(w13T + [w2T]),
    }
    arrays = {f"in_{k}": np.ascontiguousarray(v) for k, v in arrays.items()}
    nc = bacc.Bacc("TRN2", target_bir_lowering=False, num_devices=1, dynamic_dma_scratch_size=14336)
    args = [nc.dram_tensor(k, v.shape, mybir.dt.from_np(v.dtype), kind="ExternalInput").ap() for k, v in arrays.items()]
    out = nc.dram_tensor("out_t", (C, NODES), F32, kind="ExternalOutput").ap()
    gnn_mix_moe(nc, *args, out)
    r = run_bass_kernel_spmd(nc, [arrays], core_ids=[0])
    return np.ascontiguousarray(r.results[0]["out_t"].T)
```
